# Optimizing a Trainium2 kernel written in Bass

```python
import numpy as np
import jax
import jax.numpy as jnp

def _softmax(x, axis=-1):
    return jax.nn.softmax(x, axis=axis)

def _gelu(x):
    return jax.nn.gelu(x, approximate=True)

def _silu(x):
    return jax.nn.silu(x)

def _sigmoid(x):
    return jax.nn.sigmoid(x)

def _layernorm(x, axis=-1, eps=1e-05):
    m = jnp.mean(x, axis=axis, keepdims=True)
    v = jnp.var(x, axis=axis, keepdims=True)
    return (x - m) / jnp.sqrt(v + eps)

def _scatter_add(tgt, idx, src, axis=0):
    return tgt.at[idx].add(src)

def _segment_sum(src, seg, n):
    return jax.ops.segment_sum(src, seg, n)
kernel_name = 'mk_decoder_preln_d2_seqx_r8_6b60b1'

def setup_inputs(seed: int=0):
    np.random.seed(seed)
    _w = jnp.asarray

    def _rec_inputs():
        import jax
        import jax.numpy as jnp
        _rk = jax.random.key(seed)
        x = 7.22e-05 + 1 * jax.random.normal(jax.random.fold_in(_rk, 1), (8, 256, 128), jnp.float32)
        _lenS = 256 - jax.random.randint(jax.random.fold_in(_rk, 7), (8,), 0, max(1, 256 // 4) + 1, jnp.int32)
        _lenS2 = 256 - jax.random.randint(jax.random.fold_in(_rk, 8), (8,), 0, max(1, 256 // 4) + 1, jnp.int32)
        _ctx_1024P = jax.random.normal(jax.random.fold_in(_rk, 11), (8, 16, 128), jnp.float32)
        _ctx_1024c = jax.random.dirichlet(jax.random.fold_in(_rk, 511), 0.3 * jnp.ones((16,), jnp.float32), (8, 256))
        _ctx_1024t = jnp.einsum('bsk,bkd->bsd', _ctx_1024c, _ctx_1024P)
        _ctx_1024t = _ctx_1024t * jax.lax.rsqrt(jnp.mean(jnp.square(_ctx_1024t)) + 1e-12) * 0.953939
        ctx_1024 = 4.13588e-05 + 0.999923 * (_ctx_1024t + 0.3 * jax.random.normal(jax.random.fold_in(_rk, 611), (8, 256, 128), jnp.float32))
        return (x, ctx_1024)
    x, ctx_1024 = _rec_inputs()

    def _L0_attn_setup():
        import jax, jax.numpy as jnp
        import numpy as np
        D_MODEL = 128
        N_HEADS = 16
        HEAD_DIM = D_MODEL // N_HEADS
        key = jax.random.key(seed)
        kx, kq, kk, kv, ko = jax.random.split(key, 5)
        B, S = (4, 256)
        scale = 0.02
        return {'x': jax.random.normal(kx, (B, S, D_MODEL), dtype=jnp.float32), 'Wq': jax.random.normal(kq, (D_MODEL, D_MODEL), dtype=jnp.float32) * scale, 'Wk': jax.random.normal(kk, (D_MODEL, HEAD_DIM), dtype=jnp.float32) * scale, 'Wv': jax.random.normal(kv, (D_MODEL, HEAD_DIM), dtype=jnp.float32) * scale, 'Wo': jax.random.normal(ko, (D_MODEL, D_MODEL), dtype=jnp.float32) * scale}
    _L0_attn_all = _L0_attn_setup()
    _L0_attn_in = {k: v for k, v in _L0_attn_all.items() if k in ('Wq', 'Wk', 'Wv', 'Wo')}
    del _L0_attn_all

    def _L0_xattn_setup():
        import jax, jax.numpy as jnp
        import numpy as np
        D_MODEL = 128
        NHEAD = 16
        HEAD_DIM = D_MODEL // NHEAD
        key = jax.random.key(seed)
        ks = jax.random.split(key, 11)
        B, S, D = (4, 256, D_MODEL)
        scale = 1.0 / np.sqrt(D)
        inp = {'q': jax.random.normal(ks[0], (B, S, D), jnp.float32), 'k': jax.random.normal(ks[1], (B, S, D), jnp.float32), 'v': jax.random.normal(ks[2], (B, S, D), jnp.float32), 'Wq': jax.random.normal(ks[3], (D, D), jnp.float32) * scale, 'bq': jnp.zeros((D,), jnp.float32), 'Wk': jax.random.normal(ks[4], (D, D), jnp.float32) * scale, 'bk': jnp.zeros((D,), jnp.float32), 'Wv': jax.random.normal(ks[5], (D, D), jnp.float32) * scale, 'bv': jnp.zeros((D,), jnp.float32), 'Wo': jax.random.normal(ks[6], (D, D), jnp.float32) * scale, 'bo': jnp.zeros((D,), jnp.float32)}
        return inp
    _L0_xattn_all = _L0_xattn_setup()
    _L0_xattn_in = {k: v for k, v in _L0_xattn_all.items() if k in ('Wq', 'bq', 'Wk', 'bk', 'Wv', 'bv', 'Wo', 'bo')}
    del _L0_xattn_all

    def _L0_ffn_setup():
        import jax, jax.numpy as jnp
        import numpy as np
        TOP_K = 2
        key = jax.random.key(seed)
        ks = jax.random.split(key, 6)
        B, T, H, E, F = (2, 256, 128, 8, 512)
        s = 0.02
        return {'hidden_states': jax.random.normal(ks[0], (B, T, H), dtype=jnp.float32), 'router_w': jax.random.normal(ks[1], (E, H), dtype=jnp.float32) * s, 'w1': jax.random.normal(ks[2], (E, F, H), dtype=jnp.float32) * s, 'b1': jax.random.normal(ks[3], (E, F), dtype=jnp.float32) * s, 'w2': jax.random.normal(ks[4], (E, H, F), dtype=jnp.float32) * s, 'b2': jax.random.normal(ks[5], (E, H), dtype=jnp.float32) * s}
    _L0_ffn_all = _L0_ffn_setup()
    _L0_ffn_in = {k: v for k, v in _L0_ffn_all.items() if k in ('router_w', 'w1', 'b1', 'w2', 'b2')}
    del _L0_ffn_all

    def _L1_attn_setup():
        import jax, jax.numpy as jnp
        import numpy as np
        E = 128
        H = 16
        D = E // H
        K = 15
        PAD_L = K // 2
        T, B = (256, 4)

        def dynamic_conv_tbc(x, dyn_w, dyn_b):
            t, b, c = x.shape
            r = c // H
            w = jax.nn.softmax((x @ dyn_w.T + dyn_b).reshape(t, b, H, K), axis=-1)
            xpad = jnp.pad(x, ((PAD_L, K - 1 - PAD_L), (0, 0), (0, 0)))
            xh = xpad.reshape(t + K - 1, b, H, r)
            out = jnp.zeros((t, b, H, r), x.dtype)
            for k in range(K):
                out = out + w[..., k:k + 1] * xh[k:k + t]
            return out.reshape(t, b, c)
        key = jax.random.key(seed)
        ks = jax.random.split(key, 6)
        s = 0.02
        return {'x': jax.random.normal(ks[0], (T, B, E), dtype=jnp.float32), 'in_proj_w': jax.random.normal(ks[1], (3 * E, E), dtype=jnp.float32) * s, 'in_proj_b': jnp.zeros((3 * E,), jnp.float32), 'out_proj_w': jax.random.normal(ks[2], (E, 2 * E), dtype=jnp.float32) * s, 'out_proj_b': jnp.zeros((E,), jnp.float32), 'dyn_w': jax.random.normal(ks[3], (H * K, E), dtype=jnp.float32) * s, 'dyn_b': jnp.zeros((H * K,), jnp.float32)}
    _L1_attn_all = _L1_attn_setup()
    _L1_attn_in = {k: v for k, v in _L1_attn_all.items() if k in ('in_proj_w', 'in_proj_b', 'out_proj_w', 'out_proj_b', 'dyn_w', 'dyn_b')}
    del _L1_attn_all

    def _L1_xattn_setup():
        import jax, jax.numpy as jnp
        import numpy as np
        EMBED_DIM = 128
        NUM_HEADS = 16
        HEAD_DIM = EMBED_DIM // NUM_HEADS
        SCALE = HEAD_DIM ** (-0.5)
        key = jax.random.key(seed)
        k1, k2, k3, k4, k5, k6 = jax.random.split(key, 6)
        B, Tq, Tk = (2, 256, 256)
        std = EMBED_DIM ** (-0.5)
        return {'x_q': jax.random.normal(k1, (B, Tq, EMBED_DIM), jnp.float32), 'x_kv': jax.random.normal(k2, (B, Tk, EMBED_DIM), jnp.float32), 'w_q': jax.random.normal(k3, (EMBED_DIM, EMBED_DIM), jnp.float32) * std, 'w_kv': jax.random.normal(k4, (EMBED_DIM, 2 * EMBED_DIM), jnp.float32) * std, 'w_proj': jax.random.normal(k5, (EMBED_DIM, EMBED_DIM), jnp.float32) * std, 'w_rel': jax.random.normal(k6, (1, NUM_HEADS), jnp.float32) * 0.02}
    _L1_xattn_all = _L1_xattn_setup()
    _L1_xattn_in = {k: v for k, v in _L1_xattn_all.items() if k in ('w_q', 'w_kv', 'w_proj', 'w_rel')}
    del _L1_xattn_all

    def _L1_ffn_setup():
        import jax, jax.numpy as jnp
        import numpy as np
        EPS = 1e-06
        N_EXPERTS = 8

        def _rms_norm(x, scale, eps=EPS):
            mean_sq = jnp.mean(x.astype(jnp.float32) ** 2, axis=-1, keepdims=True)
            s = scale.astype(jnp.float32) * jax.lax.rsqrt(mean_sq + eps)
            return x * s.astype(x.dtype)

        def _dist2(x, y):
            nx = jnp.sum(x ** 2, axis=-1)[..., :, None]
            ny = jnp.sum(y ** 2, axis=-1)[..., None, :]
            return nx + ny - 2.0 * (x @ y.T)
        key = jax.random.key(seed)
        ks = jax.random.split(key, 5)
        dim, hidden, E = (128, 256, N_EXPERTS)
        x = jax.random.normal(ks[0], (4, 256, dim), dtype=jnp.float32)
        scale = jnp.ones((dim,), dtype=jnp.float32)
        centroids = jax.random.normal(ks[1], (E, dim), dtype=jnp.float32)
        up_w = jax.random.normal(ks[2], (E, dim, hidden * 2), dtype=jnp.float32) * dim ** (-0.5)
        down_w = jax.random.normal(ks[3], (E, hidden, dim), dtype=jnp.float32) * hidden ** (-0.5)
        return {'x': x, 'scale': scale, 'centroids': centroids, 'up_w': up_w, 'down_w': down_w}
    _L1_ffn_all = _L1_ffn_setup()
    _L1_ffn_in = {k: v for k, v in _L1_ffn_all.items() if k in ('scale', 'centroids', 'up_w', 'down_w')}
    del _L1_ffn_all
    return {'x': x, 'ctx_1024': ctx_1024, 'L0_attn_Wq': _L0_attn_in['Wq'], 'L0_attn_Wk': _L0_attn_in['Wk'], 'L0_attn_Wv': _L0_attn_in['Wv'], 'L0_attn_Wo': _L0_attn_in['Wo'], 'L0_xattn_Wq': _L0_xattn_in['Wq'], 'L0_xattn_bq': _L0_xattn_in['bq'], 'L0_xattn_Wk': _L0_xattn_in['Wk'], 'L0_xattn_bk': _L0_xattn_in['bk'], 'L0_xattn_Wv': _L0_xattn_in['Wv'], 'L0_xattn_bv': _L0_xattn_in['bv'], 'L0_xattn_Wo': _L0_xattn_in['Wo'], 'L0_xattn_bo': _L0_xattn_in['bo'], 'L0_ffn_router_w': _L0_ffn_in['router_w'], 'L0_ffn_w1': _L0_ffn_in['w1'], 'L0_ffn_b1': _L0_ffn_in['b1'], 'L0_ffn_w2': _L0_ffn_in['w2'], 'L0_ffn_b2': _L0_ffn_in['b2'], 'L1_attn_in_proj_w': _L1_attn_in['in_proj_w'], 'L1_attn_in_proj_b': _L1_attn_in['in_proj_b'], 'L1_attn_out_proj_w': _L1_attn_in['out_proj_w'], 'L1_attn_out_proj_b': _L1_attn_in['out_proj_b'], 'L1_attn_dyn_w': _L1_attn_in['dyn_w'], 'L1_attn_dyn_b': _L1_attn_in['dyn_b'], 'L1_xattn_w_q': _L1_xattn_in['w_q'], 'L1_xattn_w_kv': _L1_xattn_in['w_kv'], 'L1_xattn_w_proj': _L1_xattn_in['w_proj'], 'L1_xattn_w_rel': _L1_xattn_in['w_rel'], 'L1_ffn_scale': _L1_ffn_in['scale'], 'L1_ffn_centroids': _L1_ffn_in['centroids'], 'L1_ffn_up_w': _L1_ffn_in['up_w'], 'L1_ffn_down_w': _L1_ffn_in['down_w']}

def reference(x, ctx_1024, L0_attn_Wq, L0_attn_Wk, L0_attn_Wv, L0_attn_Wo, L0_xattn_Wq, L0_xattn_bq, L0_xattn_Wk, L0_xattn_bk, L0_xattn_Wv, L0_xattn_bv, L0_xattn_Wo, L0_xattn_bo, L0_ffn_router_w, L0_ffn_w1, L0_ffn_b1, L0_ffn_w2, L0_ffn_b2, L1_attn_in_proj_w, L1_attn_in_proj_b, L1_attn_out_proj_w, L1_attn_out_proj_b, L1_attn_dyn_w, L1_attn_dyn_b, L1_xattn_w_q, L1_xattn_w_kv, L1_xattn_w_proj, L1_xattn_w_rel, L1_ffn_scale, L1_ffn_centroids, L1_ffn_up_w, L1_ffn_down_w):
    import jax
    import jax.numpy as jnp

    def _L0_attn_ref(x, Wq, Wk, Wv, Wo):
        import jax, jax.numpy as jnp
        import numpy as np
        D_MODEL = 128
        N_HEADS = 16
        HEAD_DIM = D_MODEL // N_HEADS
        B, S, _ = x.shape
        Q = (x @ Wq).reshape(B, S, N_HEADS, HEAD_DIM).transpose(0, 2, 1, 3)
        K = x @ Wk
        V = x @ Wv
        scores = jnp.einsum('bhqd,bkd->bhqk', Q, K) / jnp.sqrt(jnp.float32(HEAD_DIM))
        attn = jax.nn.softmax(scores, axis=-1)
        out = jnp.einsum('bhqk,bkd->bhqd', attn, V)
        out = out.transpose(0, 2, 1, 3).reshape(B, S, D_MODEL)
        return out @ Wo

    def _L0_xattn_ref(q, k, v, Wq, bq, Wk, bk, Wv, bv, Wo, bo):
        import jax, jax.numpy as jnp
        import numpy as np
        D_MODEL = 128
        NHEAD = 16
        HEAD_DIM = D_MODEL // NHEAD
        B, S, D = q.shape
        H, Hd = (NHEAD, HEAD_DIM)
        qh = (q @ Wq.T + bq).reshape(B, S, H, Hd).transpose(0, 2, 1, 3)
        kh = (k @ Wk.T + bk).reshape(B, S, H, Hd).transpose(0, 2, 1, 3)
        vh = (v @ Wv.T + bv).reshape(B, S, H, Hd).transpose(0, 2, 1, 3)
        scores = jnp.einsum('bhqd,bhkd->bhqk', qh, kh) / jnp.sqrt(jnp.float32(Hd))
        attn = jax.nn.softmax(scores, axis=-1)
        out = jnp.einsum('bhqk,bhkd->bhqd', attn, vh)
        out = out.transpose(0, 2, 1, 3).reshape(B, S, D)
        return out @ Wo.T + bo

    def _L0_ffn_ref(hidden_states, router_w, w1, b1, w2, b2):
        import jax, jax.numpy as jnp
        import numpy as np
        TOP_K = 2
        x = hidden_states
        router_logits = jnp.einsum('bth,eh->bte', x, router_w)
        topk_values, topk_indices = jax.lax.top_k(router_logits, TOP_K)
        topk_weights = jax.nn.softmax(topk_values.astype(jnp.float32), axis=-1).astype(x.dtype)
        h1 = jnp.einsum('bth,efh->btef', x, w1) + b1
        h1 = jax.nn.gelu(h1, approximate=False)
        expert_outputs = jnp.einsum('btef,ehf->bteh', h1, w2) + b2
        gather_idx = topk_indices[..., None]
        topk_expert_outputs = jnp.take_along_axis(expert_outputs, gather_idx, axis=2)
        mixed_output = jnp.sum(topk_expert_outputs * topk_weights[..., None], axis=2)
        return mixed_output

    def _L1_attn_ref(x, in_proj_w, in_proj_b, out_proj_w, out_proj_b, dyn_w, dyn_b):
        import jax, jax.numpy as jnp
        import numpy as np
        E = 128
        H = 16
        D = E // H
        K = 15
        PAD_L = K // 2
        T, B = (256, 4)

        def dynamic_conv_tbc(x, dyn_w, dyn_b):
            t, b, c = x.shape
            r = c // H
            w = jax.nn.softmax((x @ dyn_w.T + dyn_b).reshape(t, b, H, K), axis=-1)
            xpad = jnp.pad(x, ((PAD_L, K - 1 - PAD_L), (0, 0), (0, 0)))
            xh = xpad.reshape(t + K - 1, b, H, r)
            out = jnp.zeros((t, b, H, r), x.dtype)
            for k in range(K):
                out = out + w[..., k:k + 1] * xh[k:k + t]
            return out.reshape(t, b, c)
        t, b, _ = x.shape
        qkv = x @ in_proj_w.T + in_proj_b
        q, k, v = jnp.split(qkv, 3, axis=-1)
        q = q * D ** (-0.5)

        def heads(z):
            return z.reshape(t, b * H, D).transpose(1, 0, 2)
        qh, kh, vh = (heads(q), heads(k), heads(v))
        scores = jnp.einsum('ntd,nsd->nts', qh, kh)
        attn = jax.nn.softmax(scores, axis=-1)
        o = jnp.einsum('nts,nsd->ntd', attn, vh)
        attn_out = o.transpose(1, 0, 2).reshape(t, b, E)
        conv_out = dynamic_conv_tbc(v, dyn_w, dyn_b)
        cat = jnp.concatenate([attn_out, conv_out], axis=-1)
        return cat @ out_proj_w.T + out_proj_b

    def _L1_xattn_ref(x_q, x_kv, w_q, w_kv, w_proj, w_rel):
        import jax, jax.numpy as jnp
        import numpy as np
        EMBED_DIM = 128
        NUM_HEADS = 16
        HEAD_DIM = EMBED_DIM // NUM_HEADS
        SCALE = HEAD_DIM ** (-0.5)
        B, Tq, _ = x_q.shape
        Tk = x_kv.shape[1]
        q = x_q @ w_q
        kv = x_kv @ w_kv
        k, v = jnp.split(kv, 2, axis=-1)

        def heads(y, T):
            return y.reshape(B, T, NUM_HEADS, HEAD_DIM).transpose(0, 2, 1, 3)
        q = heads(q, Tq)
        k = heads(k, Tk)
        v = heads(v, Tk)
        logits = jnp.einsum('bhqd,bhkd->bhqk', q, k) * SCALE
        rel = jnp.arange(Tq, dtype=jnp.float32)[:, None] - jnp.arange(Tk, dtype=jnp.float32)[None, :]
        bias = rel[..., None] * w_rel[0]
        bias = bias.transpose(2, 0, 1)[None]
        logits = logits + bias
        attn = jax.nn.softmax(logits, axis=-1)
        out = jnp.einsum('bhqk,bhkd->bhqd', attn, v)
        out = out.transpose(0, 2, 1, 3).reshape(B, Tq, EMBED_DIM)
        return out @ w_proj

    def _L1_ffn_ref(x, scale, centroids, up_w, down_w):
        import jax, jax.numpy as jnp
        import numpy as np
        EPS = 1e-06
        N_EXPERTS = 8

        def _rms_norm(x, scale, eps=EPS):
            mean_sq = jnp.mean(x.astype(jnp.float32) ** 2, axis=-1, keepdims=True)
            s = scale.astype(jnp.float32) * jax.lax.rsqrt(mean_sq + eps)
            return x * s.astype(x.dtype)

        def _dist2(x, y):
            nx = jnp.sum(x ** 2, axis=-1)[..., :, None]
            ny = jnp.sum(y ** 2, axis=-1)[..., None, :]
            return nx + ny - 2.0 * (x @ y.T)
        skip = x
        xn = _rms_norm(x, scale)
        ids = jnp.argmin(_dist2(xn, centroids), axis=-1)
        out = jnp.zeros_like(x)
        for e in range(N_EXPERTS):
            h = jnp.einsum('bsd,dh->bsh', xn, up_w[e])
            a, g = jnp.split(h, 2, axis=-1)
            y = jnp.einsum('bsh,hd->bsd', a * jax.nn.silu(g), down_w[e])
            out = jnp.where((ids == e)[..., None], y, out)
        return out + skip
    x = x + _L0_attn_ref(_layernorm(x, axis=-1), L0_attn_Wq, L0_attn_Wk, L0_attn_Wv, L0_attn_Wo)
    x = x + _L0_xattn_ref(_layernorm(x, axis=-1), ctx_1024, ctx_1024, L0_xattn_Wq, L0_xattn_bq, L0_xattn_Wk, L0_xattn_bk, L0_xattn_Wv, L0_xattn_bv, L0_xattn_Wo, L0_xattn_bo)
    x = x + _L0_ffn_ref(_layernorm(x, axis=-1), L0_ffn_router_w, L0_ffn_w1, L0_ffn_b1, L0_ffn_w2, L0_ffn_b2)
    x = x + _L1_attn_ref(_layernorm(x, axis=-1), L1_attn_in_proj_w, L1_attn_in_proj_b, L1_attn_out_proj_w, L1_attn_out_proj_b, L1_attn_dyn_w, L1_attn_dyn_b)
    x = x + _L1_xattn_ref(_layernorm(x, axis=-1), ctx_1024, L1_xattn_w_q, L1_xattn_w_kv, L1_xattn_w_proj, L1_xattn_w_rel)
    x = x + _L1_ffn_ref(_layernorm(x, axis=-1), L1_ffn_scale, L1_ffn_centroids, L1_ffn_up_w, L1_ffn_down_w)
    return x

_drawn_inputs = setup_inputs


def setup_inputs(seed=0):
    import zlib

    import numpy as np

    out = dict(_drawn_inputs(seed))
    spreads = {'L0_xattn_bq': (0.0, 0.1),
     'L0_xattn_bk': (0.0, 2.0),
     'L0_xattn_bv': (0.0, 0.1),
     'L0_xattn_bo': (0.0, 0.1),
     'L1_attn_in_proj_b': (0.0, 0.1),
     'L1_attn_out_proj_b': (0.0, 0.1),
     'L1_attn_dyn_b': (0.0, 1.796),
     'L1_ffn_scale': (1.0, 0.2)}
    factors = {'L0_attn_Wq': 8.0,
     'L0_attn_Wk': 8.0,
     'L0_attn_Wv': 3.301,
     'L0_attn_Wo': 3.217,
     'L0_ffn_b1': 3.731,
     'L1_attn_dyn_w': 20.004}
    for name, (base, spread) in spreads.items():
        noise = np.random.default_rng([zlib.crc32(name.encode()), seed]).standard_normal(out[name].shape)
        drawn = base * np.exp(spread * noise) if base else spread * noise
        out[name] = jnp.asarray(drawn.astype(out[name].dtype))
    for name, factor in factors.items():
        out[name] = (out[name] * factor).astype(out[name].dtype)
    return out
```

```python
from contextlib import ExitStack, contextmanager

import concourse.bass as bass
from concourse import mybir

F32 = mybir.dt.float32
BF16 = mybir.dt.bfloat16
I32 = mybir.dt.int32
ALU = mybir.AluOpType
ACT = mybir.ActivationFunctionType
AX = mybir.AxisListType

P = 128
B, S, D = 8, 256, 128
H, HD = 16, 8
TILES = B * S // P
HALVES = S // P
LN_EPS = 1e-5
RMS_EPS = 1e-6
SCALE = HD ** -0.5
RSQRT_SEED = 1597463007.0

QUAD = 4
NQUAD = H // QUAD
SLOTS = 6
ROWS_QK = SLOTS * HD
ROW_REL = ROWS_QK
ROWS_MAX = 96
ROW_M = 96
ROWS_ALL = 98
VW = HD + 1
VCOLS = H * VW + 32


@contextmanager
def phase_semaphores(nc, name):
    taken = []

    def sem(nm):
        taken.append(nc.alloc_semaphore(f"{name}_{nm}"))
        return taken[-1]

    yield sem
    with nc.Block() as block:
        @block.gpsimd
        def _(pool):
            nc.clear_and_free_semaphores(taken)


def newton_rsqrt(pool, done, base, var, gain, eps, y, t):
    k = 0

    def step(ins):
        nonlocal k
        ins.then_inc(done, 1)
        k += 1
        pool.wait_ge(done, base + k)

    step(pool.tensor_scalar(t[0], var, gain, eps, ALU.mult, ALU.add))
    step(pool.tensor_scalar(y.bitcast(I32), t[0].bitcast(I32), -0.5, RSQRT_SEED, ALU.mult, ALU.add))
    for _ in range(4):
        step(pool.tensor_tensor(t[1], y, y, ALU.mult))
        step(pool.tensor_tensor(t[1], t[1], t[0], ALU.mult))
        step(pool.tensor_scalar(t[1], t[1], -0.5, 1.5, ALU.mult, ALU.add))
        step(pool.tensor_tensor(y, y, t[1], ALU.mult))
    assert k == NEWTON_STEPS


NEWTON_STEPS = 18


def attention_steps(n):
    out = []

    def add(kind, v, k=0):
        if 0 <= v < n:
            out.append((kind, v, k))

    add("stat", 0), add("norm", 0), add("xnt", 0), add("qk", 0), add("stat", 1)
    for t in range(n + 2):
        head = iter(range(H))

        def maxima(m):
            for _ in range(m):
                add("max", t, next(head))

        add("scores", t - 1, 0), maxima(2), add("norm", t + 1), add("xnt", t + 1)
        add("scores", t - 1, 1), add("pv", t - 2, 3), add("ot", t - 2, 1)
        maxima(2), add("qk", t + 1), maxima(2)
        add("scores", t - 1, 2), maxima(2), add("fin", t - 2, 0)
        add("scores", t - 1, 3), add("pv", t - 1, 0), maxima(1), add("fin", t - 2, 1), maxima(2)
        add("scores", t - 1, 4), maxima(2), add("ont", t - 2)
        add("scores", t - 1, 5), add("pv", t - 1, 1), add("ot", t - 1, 0), maxima(1), add("out", t - 2), maxima(2)
        add("scores", t - 1, 6), add("negm", t), add("v", t), add("stat", t + 2)
        add("scores", t - 1, 7), add("pv", t - 1, 2)
    return out


def attention_phase(nc, name, x_all, ident, layers, ctxT, scratch):
    n = B * len(layers)
    with ExitStack() as ctx:
        def sb(nm, shape, dt):
            return ctx.enter_context(nc.sbuf_tensor(f"{name}_{nm}", shape, dt))

        def ps(nm, shape):
            return ctx.enter_context(nc.psum_tensor(f"{name}_{nm}", shape, F32))

        sem = ctx.enter_context(phase_semaphores(nc, name))

        bn = sb("bn", [P, HALVES, 6], F32)
        mv = sb("mv", [P, HALVES, 2], F32)
        nt = [sb(f"nt{i}", [P, HALVES], F32) for i in range(2)]
        rstd = sb("rstd", [P, HALVES], F32)
        xn = sb("xn", [P, HALVES, D], F32)
        xnT = [sb(f"xnT{i}", [P, S], F32) for i in range(2)]
        qk32 = sb("qk32", [P, 2, S], F32)
        r32 = sb("r32", [P, 2, S], F32)
        parts = sb("parts", [P, 3, 2, S], BF16)
        stackQ = [sb(f"stackQ{i}", [ROWS_ALL, H, S], BF16) for i in range(2)]
        stackK = [sb(f"stackK{i}", [ROWS_ALL, H, S], BF16) for i in range(2)]
        mx = sb("mx", [P, HALVES, H], F32)
        mparts = sb("mparts", [H, 2, S], BF16)
        Vp = [sb(f"Vp{i}", [P, HALVES, VCOLS], F32) for i in range(2)]
        prob = [sb(f"prob{i}", [P, QUAD, HALVES, S], F32) for i in range(2)]
        oT = [sb(f"oT{i}", [P, 2, S], F32) for i in range(2)]
        rec = sb("rec", [P, HALVES, 8, 1], F32)
        on = sb("on", [P, HALVES, D], F32)
        onT = sb("onT", [P, S], F32)

        scoresP = [ps(f"scoresP{i}", [P, 2, HALVES, S]) for i in range(2)]
        maxP = [ps(f"maxP{i}", [P, HALVES, S]) for i in range(2)]
        outP = ps("outP", [P, 2, S])
        misc = ps("misc", [P, 512])

        W = []
        for i, lay in enumerate(layers):
            w = {k: sb(f"{k}{i}", list(lay[k].shape), F32) for k in ("wq", "wk", "wv", "wo")}
            if lay.get("bq") is not None:
                for k in ("bq", "bk", "bv"):
                    w[k] = sb(f"{k}{i}", [P, 1], F32)
                w["bo"] = sb(f"bo{i}", [P, 1, D], F32)
                w["bvw"] = sb(f"bvw{i}", [P, P], F32)
            W.append(w)
        biased = [i for i, lay in enumerate(layers) if lay.get("bq") is not None]
        rel = layers[0].get("w_rel")
        if rel is not None:
            wr = sb("wr", [1, H], F32)
            wr1 = sb("wr1", [1, H], F32)
            wparts = sb("wparts", [1, 3, H], BF16)
            relrow = sb("relrow", [1, 5, H, S], BF16)
            pos = sb("pos", [1, S], F32)

        s_w = sem("s_w")
        s_zeros = sem("s_zeros")
        s_ones = sem("s_ones")
        s_bvw = sem("s_bvw")
        s_bo_mm = sem("s_bo_mm")
        s_bo = sem("s_bo")
        s_rel = sem("s_rel")
        s_relrows = sem("s_relrows")
        s_bn = sem("s_bn")
        s_stat = sem("s_stat")
        s_newton = sem("s_newton")
        s_norm = sem("s_norm")
        s_xbias = sem("s_xbias")
        s_xnT_mm = sem("s_xnT_mm")
        s_xnT = sem("s_xnT")
        s_qk_mm = sem("s_qk_mm")
        s_qk = sem("s_qk")
        s_part = sem("s_part")
        s_parts = sem("s_parts")
        s_spill = sem("s_spill")
        s_load = [sem("s_load0"), sem("s_load1")]
        s_max_mm = sem("s_max_mm")
        s_max = sem("s_max")
        s_negm_mm = sem("s_negm_mm")
        s_mhi = sem("s_mhi")
        s_mlo = sem("s_mlo")
        s_mrows = sem("s_mrows")
        s_v_mm = sem("s_v_mm")
        s_v = sem("s_v")
        s_scores = sem("s_scores")
        s_exp = sem("s_exp")
        s_pv = sem("s_pv")
        s_oT = sem("s_oT")
        s_fin_mm = sem("s_fin_mm")
        s_rec = sem("s_rec")
        s_on = sem("s_on")
        s_ont_mm = sem("s_ont_mm")
        s_onT = sem("s_onT")
        s_out_mm = sem("s_out_mm")
        s_x = sem("s_x")

        STEPS = attention_steps(n)
        n_w = sum(4 + (4 if i in biased else 0) for i in range(len(layers))) + (rel is not None)

        def layer(v):
            return layers[v // B]

        def head_of(v, h):
            return 0 if layer(v)["mqa"] else h

        def loaded(v, half):
            shared = sum(layer(u)["mqa"] for u in range(v + 1))
            return 32 * (v + 1) - (16 * shared if half else 0)

        def kvT(v):
            if layer(v)["ctx"]:
                return ctxT[:, (v % B) * S:(v % B + 1) * S]
            return xnT[v % 2][:, :]

        block = ctx.enter_context(nc.Block())

        @block.sync
        def _(sp):
            for lay, w in zip(layers, W):
                for k in ("wq", "wk", "wv", "wo"):
                    sp.dma_start(w[k][:, :], lay[k]).then_inc(s_w, 16)
                if "bq" in w:
                    for k in ("bq", "bk", "bv"):
                        sp.dma_start(w[k][:, :], lay[k]).then_inc(s_w, 16)
                    sp.dma_start(w["bo"][:, 0, :], lay["bo"].partition_broadcast(P)).then_inc(s_w, 16)
            if rel is not None:
                sp.dma_start(wr[:, :], rel).then_inc(s_w, 16)
                sp.wait_ge(s_zeros, 4)
                sp.wait_ge(s_ones, 4)
                sp.wait_ge(s_rel, 11)
                for i in range(2):
                    for c in range(3):
                        for dst, src in ((stackQ[i], c), (stackK[i], 3)):
                            sp.dma_start(dst[ROW_REL + c:ROW_REL + c + 1, :, :], relrow[:, src, :, :]).then_inc(s_relrows, 16)
                        for dst, src in ((stackQ[i], 4), (stackK[i], c)):
                            sp.dma_start(dst[ROW_REL + 3 + c:ROW_REL + 4 + c, :, :], relrow[:, src, :, :]).then_inc(s_relrows, 16)

            def load(v, half):
                if v >= 2:
                    sp.wait_ge(s_scores, 8 * (v - 2) + (8 if layer(v - 2)["mqa"] else 4 * (half + 1)))
                if v == 0 and half == 0:
                    sp.wait_ge(s_zeros, 4)
                    sp.wait_ge(s_ones, 4)
                if half == 0:
                    sp.wait_ge(s_spill, 96 * (v + 1))
                lo = half * H // 2
                sp.dma_start(stackQ[v % 2][0:ROWS_QK, lo:lo + H // 2, :],
                             scratch[v % 2, 0].rearrange("s (d h) q -> (s d) h q", h=H)[:, lo:lo + H // 2, :])\
                    .then_inc(s_load[half], 16)
                if layer(v)["mqa"]:
                    if half == 0:
                        sp.wait_ge(s_scores, 8 * max(v - 1, 0))
                        sp.dma_start(stackK[v % 2][0:ROWS_QK, 0:1, :],
                                     scratch[v % 2, 1].rearrange("s (d h) q -> (s d) h q", h=H)[:, 0:1, :])\
                            .then_inc(s_load[half], 16)
                else:
                    sp.dma_start(stackK[v % 2][0:ROWS_QK, lo:lo + H // 2, :],
                                 scratch[v % 2, 1].rearrange("s (d h) q -> (s d) h q", h=H)[:, lo:lo + H // 2, :])\
                        .then_inc(s_load[half], 16)

            for kind, v, k in STEPS:
                if kind == "qk":
                    sp.wait_ge(s_parts, v + 1)
                    if v >= 2:
                        sp.wait_ge(s_load[0], loaded(v - 2, 0))
                        sp.wait_ge(s_load[1], loaded(v - 2, 1))
                    for qk, groups in ((0, ((0, 1, 3), (1, 1, 2), (2, 1, 1))), (1, ((0, 3, 1), (0, 2, 1), (0, 1, 1)))):
                        slot = 0
                        for part, many, times in groups:
                            src = parts[:, part:part + many, qk, :]
                            if times > 1:
                                src = parts[:, part:part + 1, qk, :].to_broadcast([P, times, S])
                            m = many * times
                            sp.dma_start(scratch[v % 2, qk, slot:slot + m].rearrange("s p q -> p s q"), src)\
                                .then_inc(s_spill, 16)
                            slot += m
                    load(v, 0)
                elif kind == "negm":
                    sp.wait_ge(s_mlo, v + 1)
                    for c in range(2):
                        sp.dma_start(stackQ[v % 2][ROW_M + c:ROW_M + c + 1, :, :], mparts[:, c, :])\
                            .then_inc(s_mrows, 16)
                if kind == "negm" and v + 1 < n or kind == "qk" and v == 0:
                    load(v + 1 if kind == "negm" else 0, 1)

        @block.gpsimd
        def _(pool):
            for i, t in enumerate((stackK[0][ROW_M:ROWS_ALL, :, :], stackK[1][ROW_M:ROWS_ALL, :, :],
                                   Vp[0][:, :, :], Vp[1][:, :, :])):
                pool.memset(t, 1.0).then_inc(s_ones, 1)
                pool.wait_ge(s_ones, i + 1)
            if rel is not None:
                pool.iota(pos[:, :], [[1, S]], base=0, channel_multiplier=0,
                          allow_small_or_imprecise_dtypes=True).then_inc(s_rel, 1)
            b1 = B * biased[0] if biased else 0
            for kind, v, k in STEPS:
                if kind == "stat":
                    pool.wait_ge(s_stat, v + 1)
                    if v >= 1:
                        pool.wait_ge(s_norm, v)
                    newton_rsqrt(pool, s_newton, NEWTON_STEPS * v, mv[:, :, 1], 1.0, LN_EPS, rstd[:, :],
                                 [t[:, :] for t in nt])
                elif kind == "qk":
                    pool.wait_ge(s_qk, v + 1)
                    if v >= 1:
                        pool.wait_ge(s_spill, 96 * v)
                    pool.tensor_tensor(parts[:, 1, :, :], qk32[:, :, :], parts[:, 0, :, :], ALU.subtract).then_inc(s_part, 1)
                    pool.tensor_tensor(r32[:, :, :], qk32[:, :, :], parts[:, 0, :, :], ALU.subtract).then_inc(s_part, 1)
                    pool.wait_ge(s_part, 2 * v + 2)
                    pool.tensor_tensor(parts[:, 2, :, :], r32[:, :, :], parts[:, 1, :, :], ALU.subtract).then_inc(s_parts, 1)
                    if v // B in biased:
                        xt = x_all[:, 2 * (v % B):2 * (v % B) + 2, :]
                        bo = W[v // B]["bo"][:, :, :].to_broadcast([P, HALVES, D])
                        if v == b1:
                            pool.wait_ge(s_bo, 1)
                        pool.wait_ge(s_norm, v + 1)
                        pool.tensor_tensor(xt, xt, bo, ALU.add).then_inc(s_xbias, 1)

        @block.scalar
        def _(act):
            for i in biased:
                act.wait_ge(s_w, 16 * n_w)
                act.activation(W[i]["bvw"][:, :], ident[:, :], ACT.Identity, bias=W[i]["bv"][:, 0:1], scale=0.0)\
                    .then_inc(s_bvw, 1)
            for kind, v, k in STEPS:
                if kind == "xnt":
                    act.wait_ge(s_xnT_mm, v + 1)
                    act.activation(xnT[v % 2][:, :], misc[:, 0:S], ACT.Copy).then_inc(s_xnT, 1)
                elif kind == "qk":
                    act.wait_ge(s_qk_mm, v + 1)
                    if v >= 1:
                        act.wait_ge(s_parts, v)
                        act.wait_ge(s_spill, 96 * v)
                    w = W[v // B]
                    if "bq" in w:
                        if v == B * biased[0]:
                            act.wait_ge(s_w, 16 * n_w)
                        for c, bias in ((0, w["bq"]), (1, w["bk"])):
                            act.activation(qk32[:, c, :], misc[:, c * S:(c + 1) * S], ACT.Identity, bias=bias[:, 0:1])
                            ins = act.activation(parts[:, 0, c, :], misc[:, c * S:(c + 1) * S], ACT.Identity, bias=bias[:, 0:1])
                    else:
                        act.activation(qk32[:, :, :].rearrange("p a b -> p (a b)"), misc[:, :], ACT.Copy)
                        ins = act.activation(parts[:, 0, :, :].rearrange("p a b -> p (a b)"), misc[:, :], ACT.Copy)
                    ins.then_inc(s_qk, 1)
                elif kind == "v":
                    act.wait_ge(s_v_mm, v + 1)
                    if v == 0:
                        act.wait_ge(s_zeros, 4)
                        act.wait_ge(s_ones, 4)
                    if v >= 2:
                        act.wait_ge(s_pv, NQUAD * (v - 1))
                    nh = 1 if layer(v)["mqa"] else H
                    act.activation(
                        Vp[v % 2][:, :, 0:nh * VW].rearrange("p k (h w) -> p k h w", w=VW)[:, :, :, 0:HD],
                        misc[:, 0:2 * P].rearrange("p (k c) -> p k c", k=2)[:, :, 0:nh * HD].rearrange("p k (h w) -> p k h w", w=HD),
                        ACT.Copy).then_inc(s_v, 1)
                elif kind == "scores":
                    m = 8 * v + k
                    act.wait_ge(s_scores, m + 1)
                    q = m // 2
                    if k % 2 == 0 and q >= 2:
                        act.wait_ge(s_pv, q - 1)
                    act.activation(prob[q % 2][:, 2 * (m % 2):2 * (m % 2) + 2, :, :].rearrange("p a b c -> p (a b c)"),
                                   scoresP[m % 2][:, :, :, :].rearrange("p a b c -> p (a b c)"),
                                   ACT.Exp, scale=SCALE).then_inc(s_exp, 1)
                elif kind == "ot":
                    act.wait_ge(s_pv, NQUAD * v + 2 * k + 2)
                    if v >= 1:
                        act.wait_ge(s_fin_mm, 2 * (v - 1) + k + 1)
                    act.activation(oT[k][:, :, :].rearrange("p a b -> p (a b)"),
                                   outP[:, :, :].rearrange("p a b -> p (a b)"), ACT.Copy).then_inc(s_oT, 1)
                elif kind == "ont":
                    act.wait_ge(s_ont_mm, v + 1)
                    if v >= 1:
                        act.wait_ge(s_out_mm, v)
                    act.activation(onT[:, :], misc[:, 0:S], ACT.Copy).then_inc(s_onT, 1)

        @block.vector
        def _(dve):
            for i in range(2):
                for t in (stackQ[i], stackK[i]):
                    dve.memset(t[0:ROW_M, :, :].rearrange("p h q -> p (h q)").bitcast(F32), 0.0).then_inc(s_zeros, 1)
            if biased:
                w = W[biased[0]]
                dve.wait_ge(s_bo_mm, 1)
                dve.tensor_tensor(w["bo"][:, 0, :], misc[:, 0:D], w["bo"][:, 0, :], ALU.add).then_inc(s_bo, 1)
            if rel is not None:
                dve.wait_ge(s_w, 16 * n_w)
                dve.wait_ge(s_rel, 1)
                k = 1

                def step(ins):
                    nonlocal k
                    ins.then_inc(s_rel, 1)
                    k += 1
                    dve.wait_ge(s_rel, k)

                step(dve.tensor_scalar(wr[:, :], wr[:, :], 1.0 / SCALE, None, ALU.mult))
                step(dve.tensor_copy(wparts[:, 0, :], wr[:, :]))
                step(dve.tensor_tensor(wr1[:, :], wr[:, :], wparts[:, 0, :], ALU.subtract))
                step(dve.tensor_copy(wparts[:, 1, :], wr1[:, :]))
                step(dve.tensor_tensor(wparts[:, 2, :], wr1[:, :], wparts[:, 1, :], ALU.subtract))
                for c in range(3):
                    src = wparts[:, c, :].rearrange("p (h o) -> p h o", o=1).to_broadcast([1, H, S])
                    step(dve.tensor_copy(relrow[:, c, :, :], src))
                i_row = pos[:, :].rearrange("p (o q) -> p o q", o=1).to_broadcast([1, H, S])
                step(dve.tensor_scalar(relrow[:, 3, :, :], i_row, -1.0, None, ALU.mult))
                step(dve.tensor_copy(relrow[:, 4, :, :], i_row))
            for kind, v, k in STEPS:
                xt = x_all[:, 2 * (v % B):2 * (v % B) + 2, :]
                if kind == "stat":
                    if v >= B:
                        dve.wait_ge(s_x, v - B + 1)
                    if v >= 1:
                        dve.wait_ge(s_newton, NEWTON_STEPS * v)
                        dve.wait_ge(s_norm, v)
                    for c in range(HALVES):
                        dve.bn_stats(bn[:, c, :], xt[:, c, :]).then_inc(s_bn, 1)
                    dve.wait_ge(s_bn, 2 * v + 2)
                    for c in range(HALVES):
                        ins = dve.bn_aggr(mv[:, c, :], bn[:, c, :])
                    ins.then_inc(s_stat, 1)
                elif kind == "norm":
                    dve.wait_ge(s_newton, NEWTON_STEPS * (v + 1))
                    dve.wait_ge(s_stat, v + 1)
                    if v >= 1:
                        dve.wait_ge(s_xnT_mm, v)
                    for c in range(HALVES):
                        ins = dve.tensor_scalar(xn[:, c, :], xt[:, c, :], mv[:, c, 0:1], rstd[:, c:c + 1],
                                                ALU.subtract, ALU.mult)
                    ins.then_inc(s_norm, 1)
                elif kind == "max":
                    m = H * v + k
                    dve.wait_ge(s_max_mm, m + 1)
                    if k == 0 and v >= 1:
                        dve.wait_ge(s_negm_mm, v)
                    dve.tensor_reduce(mx[:, :, k:k + 1], maxP[m % 2][:, :, :], AX.X, ALU.max).then_inc(s_max, 1)
                elif kind == "negm":
                    dve.wait_ge(s_negm_mm, v + 1)
                    if v >= 1:
                        dve.wait_ge(s_mrows, 32 * v)
                    dve.tensor_scalar(mparts[:, 0, :], misc[0:H, 0:S], -1.0, None, ALU.mult).then_inc(s_mhi, 1)
                    dve.wait_ge(s_mhi, v + 1)
                    dve.scalar_tensor_tensor(out=mparts[:, 1, :], in0=misc[0:H, 0:S], scalar=-1.0,
                                             in1=mparts[:, 0, :], op0=ALU.mult, op1=ALU.subtract).then_inc(s_mlo, 1)
                elif kind == "fin":
                    m = 2 * v + k
                    dve.wait_ge(s_fin_mm, m + 1)
                    if m >= 1:
                        dve.wait_ge(s_on, m)
                    grouped = misc[:, :].rearrange("p (q h c) -> p q h c", q=HALVES, c=32)
                    dve.reciprocal(rec[:, :, :, :], grouped[:, :, :, HD:HD + 1]).then_inc(s_rec, 1)
                    dve.wait_ge(s_rec, m + 1)
                    if k == 0 and v >= 1:
                        dve.wait_ge(s_ont_mm, v)
                    dve.tensor_tensor(on[:, :, k * 64:(k + 1) * 64].rearrange("p q (h d) -> p q h d", d=HD),
                                      grouped[:, :, :, 0:HD], rec[:, :, :, :].to_broadcast([P, HALVES, 8, HD]),
                                      ALU.mult).then_inc(s_on, 1)
                elif kind == "out":
                    dve.wait_ge(s_out_mm, v + 1)
                    if v // B in biased:
                        dve.wait_ge(s_xbias, v - B * biased[0] + 1)
                    dve.tensor_tensor(xt, misc[:, 0:S].rearrange("p (q d) -> p q d", d=D), xt, ALU.add).then_inc(s_x, 1)

        @block.tensor
        def _(pe):
            pe.wait_ge(s_w, 16 * n_w)
            if biased:
                w = W[biased[0]]
                pe.wait_ge(s_bvw, 1)
                pe.matmul(misc[:, 0:D], w["bvw"][:, :], w["wo"][:, :], start=True, stop=True).then_inc(s_bo_mm, 1)
                pe.wait_ge(s_bo, 1)
            if rel is not None:
                pe.wait_ge(s_relrows, 16 * 24)
            for kind, v, k in STEPS:
                p = v % 2
                if kind == "xnt":
                    pe.wait_ge(s_norm, v + 1)
                    if v >= 2:
                        pe.wait_ge(s_v, v - 1)
                    elif v == 1:
                        pe.wait_ge(s_qk, 1)
                    for c in range(HALVES):
                        ins = pe.transpose(misc[:, c * P:(c + 1) * P], xn[:, c, :], ident[:, :])
                    ins.then_inc(s_xnT_mm, 1)
                elif kind == "qk":
                    pe.wait_ge(s_xnT, v + 1)
                    w = W[v // B]
                    pe.matmul(misc[:, 0:S], w["wq"][:, :], xnT[p][:, :], start=True, stop=True)
                    pe.matmul(misc[:, S:2 * S], w["wk"][:, :], kvT(v), start=True, stop=True).then_inc(s_qk_mm, 1)
                elif kind == "max":
                    m = H * v + k
                    if k == 0:
                        pe.wait_ge(s_load[0], loaded(v, 0))
                    if k == H // 2:
                        pe.wait_ge(s_load[1], loaded(v, 1))
                    if m >= 2:
                        pe.wait_ge(s_max, m - 1)
                    for c in range(HALVES):
                        ins = pe.matmul(maxP[m % 2][:, c, :], stackQ[p][0:ROWS_MAX, k, c * P:(c + 1) * P],
                                        stackK[p][0:ROWS_MAX, head_of(v, k), :], start=True, stop=True)
                    ins.then_inc(s_max_mm, 1)
                elif kind == "negm":
                    pe.wait_ge(s_max, H * (v + 1))
                    pe.wait_ge(s_qk, min(v + 2, n))
                    if v >= 2:
                        pe.wait_ge(s_x, v - 1)
                    for c in range(HALVES):
                        ins = pe.transpose(misc[0:H, c * P:(c + 1) * P], mx[:, c, :], ident[:, :])
                    ins.then_inc(s_negm_mm, 1)
                elif kind == "v":
                    pe.wait_ge(s_mlo, v + 1)
                    nv = HD if layer(v)["mqa"] else D
                    for c in range(HALVES):
                        ins = pe.matmul(misc[:, c * P:c * P + nv], kvT(v)[:, c * P:(c + 1) * P],
                                        W[v // B]["wv"][:, :], start=True, stop=True)
                    ins.then_inc(s_v_mm, 1)
                elif kind == "scores":
                    m = 8 * v + k
                    if k == 0:
                        pe.wait_ge(s_mrows, 32 * (v + 1))
                    if m >= 2:
                        pe.wait_ge(s_exp, m - 1)
                    for a in range(2):
                        h = 2 * k + a
                        for c in range(HALVES):
                            ins = pe.matmul(scoresP[m % 2][:, a, c, :], stackK[p][:, head_of(v, h), c * P:(c + 1) * P],
                                            stackQ[p][:, h, :], start=True, stop=True)
                    ins.then_inc(s_scores, 1)
                elif kind == "pv":
                    q = NQUAD * v + k
                    pe.wait_ge(s_exp, 2 * q + 2)
                    if k == 0:
                        pe.wait_ge(s_v, v + 1)
                    if k % 2 == 0 and q >= 2:
                        pe.wait_ge(s_oT, q // 2)
                    for c in range(HALVES):
                        for g in range(QUAD):
                            at = VW * head_of(v, QUAD * k + g)
                            ins = pe.matmul(outP[32 * g:32 * g + 32, k % 2, :], Vp[p][:, c, at:at + 32],
                                            prob[k % 2][:, g, c, :], start=(c == 0), stop=(c == HALVES - 1),
                                            skip_group_check=True)
                    ins.then_inc(s_pv, 1)
                elif kind == "fin":
                    pe.wait_ge(s_oT, 2 * v + k + 1)
                    pe.wait_ge(s_qk, min(v + 4, n))
                    if k == 1:
                        pe.wait_ge(s_on, 2 * v + 1)
                    elif v + 1 < n:
                        pe.wait_ge(s_v, v + 2)
                    else:
                        pe.wait_ge(s_x, v)
                    for c in range(HALVES):
                        for j in range(2):
                            at = (2 * c + j) * P
                            ins = pe.transpose(misc[:, at:at + P], oT[k][:, j, c * P:(c + 1) * P], ident[:, :])
                    ins.then_inc(s_fin_mm, 1)
                elif kind == "ont":
                    pe.wait_ge(s_on, 2 * v + 2)
                    for c in range(HALVES):
                        ins = pe.transpose(misc[:, c * P:(c + 1) * P], on[:, c, :], ident[:, :])
                    ins.then_inc(s_ont_mm, 1)
                elif kind == "out":
                    pe.wait_ge(s_onT, v + 1)
                    for c in range(HALVES):
                        ins = pe.matmul(misc[:, c * D:(c + 1) * D], onT[:, c * P:(c + 1) * P], W[v // B]["wo"][:, :],
                                        start=True, stop=True)
                    ins.then_inc(s_out_mm, 1)


CHUNKS = 4
CT = TILES // CHUNKS
CN = CT * P
E = 8


class Norm:

    def __init__(self, sb, ps, sem):
        self.bn = sb("bn", [P, TILES, 6], F32)
        self.mv = sb("mv", [P, TILES, 2], F32)
        self.nt = [sb(f"nt{i}", [P, CT], F32) for i in range(2)]
        self.rstd = sb("rstd", [P, TILES], F32)
        self.xnT = sb("xnT", [P, TILES * P], F32)
        self.turnP = [ps(f"turnP{i}", [P, CN]) for i in range(2)]
        self.s_bn = sem("s_bn")
        self.s_stat = sem("s_stat")
        self.s_newton = sem("s_newton")
        self.s_norm = sem("s_norm")
        self.s_turn = sem("s_turn")
        self.s_xnT = sem("s_xnT")


def norm_stats(dve, n, x_all):
    for c in range(CHUNKS):
        for i in range(CT * c, CT * c + CT):
            dve.bn_stats(n.bn[:, i, :], x_all[:, i, :]).then_inc(n.s_bn, 1)
        dve.wait_ge(n.s_bn, CT * (c + 1))
        for i in range(CT * c, CT * c + CT):
            ins = dve.bn_aggr(n.mv[:, i, :], n.bn[:, i, :])
        ins.then_inc(n.s_stat, 1)


def norm_rstd(pool, n, c, base=0, src=None, gain=1.0, eps=LN_EPS, out=None):
    src = n.mv[:, CT * c:CT * c + CT, 1] if src is None else src
    out = n.rstd[:, CT * c:CT * c + CT] if out is None else out
    newton_rsqrt(pool, n.s_newton, base, src, gain, eps, out, [t[:, :] for t in n.nt])


def norm_turn(pe, n, c, src, ident):
    pe.wait_ge(n.s_norm, c + 1)
    if c >= 2:
        pe.wait_ge(n.s_xnT, c - 1)
    for i in range(CT):
        ins = pe.transpose(n.turnP[c % 2][:, i * P:(i + 1) * P], src(i), ident[:, :])
    ins.then_inc(n.s_turn, 1)


def norm_copy(act, n, c):
    act.wait_ge(n.s_turn, c + 1)
    act.activation(n.xnT[:, c * CN:(c + 1) * CN], n.turnP[c % 2][:, :], ACT.Copy).then_inc(n.s_xnT, 1)


def ffn_phase(nc, name, x_all, ident, gated, experts, router, rms_scale, gate_scratch):
    n_up = 4
    n_down = 2 if gated else 4
    w_cols = experts.shape[2]
    with ExitStack() as ctx:
        def sb(nm, shape, dt=F32):
            return ctx.enter_context(nc.sbuf_tensor(f"{name}_{nm}", shape, dt))

        def ps(nm, shape):
            return ctx.enter_context(nc.psum_tensor(f"{name}_{nm}", shape, F32))

        sem = ctx.enter_context(phase_semaphores(nc, name))

        n = Norm(sb, ps, sem)
        xn = sb("xn", [P, TILES, D])
        rT = sb("rT", [P, E])
        iota = sb("iota", [P, 1, E])
        lg = sb("lg", [P, TILES, E])
        lg2 = sb("lg2", [P, TILES, E])
        t8 = sb("t8", [P, TILES, E])
        first = sb("first", [P, TILES, E])
        second = sb("second", [P, TILES, E])
        gates = sb("gates", [P, TILES, E])
        best = sb("best", [P, TILES, 1])
        at = sb("at", [P, TILES, 1])
        best2 = sb("best2", [P, TILES, 1])
        g1 = sb("g1", [P, TILES, 1])
        g2 = sb("g2", [P, TILES, 1])
        gT = sb("gT", [P, P])
        gb = [sb(f"gb{i}", [P, TILES, P]) for i in range(2)]
        wts = [sb(f"wts{i}", [P, w_cols]) for i in range(2)]
        hT = [sb(f"hT{i}", [P, n_down, CN]) for i in range(2)]
        sg = [sb(f"sg{i}", [P, CN]) for i in range(2)] if gated else None
        y = sb("y", [P, CN])
        acc = sb("acc", [P, TILES * P])
        if gated:
            xs = [sb(f"xs{i}", [P, CT, D]) for i in range(2)]
            sq = sb("sq", [P, D])
            ms = sb("ms", [P, TILES])
            rms = sb("rms", [P, TILES])
            nx = sb("nx", [P, TILES, 1])
            scale_b = sb("scale_b", [P, D])
            rT2 = sb("rT2", [P, E])
            ones = sb("ones", [P, P])

        hP = [ps(f"hP{i}", [P, CN]) for i in range(n_up)]
        yP = [ps(f"yP{i}", [P, CN]) for i in range(2)]
        routeP = yP[0]
        nyP = yP[1]

        s_in = sem("s_in")
        s_setup = sem("s_setup")
        s_sq = sem("s_sq")
        s_xh = sem("s_xh")
        s_skip = sem("s_skip")
        s_rT2 = sem("s_rT2")
        s_logit = sem("s_logit")
        s_route = sem("s_route")
        s_ed = sem("s_ed")
        s_spill = sem("s_spill")
        s_gb = [sem("s_gb0"), sem("s_gb1")]
        s_wts = [sem("s_wts0"), sem("s_wts1")]
        s_up = sem("s_up")
        s_free = sem("s_free")
        s_act = sem("s_act")
        s_h = sem("s_h")
        s_down = sem("s_down")
        s_y = sem("s_y")
        s_acc = sem("s_acc")
        s_back = sem("s_back")
        s_x = sem("s_x")

        U = 2 * CHUNKS
        PAIRS = E // 2

        block = ctx.enter_context(nc.Block())

        @block.sync
        def _(sp):
            sp.dma_start(rT[:, :], router).then_inc(s_in, 16)
            if gated:
                sp.dma_start(scale_b[:, :], rms_scale.partition_broadcast(P)).then_inc(s_in, 16)
            for e in range(2):
                sp.dma_start(wts[e][:, :], experts[e]).then_inc(s_wts[e], 16)
            sp.wait_ge(s_act, 1)
            sp.dma_start(gate_scratch, gT[:, :]).then_inc(s_spill, 16)
            sp.wait_ge(s_spill, 16)
            by_expert = gate_scratch.rearrange("(t e) p -> e t p", e=E)
            for e in range(2):
                sp.dma_start(gb[e][:, :, :], by_expert[e].partition_broadcast(P)).then_inc(s_gb[e], 16)
            with sp.Fori(0, PAIRS - 1) as i:
                for e in range(2):
                    sp.wait_ge(s_y, i * U + CHUNKS * (e + 1) + 1)
                    sp.dma_start(wts[e][:, :], experts[bass.ds(i * 2 + 2 + e, 1), :, :].rearrange("o p n -> p (o n)"))\
                        .then_inc(s_wts[e], 16)
                    sp.dma_start(gb[e][:, :, :], by_expert[bass.ds(i * 2 + 2 + e, 1), :, :]
                                 .rearrange("o t p -> (o t) p").partition_broadcast(P)).then_inc(s_gb[e], 16)

        @block.gpsimd
        def _(pool):
            pool.iota(iota[:, 0, :], [[1, E]], base=0, channel_multiplier=0,
                      allow_small_or_imprecise_dtypes=True).then_inc(s_setup, 1)
            if gated:
                pool.memset(ones[:, :], 1.0).then_inc(s_setup, 1)
            pool.memset(acc[:, :], 0.0).then_inc(s_acc, 1)
            for c in range(CHUNKS):
                pool.wait_ge(n.s_stat, c + 1)
                norm_rstd(pool, n, c, base=NEWTON_STEPS * c)
            if gated:
                for c in range(CHUNKS):
                    pool.wait_ge(s_sq, CT * (c + 1))
                    norm_rstd(pool, n, c, base=NEWTON_STEPS * (CHUNKS + c), src=ms[:, CT * c:CT * c + CT],
                              gain=1.0 / D, eps=RMS_EPS, out=rms[:, CT * c:CT * c + CT])
                for c in range(CHUNKS):
                    xt = x_all[:, CT * c:CT * c + CT, :]
                    pool.wait_ge(s_xh, c + 1)
                    pool.tensor_tensor(xt, xt, xn[:, CT * c:CT * c + CT, :], ALU.add).then_inc(s_skip, 1)

        @block.scalar
        def _(act):
            if gated:
                for c in range(CHUNKS):
                    act.wait_ge(s_xh, c + 1)
                    for i in range(CT * c, CT * c + CT):
                        if i:
                            act.wait_ge(s_sq, i)
                        act.activation(sq[:, :], xn[:, i, :], ACT.Square, accum_out=ms[:, i:i + 1]).then_inc(s_sq, 1)
                for c in range(CHUNKS):
                    act.wait_ge(n.s_norm, c + 1)
                    for i in range(CT * c, CT * c + CT):
                        act.wait_ge(s_sq, TILES + i)
                        act.activation(sq[:, :], xs[c % 2][:, i % CT, :], ACT.Square, accum_out=nx[:, i, :]).then_inc(s_sq, 1)
                    norm_copy(act, n, c)
                act.wait_ge(s_in, 32)
                act.activation(rT2[:, :], rT[:, :], ACT.Square).then_inc(s_rT2, 1)
            else:
                for c in range(CHUNKS):
                    norm_copy(act, n, c)
                act.wait_ge(s_route, ROUTE_TWO)
                act.activation(g2[:, :, :], best2[:, :, :], ACT.Exp).then_inc(s_ed, 1)
            act.wait_ge(s_down, 1)
            act.activation(gT[:, :], hP[0][:, 0:P], ACT.Copy).then_inc(s_act, 1)
            with act.Fori(0, PAIRS) as i:
                for u in range(U):
                    if gated:
                        for k in range(2):
                            act.wait_ge(s_up, i * (U * n_up) + u * n_up + 2 * k + 1)
                            if u == 0:
                                act.wait_ge(s_y, i * U + 1)
                            else:
                                act.wait_ge(s_free, i * (2 * U) + 2 * u + k - 1)
                            act.activation(sg[k][:, :], hP[2 * k][:, :], ACT.Silu).then_inc(s_act, 1)
                    else:
                        act.wait_ge(s_down, i * U + max(u - 1, 0) + 1)
                        for k in range(n_up):
                            e = u // CHUNKS
                            act.wait_ge(s_up, i * (U * n_up) + u * n_up + k + 1)
                            act.activation(hT[u % 2][:, k, :], hP[k][:, :], ACT.Gelu,
                                           bias=wts[e][:, 1024 + k:1025 + k]).then_inc(s_act, 1)

        @block.vector
        def _(dve):
            norm_stats(dve, n, x_all)
            for c in range(CHUNKS):
                dve.wait_ge(n.s_newton, NEWTON_STEPS * (c + 1))
                dve.wait_ge(n.s_stat, c + 1)
                for i in range(CT * c, CT * c + CT):
                    ins = dve.tensor_scalar(xn[:, i, :], x_all[:, i, :], n.mv[:, i, 0:1], n.rstd[:, i:i + 1],
                                            ALU.subtract, ALU.mult)
                ins.then_inc(s_xh if gated else n.s_norm, 1)
            if gated:
                dve.wait_ge(s_in, 32)
                for c in range(CHUNKS):
                    dve.wait_ge(n.s_newton, NEWTON_STEPS * (CHUNKS + c + 1))
                    dve.wait_ge(s_xh, c + 1)
                    if c >= 2:
                        dve.wait_ge(n.s_turn, c - 1)
                        dve.wait_ge(s_sq, TILES + CT * (c - 1))
                    for i in range(CT * c, CT * c + CT):
                        ins = dve.scalar_tensor_tensor(out=xs[c % 2][:, i % CT, :], in0=xn[:, i, :], scalar=rms[:, i:i + 1],
                                                       in1=scale_b[:, :], op0=ALU.mult, op1=ALU.mult)
                    ins.then_inc(n.s_norm, 1)

            k = 0

            def step(ins):
                nonlocal k
                ins.then_inc(s_route, 1)
                k += 1
                dve.wait_ge(s_route, k)

            full = [P, TILES, E]
            io = iota[:, :, :].to_broadcast(full)

            def first_of(values, extreme, reduce, onehot):
                step(dve.tensor_reduce(extreme[:, :, :], values[:, :, :], AX.X, reduce))
                step(dve.tensor_tensor(t8[:, :, :], values[:, :, :], extreme[:, :, :].to_broadcast(full), ALU.is_equal))
                step(dve.scalar_tensor_tensor(out=t8[:, :, :], in0=t8[:, :, :], scalar=-float(E), in1=io,
                                              op0=ALU.mult, op1=ALU.add))
                step(dve.tensor_reduce(at[:, :, :], t8[:, :, :], AX.X, ALU.min))
                step(dve.tensor_scalar(at[:, :, :], at[:, :, :], float(E), None, ALU.add))
                ins = dve.tensor_tensor(onehot[:, :, :], io, at[:, :, :].to_broadcast(full), ALU.is_equal)
                if onehot is gates:
                    ins.then_inc(s_y, 1)
                else:
                    step(ins)

            dve.wait_ge(s_setup, 1)
            dve.wait_ge(s_logit, 1)
            if gated:
                dve.wait_ge(s_sq, 2 * TILES)
                step(dve.tensor_copy(lg2[:, 0, :], nyP[:, 0:E]))
                step(dve.tensor_tensor(t8[:, :, :], lg2[:, 0:1, :].to_broadcast(full), nx[:, :, :].to_broadcast(full), ALU.add))
                step(dve.scalar_tensor_tensor(out=lg[:, :, :], in0=routeP[:, 0:P].rearrange("p (t e) -> p t e", e=E), scalar=-2.0,
                                              in1=t8[:, :, :], op0=ALU.mult, op1=ALU.add))
                first_of(lg, best, ALU.min, gates)
            else:
                step(dve.tensor_copy(lg[:, :, :], routeP[:, 0:P].rearrange("p (t e) -> p t e", e=E)))
                first_of(lg, best, ALU.max, first)
                step(dve.scalar_tensor_tensor(out=lg2[:, :, :], in0=first[:, :, :], scalar=-3e38, in1=lg[:, :, :],
                                              op0=ALU.mult, op1=ALU.add))
                first_of(lg2, best2, ALU.max, second)
                step(dve.tensor_tensor(best2[:, :, :], best2[:, :, :], best[:, :, :], ALU.subtract))
                assert k == ROUTE_TWO
                dve.wait_ge(s_ed, 1)
                step(dve.tensor_scalar(g1[:, :, :], g2[:, :, :], 1.0, None, ALU.add))
                step(dve.reciprocal(g1[:, :, :], g1[:, :, :]))
                step(dve.tensor_tensor(g2[:, :, :], g2[:, :, :], g1[:, :, :], ALU.mult))
                step(dve.tensor_tensor(first[:, :, :], first[:, :, :], g1[:, :, :].to_broadcast(full), ALU.mult))
                step(dve.tensor_tensor(second[:, :, :], second[:, :, :], g2[:, :, :].to_broadcast(full), ALU.mult))
                dve.tensor_tensor(gates[:, :, :], first[:, :, :], second[:, :, :], ALU.add).then_inc(s_y, 1)
            with dve.Fori(0, PAIRS) as i:
                for u in range(U):
                    e, c = divmod(u, CHUNKS)

                    def combine(u):
                        e, c = divmod(u, CHUNKS)
                        dve.wait_ge(s_down, i * U + u + 2)
                        if c == 0:
                            dve.wait_ge(s_gb[e], i * 16 + 16)
                        gate = gb[e][:, CT * c:CT * c + CT, :].rearrange("p t q -> p (t q)")
                        dve.wait_ge(s_acc, i * U + u + 1)
                        if gated:
                            dve.tensor_tensor(y[:, :], yP[u % 2][:, :], gate, ALU.mult).then_inc(s_y, 1)
                        else:
                            dve.scalar_tensor_tensor(out=y[:, :], in0=yP[u % 2][:, :], scalar=wts[e][:, 1028:1029],
                                                     in1=gate, op0=ALU.add, op1=ALU.mult).then_inc(s_y, 1)
                        dve.wait_ge(s_y, i * U + u + 2)
                        dve.tensor_tensor(acc[:, c * CN:(c + 1) * CN], acc[:, c * CN:(c + 1) * CN], y[:, :], ALU.add)\
                            .then_inc(s_acc, 1)

                    if gated:
                        for k in range(2):
                            dve.wait_ge(s_act, i * (2 * U) + 2 * u + k + 2)
                            dve.wait_ge(s_up, i * (U * n_up) + u * n_up + 2 * k + 2)
                            dve.tensor_tensor(hT[u % 2][:, k, :], hP[2 * k + 1][:, :], sg[k][:, :], ALU.mult)\
                                .then_inc(s_free, 1)
                        if u >= 1:
                            combine(u - 1)
                        if u == U - 1:
                            combine(u)
                    else:
                        combine(u)
            for c in range(CHUNKS):
                dve.wait_ge(s_back, c + 1)
                if gated:
                    dve.wait_ge(s_skip, c + 1)
                xt = x_all[:, CT * c:CT * c + CT, :]
                dve.tensor_tensor(xt, hP[c][:, :].rearrange("p (t d) -> p t d", d=D), xt, ALU.add).then_inc(s_x, 1)

        @block.tensor
        def _(pe):
            src = (lambda c, i: xs[c % 2][:, i, :]) if gated else (lambda c, i: xn[:, CT * c + i, :])
            for c in range(CHUNKS):
                norm_turn(pe, n, c, lambda i: src(c, i), ident)
            pe.wait_ge(s_in, 32 if gated else 16)
            if gated:
                pe.wait_ge(s_rT2, 1)
                pe.wait_ge(s_setup, 2)
                pe.matmul(nyP[:, 0:E], ones[:, :], rT2[:, :], start=True, stop=True)
            pe.wait_ge(n.s_xnT, CHUNKS)
            for i in range(TILES):
                ins = pe.matmul(routeP[:, i * E:(i + 1) * E], n.xnT[:, i * P:(i + 1) * P], rT[:, :], start=True, stop=True)
            ins.then_inc(s_logit, 1)
            pe.wait_ge(s_y, 1)
            pe.transpose(hP[0][:, 0:P], gates[:, :, :].rearrange("p t e -> p (t e)"), ident[:, :]).then_inc(s_down, 1)
            pe.wait_ge(s_act, 1)
            with pe.Fori(0, PAIRS) as i:
                def up(u):
                    e, c = divmod(u, CHUNKS)
                    if c == 0:
                        pe.wait_ge(s_wts[e], i * 16 + 16)
                    for k in range(n_up):
                        if gated:
                            blk = (2 if k % 2 == 0 else 0) + k // 2
                            if u == 0:
                                pe.wait_ge(s_y, i * U + 1)
                            elif k % 2 == 0:
                                pe.wait_ge(s_free, i * (2 * U) + 2 * u + k // 2 - 1)
                        else:
                            blk = k
                            if u == 0:
                                pe.wait_ge(s_act, i * (n_up * U) + 1)
                            else:
                                pe.wait_ge(s_act, i * (n_up * U) + (u - 1) * n_up + k + 2)
                        pe.matmul(hP[k][:, :], wts[e][:, blk * P:(blk + 1) * P], n.xnT[:, c * CN:(c + 1) * CN],
                                  start=True, stop=True).then_inc(s_up, 1)

                def down(u):
                    e, c = divmod(u, CHUNKS)
                    pe.wait_ge(s_y, i * U + max(u - 1, 0) + 1)
                    for k in range(n_down):
                        if gated:
                            pe.wait_ge(s_free, i * (2 * U) + 2 * u + k + 1)
                        else:
                            pe.wait_ge(s_act, i * (n_up * U) + u * n_up + k + 2)
                        ins = pe.matmul(yP[u % 2][:, :], wts[e][:, 512 + k * D:512 + (k + 1) * D], hT[u % 2][:, k, :],
                                        start=(k == 0), stop=(k == n_down - 1))
                    ins.then_inc(s_down, 1)

                up(0)
                for u in range(1, U):
                    up(u)
                    down(u - 1)
                down(U - 1)
            pe.wait_ge(s_acc, E * CHUNKS + 1)
            if not gated:
                pe.wait_ge(s_act, E * CHUNKS * n_up + 1)
            else:
                pe.wait_ge(s_free, 2 * E * CHUNKS)
            for c in range(CHUNKS):
                for i in range(CT):
                    j = CT * c + i
                    ins = pe.transpose(hP[c][:, i * P:(i + 1) * P], acc[:, j * P:(j + 1) * P], ident[:, :])
                ins.then_inc(s_back, 1)


ROUTE_TWO = 15

T = B
TAPS = 15


def across_phase(nc, name, x_all, ident, w_in, b_in, w_dyn, b_dyn, w_out, b_out):
    with ExitStack() as ctx:
        def sb(nm, shape, dt=F32):
            return ctx.enter_context(nc.sbuf_tensor(f"{name}_{nm}", shape, dt))

        def ps(nm, shape):
            return ctx.enter_context(nc.psum_tensor(f"{name}_{nm}", shape, F32))

        sem = ctx.enter_context(phase_semaphores(nc, name))

        n = Norm(sb, ps, sem)
        xn = [sb(f"xn{i}", [P, CT, D]) for i in range(2)]
        win = sb("win", [P, 3 * D])
        bin_b = sb("bin_b", [P, 3 * D])
        wdyn = sb("wdyn", [P, H * TAPS])
        bdyn_b = sb("bdyn_b", [P, H * TAPS])
        wout = sb("wout", [P, 2, D])
        bout_b = sb("bout_b", [P, 1, D])
        qkv = [sb(f"qkv{i}", [P, T, 3 * D]) for i in range(2)]
        vT = [sb(f"vT{i}", [P, P]) for i in range(2)]
        taps = [sb(f"taps{i}", [P, T * H, TAPS]) for i in range(2)]
        tstat = sb("tstat", [P, T * H, 1])
        trec = [sb(f"trec{i}", [P, T, H, 1]) for i in range(2)]
        score = sb("score", [P, T, T, H])
        astat = sb("astat", [P, T, 1, H])
        arec = sb("arec", [P, T, H, 1])
        product = [sb(f"product{i}", [P, T, D]) for i in range(2)]
        cproduct = [sb(f"cproduct{i}", [P, T, D]) for i in range(2)]
        cat = sb("cat", [P, T, 2, D])
        catT = [sb(f"catT{i}", [P, 2, P]) for i in range(2)]

        inP = [ps(f"inP{i}", [P, 3 * D]) for i in range(2)]
        attP = ps("attP", [P, 4, D])
        convP = ps("convP", [P, 4, D])
        turnP = ps("turnP", [P, 2, P])
        outP = ps("outP", [P, D])

        s_w = sem("s_w")
        s_xb = sem("s_xb")
        s_in_mm = sem("s_in_mm")
        s_qkv = sem("s_qkv")
        s_vT_mm = sem("s_vT_mm")
        s_vT = sem("s_vT")
        s_dyn_mm = sem("s_dyn_mm")
        s_dyn = sem("s_dyn")
        s_tmax = sem("s_tmax")
        s_texp = sem("s_texp")
        s_tsum = sem("s_tsum")
        s_taps = sem("s_taps")
        s_prod = sem("s_prod")
        s_score = sem("s_score")
        s_amax = sem("s_amax")
        s_aexp = sem("s_aexp")
        s_asum = sem("s_asum")
        s_arec = sem("s_arec")
        s_weigh = sem("s_weigh")
        s_att = sem("s_att")
        s_attn = sem("s_attn")
        s_cprod = sem("s_cprod")
        s_conv = sem("s_conv")
        s_convn = sem("s_convn")
        s_cat_mm = sem("s_cat_mm")
        s_cat = sem("s_cat")
        s_out_mm = sem("s_out_mm")
        s_x = sem("s_x")

        HT = T // 2

        def outD(m):
            return n.turnP[m % 2][:, 0:H * TAPS]

        block = ctx.enter_context(nc.Block())

        @block.sync
        def _(sp):
            sp.dma_start(win[:, :], w_in).then_inc(s_w, 16)
            sp.dma_start(bin_b[:, :], b_in.partition_broadcast(P)).then_inc(s_w, 16)
            sp.dma_start(wdyn[:, :], w_dyn).then_inc(s_w, 16)
            sp.dma_start(bdyn_b[:, :], b_dyn.partition_broadcast(P)).then_inc(s_w, 16)
            sp.dma_start(wout[:, :, :], w_out.rearrange("(c k) n -> k c n", k=P)).then_inc(s_w, 16)
            sp.dma_start(bout_b[:, 0, :], b_out.partition_broadcast(P)).then_inc(s_w, 16)

        @block.gpsimd
        def _(pool):
            for c in range(CHUNKS):
                pool.wait_ge(n.s_stat, c + 1)
                norm_rstd(pool, n, c, base=NEWTON_STEPS * c)
            pool.wait_ge(s_w, 96)
            pool.wait_ge(n.s_norm, CHUNKS)
            pool.tensor_tensor(x_all[:, :, :], x_all[:, :, :], bout_b[:, :, :].to_broadcast([P, TILES, D]), ALU.add)\
                .then_inc(s_xb, 1)
            for half in range(HALVES):
                pool.wait_ge(s_taps, half + 1)
                tap = taps[half][:, :, :].rearrange("p (t h) k -> p t h k", h=H)
                for t in range(T):
                    m = half * T + t
                    if m >= 2:
                        pool.wait_ge(s_conv, m - 1)
                    w = tap[:, t, :, T - 1 - t:2 * T - 1 - t].rearrange("p h (s o) -> p s h o", o=1)
                    pool.tensor_tensor(cproduct[m % 2][:, :, :].rearrange("p s (h d) -> p s h d", d=HD),
                                       qkv[half][:, :, 2 * D:].rearrange("p s (h d) -> p s h d", d=HD),
                                       w.to_broadcast([P, T, H, HD]), ALU.mult).then_inc(s_cprod, 1)

        @block.scalar
        def _(act):
            for c in range(CHUNKS):
                norm_copy(act, n, c)
            for half in range(HALVES):
                for t in range(T):
                    m = half * T + t
                    act.wait_ge(s_vT_mm, m + 1)
                    if m >= 2:
                        act.wait_ge(s_dyn_mm, m - 1)
                    act.activation(vT[m % 2][:, :], turnP[:, 0, :], ACT.Copy).then_inc(s_vT, 1)
                act.wait_ge(s_tmax, 2 * half + 2)
                tap = taps[half][:, :, :].rearrange("p a b -> p (a b)")
                act.activation(tap, tap, ACT.Exp).then_inc(s_texp, 1)
            for half in range(HALVES):
                act.wait_ge(s_amax, 2 * half + 2)
                flat = score[:, :, :, :].rearrange("p a b c -> p (a b c)")
                act.activation(flat, flat, ACT.Exp, scale=SCALE).then_inc(s_aexp, 1)
                for t in range(T):
                    m = half * T + t
                    act.wait_ge(s_cat_mm, m + 1)
                    if m >= 2:
                        act.wait_ge(s_out_mm, m - 1)
                    act.activation(catT[m % 2][:, :, :], turnP[:, :, :], ACT.Copy).then_inc(s_cat, 1)

        @block.vector
        def _(dve):
            norm_stats(dve, n, x_all)
            for c in range(CHUNKS):
                dve.wait_ge(n.s_newton, NEWTON_STEPS * (c + 1))
                dve.wait_ge(n.s_stat, c + 1)
                if c >= 2:
                    dve.wait_ge(n.s_turn, c - 1)
                for i in range(CT):
                    j = CT * c + i
                    ins = dve.tensor_scalar(xn[c % 2][:, i, :], x_all[:, j, :], n.mv[:, j, 0:1], n.rstd[:, j:j + 1],
                                            ALU.subtract, ALU.mult)
                ins.then_inc(n.s_norm, 1)
            dve.wait_ge(s_w, 96)

            def project(half):
                for t in range(T):
                    m = half * T + t
                    dve.wait_ge(s_in_mm, m + 1)
                    dve.tensor_tensor(qkv[half][:, t, :], inP[m % 2][:, :], bin_b[:, :], ALU.add).then_inc(s_qkv, 1)
                    if t >= 1:
                        dynamic(half, t - 1)
                dynamic(half, T - 1)

            def dynamic(half, t):
                dve.wait_ge(s_dyn_mm, half * T + t + 1)
                flat = taps[half][:, :, :].rearrange("p (t h) k -> p t (h k)", h=H)
                dve.tensor_tensor(flat[:, t, :], outD(half * T + t), bdyn_b[:, :], ALU.add).then_inc(s_dyn, 1)

            def tap_max(half):
                dve.wait_ge(s_dyn, T * (half + 1))
                if half:
                    dve.wait_ge(s_tmax, 2)
                dve.tensor_reduce(tstat[:, :, :], taps[half][:, :, :], AX.X, ALU.max).then_inc(s_tmax, 1)
                dve.wait_ge(s_tmax, 2 * half + 1)
                dve.tensor_tensor(taps[half][:, :, :], taps[half][:, :, :],
                                  tstat[:, :, :].to_broadcast([P, T * H, TAPS]), ALU.subtract).then_inc(s_tmax, 1)

            def tap_sum(half):
                dve.wait_ge(s_texp, half + 1)
                flat = trec[half][:, :, :, :].rearrange("p t h o -> p (t h) o")
                dve.tensor_reduce(flat, taps[half][:, :, :], AX.X, ALU.add).then_inc(s_tsum, 1)
                dve.wait_ge(s_tsum, half + 1)
                dve.reciprocal(flat, flat).then_inc(s_taps, 1)

            def scores(half):
                if half:
                    dve.wait_ge(s_weigh, T * half)
                for t in range(T):
                    m = half * T + t
                    if m:
                        dve.wait_ge(s_score, m)
                    if half and t < 2:
                        dve.wait_ge(s_att, T * half)
                    q = qkv[half][:, t:t + 1, 0:D].to_broadcast([P, T, D])
                    dve.tensor_tensor(product[t % 2][:, :, :], q, qkv[half][:, :, D:2 * D], ALU.mult).then_inc(s_prod, 1)
                    dve.wait_ge(s_prod, m + 1)
                    dve.tensor_reduce(score[:, t, :, :],
                                      product[t % 2][:, :, :].rearrange("p s (h d) -> p s h d", d=HD),
                                      AX.X, ALU.add).then_inc(s_score, 1)

            def softmax(half):
                by_source = score[:, :, :, :].rearrange("p t s h -> p t h s")
                dve.wait_ge(s_score, T * (half + 1))
                if half:
                    dve.wait_ge(s_amax, 2)
                dve.tensor_reduce(astat[:, :, 0, :].rearrange("p t (h o) -> p t h o", o=1), by_source, AX.X, ALU.max).then_inc(s_amax, 1)
                dve.wait_ge(s_amax, 2 * half + 1)
                dve.tensor_tensor(score[:, :, :, :], score[:, :, :, :], astat[:, :, :, :].to_broadcast([P, T, T, H]),
                                  ALU.subtract).then_inc(s_amax, 1)
                dve.wait_ge(s_aexp, half + 1)
                if half:
                    dve.wait_ge(s_attn, 2 * half)
                dve.tensor_reduce(arec[:, :, :, :], by_source, AX.X, ALU.add).then_inc(s_asum, 1)
                dve.wait_ge(s_asum, half + 1)
                dve.reciprocal(arec[:, :, :, :], arec[:, :, :, :]).then_inc(s_arec, 1)

            def weigh(half):
                for t in range(T):
                    m = half * T + t
                    if t >= 2:
                        dve.wait_ge(s_att, m - 1)
                    else:
                        dve.wait_ge(s_score, T * (half + 1))
                    w = score[:, t, :, :].rearrange("p s (h o) -> p s h o", o=1)
                    dve.tensor_tensor(product[t % 2][:, :, :].rearrange("p s (h d) -> p s h d", d=HD),
                                      qkv[half][:, :, 2 * D:].rearrange("p s (h d) -> p s h d", d=HD),
                                      w.to_broadcast([P, T, H, HD]), ALU.mult).then_inc(s_weigh, 1)
                    if t == HT:
                        normalise(half, 0)
                normalise(half, 1)

            def normalise(half, j):
                g = 2 * half + j
                ts = slice(HT * j, HT * (j + 1))
                for c, (done, src, r, ready, out) in enumerate((
                        (s_att, attP, arec, s_arec, s_attn), (s_conv, convP, trec[half], s_taps, s_convn))):
                    dve.wait_ge(done, half * T + HT * (j + 1))
                    dve.wait_ge(ready, half + 1)
                    if half:
                        dve.wait_ge(s_cat_mm, T * (half - 1) + HT * (j + 1))
                    dve.tensor_tensor(cat[:, ts, c, :].rearrange("p t (h d) -> p t h d", d=HD),
                                      src[:, :, :].rearrange("p t (h d) -> p t h d", d=HD),
                                      r[:, ts, :, :].to_broadcast([P, HT, H, HD]), ALU.mult).then_inc(out, 1)

            def residual(half):
                for t in range(T):
                    m = half * T + t
                    dve.wait_ge(s_out_mm, m + 1)
                    if m == 0:
                        dve.wait_ge(s_xb, 1)
                    xt = x_all[:, HALVES * t + half, :]
                    dve.tensor_tensor(xt, outP[:, :], xt, ALU.add).then_inc(s_x, 1)

            project(0)
            tap_max(0)
            project(1)
            tap_sum(0)
            tap_max(1)
            scores(0)
            tap_sum(1)
            softmax(0)
            weigh(0)
            residual(0)
            scores(1)
            softmax(1)
            weigh(1)
            residual(1)

        @block.tensor
        def _(pe):
            for c in range(CHUNKS):
                norm_turn(pe, n, c, lambda i: xn[c % 2][:, i, :], ident)
            pe.wait_ge(s_w, 96)
            pe.wait_ge(n.s_xnT, CHUNKS)

            def into(m):
                half, t = divmod(m, T)
                at = (HALVES * t + half) * P
                if m >= 2:
                    pe.wait_ge(s_qkv, m - 1)
                pe.matmul(inP[m % 2][:, :], n.xnT[:, at:at + P], win[:, :], start=True, stop=True).then_inc(s_in_mm, 1)

            into(0)
            for m in range(HALVES * T):
                half, t = divmod(m, T)
                if m + 1 < HALVES * T:
                    into(m + 1)
                pe.wait_ge(s_qkv, m + 1)
                if m:
                    pe.wait_ge(s_vT, m)
                pe.transpose(turnP[:, 0, :], qkv[half][:, t, 2 * D:], ident[:, :]).then_inc(s_vT_mm, 1)
                pe.wait_ge(s_vT, m + 1)
                if m >= 2:
                    pe.wait_ge(s_dyn, m - 1)
                pe.matmul(outD(m), vT[m % 2][:, :], wdyn[:, :], start=True, stop=True).then_inc(s_dyn_mm, 1)
            pe.wait_ge(s_dyn, HALVES * T)

            def add_up(dst, product, ready, m, done):
                pe.wait_ge(ready, m + 1)
                for s in range(T):
                    ins = pe.matmul(dst[:, m % HT, :], ident[:, :], product[:, s, :], start=(s == 0), stop=(s == T - 1))
                ins.then_inc(done, 1)

            for half in range(HALVES):
                for t in range(T):
                    m = half * T + t
                    if m % HT == 0 and m:
                        pe.wait_ge(s_attn, m // HT)
                        pe.wait_ge(s_convn, m // HT)
                    add_up(attP, product[t % 2], s_weigh, m, s_att)
                    add_up(convP, cproduct[m % 2], s_cprod, m, s_conv)
                for t in range(T):
                    m = half * T + t
                    pe.wait_ge(s_attn, 2 * half + t // HT + 1)
                    pe.wait_ge(s_convn, 2 * half + t // HT + 1)
                    if m:
                        pe.wait_ge(s_cat, m)
                    for c in range(2):
                        ins = pe.transpose(turnP[:, c, :], cat[:, t, c, :], ident[:, :])
                    ins.then_inc(s_cat_mm, 1)
                    pe.wait_ge(s_cat, m + 1)
                    if m:
                        pe.wait_ge(s_x, m)
                    for c in range(2):
                        ins = pe.matmul(outP[:, :], catT[m % 2][:, c, :], wout[:, c, :], start=(c == 0), stop=(c == 1))
                    ins.then_inc(s_out_mm, 1)


def build_decoder(nc, a, out):
    with ExitStack() as ctx:
        def sb(name, shape, dt=F32):
            return ctx.enter_context(nc.sbuf_tensor(name, shape, dt))

        x_all = sb("x_all", [P, TILES, D])
        ident = sb("ident", [P, P])
        part_scratch = nc.dram_tensor("part_scratch", [2, 2, SLOTS, P, S], BF16, kind="Internal").ap()
        gate_scratch = nc.dram_tensor("gate_scratch", [TILES * E, P], F32, kind="Internal").ap()
        s_in = ctx.enter_context(nc.semaphore("s_in"))
        s_ident = ctx.enter_context(nc.semaphore("s_ident"))
        s_out = ctx.enter_context(nc.semaphore("s_out"))

        with ExitStack() as kv:
            ctxT = kv.enter_context(nc.sbuf_tensor("ctxT_sb", [P, B * S], F32))
            with nc.Block() as block:
                @block.sync
                def _(sp):
                    sp.dma_start(x_all[:, :, :], a["x"].rearrange("(t p) d -> p t d", p=P)).then_inc(s_in, 16)
                    sp.dma_start(ctxT[:, :], a["ctxT"]).then_inc(s_in, 16)
                    sp.wait_ge(s_in, 32)

                @block.gpsimd
                def _(pool):
                    pool.memset(ident[:, :], 0.0).then_inc(s_ident, 1)
                    pool.wait_ge(s_ident, 1)
                    pool.affine_select(out=ident[:, :], in_=ident[:, :], compare_op=ALU.not_equal, fill=1.0,
                                       base=0, pattern=[[-1, P]], channel_multiplier=1).then_inc(s_ident, 1)
                    pool.wait_ge(s_ident, 2)

            shared = {k: a[f"shared_{k}"] for k in ("wq", "wk", "wv", "wo")}
            cross = {k: a[f"cross_{k}"] for k in ("wq", "wk", "wv", "wo", "bq", "bk", "bv", "bo")}
            attention_phase(nc, "self_cross", x_all, ident,
                            [{**shared, "mqa": True, "ctx": False}, {**cross, "mqa": False, "ctx": True}],
                            ctxT, part_scratch)
        ffn_phase(nc, "ffn0", x_all, ident, False, a["experts0"], a["router0"], None, gate_scratch)
        across_phase(nc, "across", x_all, ident, a["across_in"], a["across_in_b"], a["across_dyn"], a["across_dyn_b"],
                     a["across_out"], a["across_out_b"])
        with ExitStack() as kv:
            ctxT = kv.enter_context(nc.sbuf_tensor("ctxT_sb1", [P, B * S], F32))
            with nc.Block() as block:
                @block.sync
                def _(sp):
                    sp.dma_start(ctxT[:, :], a["ctxT"]).then_inc(s_in, 16)
                    sp.wait_ge(s_in, 48)

            relative = {k: a[f"relative_{k}"] for k in ("wq", "wk", "wv", "wo", "w_rel")}
            attention_phase(nc, "relative", x_all, ident, [{**relative, "mqa": False, "ctx": True}], ctxT, part_scratch)
        ffn_phase(nc, "ffn1", x_all, ident, True, a["experts1"], a["router1"], a["rms_scale"], gate_scratch)
        with nc.Block() as block:
            @block.sync
            def _(sp):
                sp.dma_start(out.rearrange("(t p) d -> p t d", p=P), x_all[:, :, :]).then_inc(s_out, 16)
                sp.wait_ge(s_out, 16)


def kernel(**inputs):
    import numpy as np
    import concourse.bacc as bacc
    from concourse.bass_utils import run_bass_kernel_spmd

    i = {k: np.asarray(v) for k, v in inputs.items()}

    def by_dim(w):
        return w.reshape(-1, H, HD).transpose(0, 2, 1).reshape(-1, D)

    def blocks(w):
        e, k, n = w.shape
        return w.reshape(e, k // P, P, n).transpose(0, 2, 1, 3).reshape(e, P, -1)

    w_kv = i["L1_xattn_w_kv"]
    arrays = {
        "x": i["x"].reshape(-1, D), "ctxT": i["ctx_1024"].reshape(-1, D).T,
        "shared_wq": by_dim(i["L0_attn_Wq"]), "shared_wk": by_dim(np.tile(i["L0_attn_Wk"], (1, H))),
        "shared_wv": i["L0_attn_Wv"], "shared_wo": i["L0_attn_Wo"],
        "cross_wq": by_dim(i["L0_xattn_Wq"].T), "cross_wk": by_dim(i["L0_xattn_Wk"].T),
        "cross_wv": i["L0_xattn_Wv"].T, "cross_wo": i["L0_xattn_Wo"].T,
        "cross_bq": by_dim(i["L0_xattn_bq"]).T, "cross_bk": by_dim(i["L0_xattn_bk"]).T,
        "cross_bv": i["L0_xattn_bv"].reshape(D, 1), "cross_bo": i["L0_xattn_bo"],
        "router0": i["L0_ffn_router_w"].T,
        "experts0": np.concatenate([i["L0_ffn_w1"].transpose(0, 2, 1), blocks(i["L0_ffn_w2"].transpose(0, 2, 1)),
                                    blocks(i["L0_ffn_b1"][:, :, None]), blocks(i["L0_ffn_b2"][:, :, None])], -1),
        "across_in": i["L1_attn_in_proj_w"].T, "across_in_b": i["L1_attn_in_proj_b"],
        "across_dyn": i["L1_attn_dyn_w"].T, "across_dyn_b": i["L1_attn_dyn_b"],
        "across_out": i["L1_attn_out_proj_w"].T, "across_out_b": i["L1_attn_out_proj_b"],
        "relative_wq": by_dim(i["L1_xattn_w_q"]), "relative_wk": by_dim(w_kv[:, :D]),
        "relative_wv": w_kv[:, D:], "relative_wo": i["L1_xattn_w_proj"], "relative_w_rel": i["L1_xattn_w_rel"],
        "router1": i["L1_ffn_centroids"].T, "rms_scale": i["L1_ffn_scale"],
        "experts1": np.concatenate([i["L1_ffn_up_w"], blocks(i["L1_ffn_down_w"])], -1),
    }
    arrays = {k: np.ascontiguousarray(v) for k, v in arrays.items()}
    nc = bacc.Bacc("TRN2", target_bir_lowering=False, num_devices=1)
    aps = {k: nc.dram_tensor(k, v.shape, mybir.dt.from_np(v.dtype), kind="ExternalInput").ap() for k, v in arrays.items()}
    out = nc.dram_tensor("out", (B * S, D), F32, kind="ExternalOutput").ap()
    build_decoder(nc, aps, out)
    r = run_bass_kernel_spmd(nc, [arrays], core_ids=[0])
    return r.results[0]["out"].reshape(B, S, D)
```

```python
from contextlib import ExitStack, contextmanager

import concourse.bass as bass
from concourse import mybir

F32 = mybir.dt.float32
BF16 = mybir.dt.bfloat16
I32 = mybir.dt.int32
ALU = mybir.AluOpType
ACT = mybir.ActivationFunctionType
AX = mybir.AxisListType

P = 128
B, S, D = 8, 256, 128
H, HD = 16, 8
TILES = B * S // P
HALVES = S // P
LN_EPS = 1e-5
RMS_EPS = 1e-6
SCALE = HD ** -0.5
RSQRT_SEED = 1597463007.0

QUAD = 4
NQUAD = H // QUAD
SLOTS = 6
ROWS_QK = SLOTS * HD
ROW_REL = ROWS_QK
ROWS_MAX = 96
ROW_M = 96
ROWS_ALL = 98
VW = HD + 1
VCOLS = H * VW + 32
STACKS = 3
VBUFS = 4
SBANKS = 3


@contextmanager
def phase_semaphores(nc, name):
    taken = []

    def sem(nm):
        taken.append(nc.alloc_semaphore(f"{name}_{nm}"))
        return taken[-1]

    yield sem
    with nc.Block() as block:
        @block.gpsimd
        def _(pool):
            nc.clear_and_free_semaphores(taken)


def newton_rsqrt(pool, done, base, var, gain, eps, y, t):
    k = 0

    def step(ins):
        nonlocal k
        ins.then_inc(done, 1)
        k += 1
        pool.wait_ge(done, base + k)

    step(pool.tensor_scalar(t[0], var, gain, eps, ALU.mult, ALU.add))
    step(pool.tensor_scalar(y.bitcast(I32), t[0].bitcast(I32), -0.5, RSQRT_SEED, ALU.mult, ALU.add))
    for _ in range(3):
        step(pool.tensor_tensor(t[1], y, y, ALU.mult))
        step(pool.tensor_tensor(t[1], t[1], t[0], ALU.mult))
        step(pool.tensor_scalar(t[1], t[1], -0.5, 1.5, ALU.mult, ALU.add))
        step(pool.tensor_tensor(y, y, t[1], ALU.mult))
    assert k == NEWTON_STEPS


NEWTON_STEPS = 14


SCORES_LAG = 6
TICK = (
    (1, "negm", -1, 0), (1, "read_negm", -1, 0), (1, "norm", 2, 0),
    (2, "pv", -2, 2),
    (3, "fin", -2, 0), (4, "read_fin", -2, 0),
    (4, "xnt", 2, 0), (5, "read_xnt", 2, 0),
    (6, "qk", 2, 0), (7, "load", 1, 0), (7, "read_qk", 2, 0),
    (7, "pv", -2, 3), (8, "ot", -2, 1),
    (9, "v", 2, 0), (10, "read_v", 2, 0),
    (10, "fin", -2, 1), (11, "read_fin", -2, 1),
    (11, "pv", -1, 0), (12, "stat", 3, 0),
    (12, "ont", -2, 0), (13, "read_ont", -2, 0),
    (14, "out", -2, 0), (15, "read_out", -2, 0),
    (15, "pv", -1, 1), (15, "ot", -1, 0),
)


def attention_steps(n):
    out = []

    def add(kind, v, k=0):
        if 0 <= v < n:
            out.append((kind, v, k))

    add("stat", 0)
    add("stat", 1)
    for v in range(2):
        for kind in ("norm", "xnt", "read_xnt", "qk", "read_qk", "v", "read_v"):
            add(kind, v)
        if v == 0:
            add("load", 0)
    for t in range(n + 2):
        for h in range(H):
            m = H * (t - 1) + h - SCORES_LAG
            add("scores", m // H, m % H)
            add("max", t, h)
            for at, kind, dv, k in TICK:
                if at == h and (kind != "stat" or t + dv >= B):
                    add(kind, t + dv, k)
    return out


def attention_phase(nc, name, x_all, ident, layers, ctxT, scratch, stackQ, stackK, Vp):
    n = B * len(layers)
    with ExitStack() as ctx:
        def sb(nm, shape, dt):
            return ctx.enter_context(nc.sbuf_tensor(f"{name}_{nm}", shape, dt))

        def ps(nm, shape):
            return ctx.enter_context(nc.psum_tensor(f"{name}_{nm}", shape, F32))

        sem = ctx.enter_context(phase_semaphores(nc, name))

        bn = sb("bn", [P, TILES, 6], F32)
        mv = sb("mv", [P, TILES, 2], F32)
        nt = [sb(f"nt{i}", [P, TILES], F32) for i in range(2)]
        rstd = sb("rstd", [P, TILES], F32)
        xn = sb("xn", [P, HALVES, D], F32)
        xnT = [sb(f"xnT{i}", [P, S], F32) for i in range(2)]
        qk32 = sb("qk32", [P, 2, S], F32)
        r32 = sb("r32", [P, 2, S], F32)
        parts = sb("parts", [P, 3, 2, S], BF16)
        mx = [sb(f"mx{i}", [P, HALVES, H], F32) for i in range(2)]
        mparts = sb("mparts", [H, 2, S], BF16)
        prob = [sb(f"prob{i}", [P, QUAD, HALVES, S], F32) for i in range(2)]
        oT = [sb(f"oT{i}", [P, 2, S], F32) for i in range(2)]
        rec = sb("rec", [P, HALVES, 8, 1], F32)
        on = sb("on", [P, HALVES, D], F32)
        onT = sb("onT", [P, S], F32)

        scoresP = [ps(f"scoresP{i}", [P, HALVES, S]) for i in range(SBANKS)]
        maxP = [ps(f"maxP{i}", [P, HALVES, S]) for i in range(2)]
        outP = ps("outP", [P, 2, S])
        miscA = ps("miscA", [P, 512])
        miscB = ps("miscB", [P, 512])

        W = []
        for i, lay in enumerate(layers):
            w = {k: sb(f"{k}{i}", list(lay[k].shape), F32) for k in ("wq", "wk", "wv", "wo")}
            if lay.get("bq") is not None:
                for k in ("bq", "bk", "bv"):
                    w[k] = sb(f"{k}{i}", [P, 1], F32)
                w["bo"] = sb(f"bo{i}", [P, 1, D], F32)
                w["bvw"] = sb(f"bvw{i}", [P, P], F32)
            W.append(w)
        biased = [i for i, lay in enumerate(layers) if lay.get("bq") is not None]
        rel = layers[0].get("w_rel")
        rel_scratch = layers[0].get("rel_scratch")
        if rel is not None:
            wr = sb("wr", [H, 1], F32)
            wr1 = sb("wr1", [H, 1], F32)
            wparts = sb("wparts", [H, 3, 1], BF16)
            relrow = sb("relrow", [H, 5, S], BF16)
            pos = sb("pos", [H, S], F32)

        s_w = sem("s_w")
        s_bvw = sem("s_bvw")
        s_bo_mm = sem("s_bo_mm")
        s_bo = sem("s_bo")
        s_rel = sem("s_rel")
        s_rel_w = sem("s_rel_w")
        s_relrows = sem("s_relrows")
        s_bn = sem("s_bn")
        s_stat = sem("s_stat")
        s_newton = sem("s_newton")
        s_norm = sem("s_norm")
        s_xbias = sem("s_xbias")
        s_xnT_mm = sem("s_xnT_mm")
        s_xnT = sem("s_xnT")
        s_qk_mm = sem("s_qk_mm")
        s_qk = sem("s_qk")
        s_part = sem("s_part")
        s_parts = sem("s_parts")
        s_spill = sem("s_spill")
        s_load = [sem("s_load0"), sem("s_load1")]
        s_max_mm = sem("s_max_mm")
        s_max = sem("s_max")
        s_negm_mm = sem("s_negm_mm")
        s_mhi = sem("s_mhi")
        s_mlo = sem("s_mlo")
        s_mrows = sem("s_mrows")
        s_v_mm = sem("s_v_mm")
        s_v = sem("s_v")
        s_scores = sem("s_scores")
        s_exp = sem("s_exp")
        s_pv = sem("s_pv")
        s_oT = sem("s_oT")
        s_fin_mm = sem("s_fin_mm")
        s_rec = sem("s_rec")
        s_on = sem("s_on")
        s_ont_mm = sem("s_ont_mm")
        s_onT = sem("s_onT")
        s_out_mm = sem("s_out_mm")
        s_x = sem("s_x")

        STEPS = attention_steps(n)
        n_w = sum(4 + (4 if i in biased else 0) for i in range(len(layers)))

        def layer(v):
            return layers[v // B]

        def head_of(v, h):
            return 0 if layer(v)["mqa"] else h

        def loaded(v, half):
            shared = sum(layer(u)["mqa"] for u in range(v + 1))
            return 32 * (v + 1) - (16 * shared if half else 0)

        def stats(v):
            return min(v + 1, 2) + max(v - B + 1, 0)

        def stat_tiles(v):
            return {0: (0, HALVES), 1: (HALVES, TILES - HALVES)}.get(v, (HALVES * (v % B), HALVES))

        def misc_of(k):
            return miscB if k == 0 else miscA

        def kvT(v):
            if layer(v)["ctx"]:
                return ctxT[:, (v % B) * S:(v % B + 1) * S]
            return xnT[v % 2][:, :]

        block = ctx.enter_context(nc.Block())

        @block.sync
        def _(sp):
            if rel is not None:
                sp.dma_start(wr[:, :], rel).then_inc(s_rel_w, 16)
            for lay, w in zip(layers, W):
                for k in ("wq", "wk", "wv", "wo"):
                    sp.dma_start(w[k][:, :], lay[k]).then_inc(s_w, 16)
                if "bq" in w:
                    for k in ("bq", "bk", "bv"):
                        sp.dma_start(w[k][:, :], lay[k]).then_inc(s_w, 16)
                    sp.dma_start(w["bo"][:, 0, :], lay["bo"].partition_broadcast(P)).then_inc(s_w, 16)
            if rel is not None:
                sp.wait_ge(s_rel, 9)
                for qk, at, src in ((0, 0, relrow[:, 0:3, :]), (1, 3, relrow[:, 0:3, :]),
                                    (0, 3, relrow[:, 4:5, :].to_broadcast([H, 3, S])),
                                    (1, 0, relrow[:, 3:4, :].to_broadcast([H, 3, S]))):
                    sp.dma_start(rel_scratch[qk, at:at + 3].rearrange("c h q -> h c q"), src).then_inc(s_rel_w, 16)
                sp.wait_ge(s_rel_w, 16 * 5)
                for i in range(STACKS):
                    for qk, dst in ((0, stackQ[i]), (1, stackK[i])):
                        sp.dma_start(dst[ROW_REL:ROW_REL + 6, :, :], rel_scratch[qk]).then_inc(s_relrows, 16)

            def load(v):
                if v >= STACKS:
                    sp.wait_ge(s_scores, H * (v - STACKS + 1))
                sp.wait_ge(s_spill, 96 * (v + 1))
                for half in range(2):
                    lo = half * H // 2
                    sp.dma_start(stackQ[v % STACKS][0:ROWS_QK, lo:lo + H // 2, :],
                                 scratch[v % 2, 0].rearrange("s (d h) q -> (s d) h q", h=H)[:, lo:lo + H // 2, :])\
                        .then_inc(s_load[half], 16)
                    if layer(v)["mqa"]:
                        nk = 1 - half
                    else:
                        nk = H // 2
                    if nk:
                        sp.dma_start(stackK[v % STACKS][0:ROWS_QK, lo:lo + nk, :],
                                     scratch[v % 2, 1].rearrange("s (d h) q -> (s d) h q", h=H)[:, lo:lo + nk, :])\
                            .then_inc(s_load[half], 16)

            for kind, v, k in STEPS:
                if kind == "read_qk":
                    sp.wait_ge(s_parts, v + 1)
                    if v >= 2:
                        sp.wait_ge(s_load[0], loaded(v - 2, 0))
                        sp.wait_ge(s_load[1], loaded(v - 2, 1))
                    for qk, groups in ((0, ((0, 1, 3), (1, 1, 2), (2, 1, 1))), (1, ((0, 3, 1), (0, 2, 1), (0, 1, 1)))):
                        slot = 0
                        for part, many, times in groups:
                            src = parts[:, part:part + many, qk, :]
                            if times > 1:
                                src = parts[:, part:part + 1, qk, :].to_broadcast([P, times, S])
                            m = many * times
                            sp.dma_start(scratch[v % 2, qk, slot:slot + m].rearrange("s p q -> p s q"), src)\
                                .then_inc(s_spill, 16)
                            slot += m
                elif kind == "load":
                    load(v)
                elif kind == "read_negm":
                    sp.wait_ge(s_mlo, v + 1)
                    for c in range(2):
                        sp.dma_start(stackQ[v % STACKS][ROW_M + c:ROW_M + c + 1, :, :], mparts[:, c, :])\
                            .then_inc(s_mrows, 16)

        @block.gpsimd
        def _(pool):
            if rel is not None:
                pool.iota(pos[:, :], [[1, S]], base=0, channel_multiplier=0,
                          allow_small_or_imprecise_dtypes=True).then_inc(s_rel, 1)
            b1 = B * biased[0] if biased else 0
            for kind, v, k in STEPS:
                if kind == "stat":
                    lo, m = stat_tiles(v)
                    pool.wait_ge(s_stat, stats(v))
                    if v >= B:
                        pool.wait_ge(s_norm, v - B + 1)
                    newton_rsqrt(pool, s_newton, NEWTON_STEPS * (stats(v) - 1), mv[:, lo:lo + m, 1], 1.0, LN_EPS,
                                 rstd[:, lo:lo + m], [t[:, 0:m] for t in nt])
                elif kind == "read_qk":
                    pool.wait_ge(s_qk, v + 1)
                    if v >= 1:
                        pool.wait_ge(s_spill, 96 * v)
                    pool.tensor_tensor(parts[:, 1, :, :], qk32[:, :, :], parts[:, 0, :, :], ALU.subtract).then_inc(s_part, 1)
                    pool.tensor_tensor(r32[:, :, :], qk32[:, :, :], parts[:, 0, :, :], ALU.subtract).then_inc(s_part, 1)
                    pool.wait_ge(s_part, 2 * v + 2)
                    pool.tensor_tensor(parts[:, 2, :, :], r32[:, :, :], parts[:, 1, :, :], ALU.subtract).then_inc(s_parts, 1)
                    if v // B in biased:
                        xt = x_all[:, 2 * (v % B):2 * (v % B) + 2, :]
                        bo = W[v // B]["bo"][:, :, :].to_broadcast([P, HALVES, D])
                        if v == b1:
                            pool.wait_ge(s_bo, 1)
                        pool.wait_ge(s_norm, v + 1)
                        pool.tensor_tensor(xt, xt, bo, ALU.add).then_inc(s_xbias, 1)

        @block.scalar
        def _(act):
            for i in biased:
                act.wait_ge(s_w, 16 * n_w)
                act.activation(W[i]["bvw"][:, :], ident[:, :], ACT.Identity, bias=W[i]["bv"][:, 0:1], scale=0.0)\
                    .then_inc(s_bvw, 1)
            for kind, v, k in STEPS:
                if kind == "read_xnt":
                    act.wait_ge(s_xnT_mm, v + 1)
                    act.activation(xnT[v % 2][:, :], miscA[:, 0:S], ACT.Copy).then_inc(s_xnT, 1)
                elif kind == "read_qk":
                    act.wait_ge(s_qk_mm, v + 1)
                    if v >= 1:
                        act.wait_ge(s_parts, v)
                        act.wait_ge(s_spill, 96 * v)
                    w = W[v // B]
                    if "bq" in w:
                        if v == B * biased[0]:
                            act.wait_ge(s_w, 16 * n_w)
                        for c, bias in ((0, w["bq"]), (1, w["bk"])):
                            act.activation(qk32[:, c, :], miscB[:, c * S:(c + 1) * S], ACT.Identity, bias=bias[:, 0:1])
                            ins = act.activation(parts[:, 0, c, :], miscB[:, c * S:(c + 1) * S], ACT.Identity, bias=bias[:, 0:1])
                    else:
                        act.activation(qk32[:, :, :].rearrange("p a b -> p (a b)"), miscB[:, :], ACT.Copy)
                        ins = act.activation(parts[:, 0, :, :].rearrange("p a b -> p (a b)"), miscB[:, :], ACT.Copy)
                    ins.then_inc(s_qk, 1)
                elif kind == "read_v":
                    act.wait_ge(s_v_mm, v + 1)
                    if v >= VBUFS:
                        act.wait_ge(s_pv, NQUAD * (v - VBUFS + 1))
                    nh = 1 if layer(v)["mqa"] else H
                    act.activation(
                        Vp[v % VBUFS][:, :, 0:nh * VW].rearrange("p k (h w) -> p k h w", w=VW)[:, :, :, 0:HD],
                        miscB[:, 0:2 * P].rearrange("p (k c) -> p k c", k=2)[:, :, 0:nh * HD].rearrange("p k (h w) -> p k h w", w=HD),
                        ACT.Copy).then_inc(s_v, 1)
                elif kind == "scores":
                    m = H * v + k
                    act.wait_ge(s_scores, m + 1)
                    q = m // QUAD
                    if k % QUAD == 0 and q >= 2:
                        act.wait_ge(s_pv, q - 1)
                    act.activation(prob[q % 2][:, m % QUAD, :, :].rearrange("p b c -> p (b c)"),
                                   scoresP[m % SBANKS][:, :, :].rearrange("p b c -> p (b c)"),
                                   ACT.Exp, scale=SCALE).then_inc(s_exp, 1)
                elif kind == "ot":
                    act.wait_ge(s_pv, NQUAD * v + 2 * k + 2)
                    if v >= 1:
                        act.wait_ge(s_fin_mm, 2 * (v - 1) + k + 1)
                    act.activation(oT[k][:, :, :].rearrange("p a b -> p (a b)"),
                                   outP[:, :, :].rearrange("p a b -> p (a b)"), ACT.Copy).then_inc(s_oT, 1)
                elif kind == "read_ont":
                    act.wait_ge(s_ont_mm, v + 1)
                    if v >= 1:
                        act.wait_ge(s_out_mm, v)
                    act.activation(onT[:, :], miscA[:, 0:S], ACT.Copy).then_inc(s_onT, 1)

        @block.vector
        def _(dve):
            if rel is not None:
                dve.wait_ge(s_rel_w, 16)
                dve.wait_ge(s_rel, 1)
                k = 1

                def step(ins):
                    nonlocal k
                    ins.then_inc(s_rel, 1)
                    k += 1
                    dve.wait_ge(s_rel, k)

                step(dve.tensor_scalar(wr[:, :], wr[:, :], 1.0 / SCALE, None, ALU.mult))
                step(dve.tensor_copy(wparts[:, 0, :], wr[:, :]))
                step(dve.tensor_tensor(wr1[:, :], wr[:, :], wparts[:, 0, :], ALU.subtract))
                step(dve.tensor_copy(wparts[:, 1, :], wr1[:, :]))
                step(dve.tensor_tensor(wparts[:, 2, :], wr1[:, :], wparts[:, 1, :], ALU.subtract))
                step(dve.tensor_copy(relrow[:, 0:3, :], wparts[:, :, :].to_broadcast([H, 3, S])))
                step(dve.tensor_scalar(relrow[:, 3, :], pos[:, :], -1.0, None, ALU.mult))
                step(dve.tensor_copy(relrow[:, 4, :], pos[:, :]))
            for kind, v, k in STEPS:
                xt = x_all[:, 2 * (v % B):2 * (v % B) + 2, :]
                if kind == "stat":
                    lo, m = stat_tiles(v)
                    if v >= B:
                        dve.wait_ge(s_x, v - B + 1)
                    for c in range(lo, lo + m):
                        dve.bn_stats(bn[:, c, :], x_all[:, c, :]).then_inc(s_bn, 1)
                    dve.wait_ge(s_bn, HALVES if v == 0 else TILES + HALVES * (stats(v) - 2))
                    for c in range(lo, lo + m):
                        ins = dve.bn_aggr(mv[:, c, :], bn[:, c, :])
                    ins.then_inc(s_stat, 1)
                    if v == 0 and biased:
                        w = W[biased[0]]
                        dve.wait_ge(s_bo_mm, 1)
                        dve.tensor_tensor(w["bo"][:, 0, :], miscA[:, 0:D], w["bo"][:, 0, :], ALU.add).then_inc(s_bo, 1)
                elif kind == "norm":
                    dve.wait_ge(s_newton, NEWTON_STEPS * stats(v))
                    dve.wait_ge(s_stat, stats(v))
                    if v >= 1:
                        dve.wait_ge(s_xnT_mm, v)
                    for c in range(HALVES):
                        j = HALVES * (v % B) + c
                        ins = dve.tensor_scalar(xn[:, c, :], xt[:, c, :], mv[:, j, 0:1], rstd[:, j:j + 1],
                                                ALU.subtract, ALU.mult)
                    ins.then_inc(s_norm, 1)
                elif kind == "max":
                    m = H * v + k
                    dve.wait_ge(s_max_mm, m + 1)
                    if k == 0 and v >= 2:
                        dve.wait_ge(s_negm_mm, v - 1)
                    dve.tensor_reduce(mx[v % 2][:, :, k:k + 1], maxP[m % 2][:, :, :], AX.X, ALU.max).then_inc(s_max, 1)
                elif kind == "read_negm":
                    dve.wait_ge(s_negm_mm, v + 1)
                    if v >= 1:
                        dve.wait_ge(s_mrows, 32 * v)
                    dve.tensor_scalar(mparts[:, 0, :], miscA[0:H, 0:S], -1.0, None, ALU.mult).then_inc(s_mhi, 1)
                    dve.wait_ge(s_mhi, v + 1)
                    dve.scalar_tensor_tensor(out=mparts[:, 1, :], in0=miscA[0:H, 0:S], scalar=-1.0,
                                             in1=mparts[:, 0, :], op0=ALU.mult, op1=ALU.subtract).then_inc(s_mlo, 1)
                elif kind == "read_fin":
                    m = 2 * v + k
                    dve.wait_ge(s_fin_mm, m + 1)
                    if m >= 1:
                        dve.wait_ge(s_on, m)
                    grouped = misc_of(k)[:, :].rearrange("p (q h c) -> p q h c", q=HALVES, c=32)
                    dve.reciprocal(rec[:, :, :, :], grouped[:, :, :, HD:HD + 1]).then_inc(s_rec, 1)
                    dve.wait_ge(s_rec, m + 1)
                    if k == 0 and v >= 1:
                        dve.wait_ge(s_ont_mm, v)
                    dve.tensor_tensor(on[:, :, k * 64:(k + 1) * 64].rearrange("p q (h d) -> p q h d", d=HD),
                                      grouped[:, :, :, 0:HD], rec[:, :, :, :].to_broadcast([P, HALVES, 8, HD]),
                                      ALU.mult).then_inc(s_on, 1)
                elif kind == "read_out":
                    dve.wait_ge(s_out_mm, v + 1)
                    if v // B in biased:
                        dve.wait_ge(s_xbias, v - B * biased[0] + 1)
                    dve.tensor_tensor(xt, miscB[:, 0:S].rearrange("p (q d) -> p q d", d=D), xt, ALU.add).then_inc(s_x, 1)

        @block.tensor
        def _(pe):
            pe.wait_ge(s_w, 16 * n_w)
            if biased:
                w = W[biased[0]]
                pe.wait_ge(s_bvw, 1)
                pe.matmul(miscA[:, 0:D], w["bvw"][:, :], w["wo"][:, :], start=True, stop=True).then_inc(s_bo_mm, 1)
                pe.wait_ge(s_bo, 1)
            for kind, v, k in STEPS:
                p = v % 2
                if kind == "xnt":
                    pe.wait_ge(s_norm, v + 1)
                    if v >= 3:
                        pe.wait_ge(s_mlo, v - 2)
                    elif v >= 1:
                        pe.wait_ge(s_xnT, v)
                    for c in range(HALVES):
                        ins = pe.transpose(miscA[:, c * P:(c + 1) * P], xn[:, c, :], ident[:, :])
                    ins.then_inc(s_xnT_mm, 1)
                elif kind == "qk":
                    pe.wait_ge(s_xnT, v + 1)
                    if v >= 4:
                        pe.wait_ge(s_on, 2 * (v - 4) + 1)
                    elif v >= 1:
                        pe.wait_ge(s_v, v)
                    w = W[v // B]
                    pe.matmul(miscB[:, 0:S], w["wq"][:, :], xnT[v % 2][:, :], start=True, stop=True)
                    pe.matmul(miscB[:, S:2 * S], w["wk"][:, :], kvT(v), start=True, stop=True).then_inc(s_qk_mm, 1)
                elif kind == "v":
                    pe.wait_ge(s_qk, v + 1)
                    nv = HD if layer(v)["mqa"] else D
                    for c in range(HALVES):
                        ins = pe.matmul(miscB[:, c * P:c * P + nv], kvT(v)[:, c * P:(c + 1) * P],
                                        W[v // B]["wv"][:, :], start=True, stop=True)
                    ins.then_inc(s_v_mm, 1)
                elif kind == "max":
                    m = H * v + k
                    if k == 0:
                        pe.wait_ge(s_load[0], loaded(v, 0))
                        if v == 0 and rel is not None:
                            pe.wait_ge(s_relrows, 16 * 2 * STACKS)
                    if k == H // 2:
                        pe.wait_ge(s_load[1], loaded(v, 1))
                    if m >= 2:
                        pe.wait_ge(s_max, m - 1)
                    for c in range(HALVES):
                        ins = pe.matmul(maxP[m % 2][:, c, :], stackQ[v % STACKS][0:ROWS_MAX, k, c * P:(c + 1) * P],
                                        stackK[v % STACKS][0:ROWS_MAX, head_of(v, k), :], start=True, stop=True)
                    ins.then_inc(s_max_mm, 1)
                elif kind == "negm":
                    pe.wait_ge(s_max, H * (v + 1))
                    if v >= 2:
                        pe.wait_ge(s_onT, v - 1)
                    else:
                        pe.wait_ge(s_xnT, min(v + 3, n))
                    for c in range(HALVES):
                        ins = pe.transpose(miscA[0:H, c * P:(c + 1) * P], mx[v % 2][:, c, :], ident[:, :])
                    ins.then_inc(s_negm_mm, 1)
                elif kind == "scores":
                    m = H * v + k
                    if k == 0:
                        pe.wait_ge(s_mrows, 32 * (v + 1))
                    if m >= SBANKS:
                        pe.wait_ge(s_exp, m - SBANKS + 1)
                    for c in range(HALVES):
                        ins = pe.matmul(scoresP[m % SBANKS][:, c, :],
                                        stackK[v % STACKS][:, head_of(v, k), c * P:(c + 1) * P],
                                        stackQ[v % STACKS][:, k, :], start=True, stop=True)
                    ins.then_inc(s_scores, 1)
                elif kind == "pv":
                    q = NQUAD * v + k
                    pe.wait_ge(s_exp, QUAD * (q + 1))
                    if k == 0:
                        pe.wait_ge(s_v, v + 1)
                    if k % 2 == 0 and q >= 2:
                        pe.wait_ge(s_oT, q // 2)
                    for c in range(HALVES):
                        for g in range(QUAD):
                            at = VW * head_of(v, QUAD * k + g)
                            ins = pe.matmul(outP[32 * g:32 * g + 32, k % 2, :], Vp[v % VBUFS][:, c, at:at + 32],
                                            prob[k % 2][:, g, c, :], start=(c == 0), stop=(c == HALVES - 1),
                                            skip_group_check=True)
                    ins.then_inc(s_pv, 1)
                elif kind == "fin":
                    pe.wait_ge(s_oT, 2 * v + k + 1)
                    if k == 0:
                        if v >= 1:
                            pe.wait_ge(s_x, v)
                        else:
                            pe.wait_ge(s_v, min(v + 4, n))
                    else:
                        pe.wait_ge(s_xnT, min(v + 5, n))
                        pe.wait_ge(s_mlo, min(v + 2, n))
                    for c in range(HALVES):
                        for j in range(2):
                            at = (2 * c + j) * P
                            ins = pe.transpose(misc_of(k)[:, at:at + P], oT[k][:, j, c * P:(c + 1) * P], ident[:, :])
                    ins.then_inc(s_fin_mm, 1)
                elif kind == "ont":
                    pe.wait_ge(s_on, 2 * v + 2)
                    for c in range(HALVES):
                        ins = pe.transpose(miscA[:, c * P:(c + 1) * P], on[:, c, :], ident[:, :])
                    ins.then_inc(s_ont_mm, 1)
                elif kind == "out":
                    pe.wait_ge(s_onT, v + 1)
                    pe.wait_ge(s_v, min(v + 5, n))
                    for c in range(HALVES):
                        ins = pe.matmul(miscB[:, c * D:(c + 1) * D], onT[:, c * P:(c + 1) * P], W[v // B]["wo"][:, :],
                                        start=True, stop=True)
                    ins.then_inc(s_out_mm, 1)


@contextmanager
def attention_buffers(nc):
    with ExitStack() as ctx:
        def sb(nm, shape, dt):
            return ctx.enter_context(nc.sbuf_tensor(nm, shape, dt))

        yield ([sb(f"stackQ{i}", [ROWS_ALL, H, S], BF16) for i in range(STACKS)],
               [sb(f"stackK{i}", [ROWS_ALL, H, S], BF16) for i in range(STACKS)],
               [sb(f"Vp{i}", [P, HALVES, VCOLS], F32) for i in range(VBUFS)])


def clear_stacks(dve, stackQ, stackK, s_zeros):
    for i in range(STACKS):
        for t in (stackQ[i], stackK[i]):
            dve.memset(t[0:ROW_M, :, :].rearrange("p h q -> p (h q)").bitcast(F32), 0.0).then_inc(s_zeros, 1)
    dve.wait_ge(s_zeros, 2 * STACKS)


def set_ones(pool, stackK, Vp, s_ones):
    for t in Vp:
        pool.memset(t[:, :, :], 1.0).then_inc(s_ones, 1)
    pool.wait_ge(s_ones, VBUFS)
    for t in stackK:
        pool.memset(t[ROW_M:ROWS_ALL, :, :], 1.0).then_inc(s_ones, 1)
    pool.wait_ge(s_ones, VBUFS + STACKS)


CHUNKS = 4
CT = TILES // CHUNKS
CN = CT * P
E = 8


class Norm:

    def __init__(self, sb, ps, sem):
        self.bn = sb("bn", [P, TILES, 6], F32)
        self.mv = sb("mv", [P, TILES, 2], F32)
        self.nt = [sb(f"nt{i}", [P, CT], F32) for i in range(2)]
        self.rstd = sb("rstd", [P, TILES], F32)
        self.xnT = sb("xnT", [P, TILES * P], F32)
        self.turnP = [ps(f"turnP{i}", [P, CN]) for i in range(2)]
        self.s_bn = sem("s_bn")
        self.s_stat = sem("s_stat")
        self.s_newton = sem("s_newton")
        self.s_norm = sem("s_norm")
        self.s_turn = sem("s_turn")
        self.s_xnT = sem("s_xnT")


def norm_stats(dve, n, x_all):
    for c in range(CHUNKS):
        for i in range(CT * c, CT * c + CT):
            dve.bn_stats(n.bn[:, i, :], x_all[:, i, :]).then_inc(n.s_bn, 1)
        dve.wait_ge(n.s_bn, CT * (c + 1))
        for i in range(CT * c, CT * c + CT):
            ins = dve.bn_aggr(n.mv[:, i, :], n.bn[:, i, :])
        ins.then_inc(n.s_stat, 1)


def norm_rstd(pool, n, c, base=0, src=None, gain=1.0, eps=LN_EPS, out=None):
    src = n.mv[:, CT * c:CT * c + CT, 1] if src is None else src
    out = n.rstd[:, CT * c:CT * c + CT] if out is None else out
    newton_rsqrt(pool, n.s_newton, base, src, gain, eps, out, [t[:, :] for t in n.nt])


def norm_turn(pe, n, c, src, ident):
    pe.wait_ge(n.s_norm, c + 1)
    if c >= 2:
        pe.wait_ge(n.s_xnT, c - 1)
    for i in range(CT):
        ins = pe.transpose(n.turnP[c % 2][:, i * P:(i + 1) * P], src(i), ident[:, :])
    ins.then_inc(n.s_turn, 1)


def norm_copy(act, n, c):
    act.wait_ge(n.s_turn, c + 1)
    act.activation(n.xnT[:, c * CN:(c + 1) * CN], n.turnP[c % 2][:, :], ACT.Copy).then_inc(n.s_xnT, 1)


def ffn_phase(nc, name, x_all, ident, gated, experts, router, rms_scale, gate_scratch):
    n_up = 4
    n_down = 2 if gated else 4
    w_cols = experts.shape[2]
    with ExitStack() as ctx:
        def sb(nm, shape, dt=F32):
            return ctx.enter_context(nc.sbuf_tensor(f"{name}_{nm}", shape, dt))

        def ps(nm, shape):
            return ctx.enter_context(nc.psum_tensor(f"{name}_{nm}", shape, F32))

        sem = ctx.enter_context(phase_semaphores(nc, name))

        n = Norm(sb, ps, sem)
        xn = sb("xn", [P, TILES, D])
        rT = sb("rT", [P, E])
        iota = sb("iota", [P, 1, E])
        lg = sb("lg", [P, TILES, E])
        lg2 = sb("lg2", [P, TILES, E])
        t8 = sb("t8", [P, TILES, E])
        first = sb("first", [P, TILES, E])
        second = sb("second", [P, TILES, E])
        gates = sb("gates", [P, TILES, E])
        best = sb("best", [P, TILES, 1])
        at = sb("at", [P, TILES, 1])
        best2 = sb("best2", [P, TILES, 1])
        g1 = sb("g1", [P, TILES, 1])
        g2 = sb("g2", [P, TILES, 1])
        gT = sb("gT", [P, P])
        gb = [sb(f"gb{i}", [P, TILES, P]) for i in range(2)]
        wts = [sb(f"wts{i}", [P, w_cols]) for i in range(2)]
        hT = [sb(f"hT{i}", [P, n_down, CN]) for i in range(2)]
        sg = [sb(f"sg{i}", [P, CN]) for i in range(2)] if gated else None
        y = sb("y", [P, CN])
        acc = sb("acc", [P, TILES * P])
        if gated:
            xs = [sb(f"xs{i}", [P, CT, D]) for i in range(2)]
            sq = sb("sq", [P, D])
            ms = sb("ms", [P, TILES])
            rms = sb("rms", [P, TILES])
            nx = sb("nx", [P, TILES, 1])
            scale_b = sb("scale_b", [P, D])
            rT2 = sb("rT2", [P, E])
            ones = sb("ones", [P, P])

        hP = [ps(f"hP{i}", [P, CN]) for i in range(n_up)]
        yP = [ps(f"yP{i}", [P, CN]) for i in range(2)]
        routeP = yP[0]
        nyP = yP[1]

        s_in = sem("s_in")
        s_setup = sem("s_setup")
        s_sq = sem("s_sq")
        s_xh = sem("s_xh")
        s_skip = sem("s_skip")
        s_rT2 = sem("s_rT2")
        s_logit = sem("s_logit")
        s_route = sem("s_route")
        s_ed = sem("s_ed")
        s_spill = sem("s_spill")
        s_gb = [sem("s_gb0"), sem("s_gb1")]
        s_wts = [sem("s_wts0"), sem("s_wts1")]
        s_up = sem("s_up")
        s_free = sem("s_free")
        s_act = sem("s_act")
        s_h = sem("s_h")
        s_down = sem("s_down")
        s_y = sem("s_y")
        s_acc = sem("s_acc")
        s_back = sem("s_back")
        s_x = sem("s_x")

        U = 2 * CHUNKS
        PAIRS = E // 2

        block = ctx.enter_context(nc.Block())

        @block.sync
        def _(sp):
            sp.dma_start(rT[:, :], router).then_inc(s_in, 16)
            if gated:
                sp.dma_start(scale_b[:, :], rms_scale.partition_broadcast(P)).then_inc(s_in, 16)
            for e in range(2):
                sp.dma_start(wts[e][:, :], experts[e]).then_inc(s_wts[e], 16)
            sp.wait_ge(s_act, 1)
            sp.dma_start(gate_scratch, gT[:, :]).then_inc(s_spill, 16)
            sp.wait_ge(s_spill, 16)
            by_expert = gate_scratch.rearrange("(t e) p -> e t p", e=E)
            for e in range(2):
                sp.dma_start(gb[e][:, :, :], by_expert[e].partition_broadcast(P)).then_inc(s_gb[e], 16)
            with sp.Fori(0, PAIRS - 1) as i:
                for e in range(2):
                    sp.wait_ge(s_y, i * U + CHUNKS * (e + 1) + 1)
                    sp.dma_start(wts[e][:, :], experts[bass.ds(i * 2 + 2 + e, 1), :, :].rearrange("o p n -> p (o n)"))\
                        .then_inc(s_wts[e], 16)
                    sp.dma_start(gb[e][:, :, :], by_expert[bass.ds(i * 2 + 2 + e, 1), :, :]
                                 .rearrange("o t p -> (o t) p").partition_broadcast(P)).then_inc(s_gb[e], 16)

        @block.gpsimd
        def _(pool):
            pool.iota(iota[:, 0, :], [[1, E]], base=0, channel_multiplier=0,
                      allow_small_or_imprecise_dtypes=True).then_inc(s_setup, 1)
            if gated:
                pool.memset(ones[:, :], 1.0).then_inc(s_setup, 1)
            pool.memset(acc[:, :], 0.0).then_inc(s_acc, 1)
            for c in range(CHUNKS):
                pool.wait_ge(n.s_stat, c + 1)
                norm_rstd(pool, n, c, base=NEWTON_STEPS * c)
            if gated:
                for c in range(CHUNKS):
                    pool.wait_ge(s_sq, CT * (c + 1))
                    norm_rstd(pool, n, c, base=NEWTON_STEPS * (CHUNKS + c), src=ms[:, CT * c:CT * c + CT],
                              gain=1.0 / D, eps=RMS_EPS, out=rms[:, CT * c:CT * c + CT])
                for c in range(CHUNKS):
                    xt = x_all[:, CT * c:CT * c + CT, :]
                    pool.wait_ge(s_xh, c + 1)
                    pool.tensor_tensor(xt, xt, xn[:, CT * c:CT * c + CT, :], ALU.add).then_inc(s_skip, 1)

        @block.scalar
        def _(act):
            if gated:
                for c in range(CHUNKS):
                    act.wait_ge(s_xh, c + 1)
                    for i in range(CT * c, CT * c + CT):
                        if i:
                            act.wait_ge(s_sq, i)
                        act.activation(sq[:, :], xn[:, i, :], ACT.Square, accum_out=ms[:, i:i + 1]).then_inc(s_sq, 1)
                for c in range(CHUNKS):
                    act.wait_ge(n.s_norm, c + 1)
                    for i in range(CT * c, CT * c + CT):
                        act.wait_ge(s_sq, TILES + i)
                        act.activation(sq[:, :], xs[c % 2][:, i % CT, :], ACT.Square, accum_out=nx[:, i, :]).then_inc(s_sq, 1)
                    norm_copy(act, n, c)
                act.wait_ge(s_in, 32)
                act.activation(rT2[:, :], rT[:, :], ACT.Square).then_inc(s_rT2, 1)
            else:
                for c in range(CHUNKS):
                    norm_copy(act, n, c)
                act.wait_ge(s_route, ROUTE_TWO)
                act.activation(g2[:, :, :], best2[:, :, :], ACT.Exp).then_inc(s_ed, 1)
            act.wait_ge(s_down, 1)
            act.activation(gT[:, :], hP[0][:, 0:P], ACT.Copy).then_inc(s_act, 1)
            with act.Fori(0, PAIRS) as i:
                for u in range(U):
                    if gated:
                        for k in range(2):
                            act.wait_ge(s_up, i * (U * n_up) + u * n_up + 2 * k + 1)
                            if u == 0:
                                act.wait_ge(s_y, i * U + 1)
                            else:
                                act.wait_ge(s_free, i * (2 * U) + 2 * u + k - 1)
                            act.activation(sg[k][:, :], hP[2 * k][:, :], ACT.Silu).then_inc(s_act, 1)
                    else:
                        act.wait_ge(s_down, i * U + max(u - 1, 0) + 1)
                        for k in range(n_up):
                            e = u // CHUNKS
                            act.wait_ge(s_up, i * (U * n_up) + u * n_up + k + 1)
                            act.activation(hT[u % 2][:, k, :], hP[k][:, :], ACT.Gelu,
                                           bias=wts[e][:, 1024 + k:1025 + k]).then_inc(s_act, 1)

        @block.vector
        def _(dve):
            norm_stats(dve, n, x_all)
            for c in range(CHUNKS):
                dve.wait_ge(n.s_newton, NEWTON_STEPS * (c + 1))
                dve.wait_ge(n.s_stat, c + 1)
                for i in range(CT * c, CT * c + CT):
                    ins = dve.tensor_scalar(xn[:, i, :], x_all[:, i, :], n.mv[:, i, 0:1], n.rstd[:, i:i + 1],
                                            ALU.subtract, ALU.mult)
                ins.then_inc(s_xh if gated else n.s_norm, 1)
            if gated:
                dve.wait_ge(s_in, 32)
                for c in range(CHUNKS):
                    dve.wait_ge(n.s_newton, NEWTON_STEPS * (CHUNKS + c + 1))
                    dve.wait_ge(s_xh, c + 1)
                    if c >= 2:
                        dve.wait_ge(n.s_turn, c - 1)
                        dve.wait_ge(s_sq, TILES + CT * (c - 1))
                    for i in range(CT * c, CT * c + CT):
                        ins = dve.scalar_tensor_tensor(out=xs[c % 2][:, i % CT, :], in0=xn[:, i, :], scalar=rms[:, i:i + 1],
                                                       in1=scale_b[:, :], op0=ALU.mult, op1=ALU.mult)
                    ins.then_inc(n.s_norm, 1)

            k = 0

            def step(ins):
                nonlocal k
                ins.then_inc(s_route, 1)
                k += 1
                dve.wait_ge(s_route, k)

            full = [P, TILES, E]
            io = iota[:, :, :].to_broadcast(full)

            def first_of(values, extreme, reduce, onehot):
                step(dve.tensor_reduce(extreme[:, :, :], values[:, :, :], AX.X, reduce))
                step(dve.tensor_tensor(t8[:, :, :], values[:, :, :], extreme[:, :, :].to_broadcast(full), ALU.is_equal))
                step(dve.scalar_tensor_tensor(out=t8[:, :, :], in0=t8[:, :, :], scalar=-float(E), in1=io,
                                              op0=ALU.mult, op1=ALU.add))
                step(dve.tensor_reduce(at[:, :, :], t8[:, :, :], AX.X, ALU.min))
                step(dve.tensor_scalar(at[:, :, :], at[:, :, :], float(E), None, ALU.add))
                ins = dve.tensor_tensor(onehot[:, :, :], io, at[:, :, :].to_broadcast(full), ALU.is_equal)
                if onehot is gates:
                    ins.then_inc(s_y, 1)
                else:
                    step(ins)

            dve.wait_ge(s_setup, 1)
            dve.wait_ge(s_logit, 1)
            if gated:
                dve.wait_ge(s_sq, 2 * TILES)
                step(dve.tensor_copy(lg2[:, 0, :], nyP[:, 0:E]))
                step(dve.tensor_tensor(t8[:, :, :], lg2[:, 0:1, :].to_broadcast(full), nx[:, :, :].to_broadcast(full), ALU.add))
                step(dve.scalar_tensor_tensor(out=lg[:, :, :], in0=routeP[:, 0:P].rearrange("p (t e) -> p t e", e=E), scalar=-2.0,
                                              in1=t8[:, :, :], op0=ALU.mult, op1=ALU.add))
                first_of(lg, best, ALU.min, gates)
            else:
                step(dve.tensor_copy(lg[:, :, :], routeP[:, 0:P].rearrange("p (t e) -> p t e", e=E)))
                first_of(lg, best, ALU.max, first)
                step(dve.scalar_tensor_tensor(out=lg2[:, :, :], in0=first[:, :, :], scalar=-3e38, in1=lg[:, :, :],
                                              op0=ALU.mult, op1=ALU.add))
                first_of(lg2, best2, ALU.max, second)
                step(dve.tensor_tensor(best2[:, :, :], best2[:, :, :], best[:, :, :], ALU.subtract))
                assert k == ROUTE_TWO
                dve.wait_ge(s_ed, 1)
                step(dve.tensor_scalar(g1[:, :, :], g2[:, :, :], 1.0, None, ALU.add))
                step(dve.reciprocal(g1[:, :, :], g1[:, :, :]))
                step(dve.tensor_tensor(g2[:, :, :], g2[:, :, :], g1[:, :, :], ALU.mult))
                step(dve.tensor_tensor(first[:, :, :], first[:, :, :], g1[:, :, :].to_broadcast(full), ALU.mult))
                step(dve.tensor_tensor(second[:, :, :], second[:, :, :], g2[:, :, :].to_broadcast(full), ALU.mult))
                dve.tensor_tensor(gates[:, :, :], first[:, :, :], second[:, :, :], ALU.add).then_inc(s_y, 1)
            with dve.Fori(0, PAIRS) as i:
                for u in range(U):
                    e, c = divmod(u, CHUNKS)

                    def combine(u):
                        e, c = divmod(u, CHUNKS)
                        dve.wait_ge(s_down, i * U + u + 2)
                        if c == 0:
                            dve.wait_ge(s_gb[e], i * 16 + 16)
                        gate = gb[e][:, CT * c:CT * c + CT, :].rearrange("p t q -> p (t q)")
                        dve.wait_ge(s_acc, i * U + u + 1)
                        if gated:
                            dve.tensor_tensor(y[:, :], yP[u % 2][:, :], gate, ALU.mult).then_inc(s_y, 1)
                        else:
                            dve.scalar_tensor_tensor(out=y[:, :], in0=yP[u % 2][:, :], scalar=wts[e][:, 1028:1029],
                                                     in1=gate, op0=ALU.add, op1=ALU.mult).then_inc(s_y, 1)
                        dve.wait_ge(s_y, i * U + u + 2)
                        dve.tensor_tensor(acc[:, c * CN:(c + 1) * CN], acc[:, c * CN:(c + 1) * CN], y[:, :], ALU.add)\
                            .then_inc(s_acc, 1)

                    if gated:
                        for k in range(2):
                            dve.wait_ge(s_act, i * (2 * U) + 2 * u + k + 2)
                            dve.wait_ge(s_up, i * (U * n_up) + u * n_up + 2 * k + 2)
                            dve.tensor_tensor(hT[u % 2][:, k, :], hP[2 * k + 1][:, :], sg[k][:, :], ALU.mult)\
                                .then_inc(s_free, 1)
                        if u >= 1:
                            combine(u - 1)
                        if u == U - 1:
                            combine(u)
                    else:
                        combine(u)
            for c in range(CHUNKS):
                dve.wait_ge(s_back, c + 1)
                if gated:
                    dve.wait_ge(s_skip, c + 1)
                xt = x_all[:, CT * c:CT * c + CT, :]
                dve.tensor_tensor(xt, hP[c][:, :].rearrange("p (t d) -> p t d", d=D), xt, ALU.add).then_inc(s_x, 1)

        @block.tensor
        def _(pe):
            src = (lambda c, i: xs[c % 2][:, i, :]) if gated else (lambda c, i: xn[:, CT * c + i, :])
            for c in range(CHUNKS):
                norm_turn(pe, n, c, lambda i: src(c, i), ident)
            pe.wait_ge(s_in, 32 if gated else 16)
            if gated:
                pe.wait_ge(s_rT2, 1)
                pe.wait_ge(s_setup, 2)
                pe.matmul(nyP[:, 0:E], ones[:, :], rT2[:, :], start=True, stop=True)
            pe.wait_ge(n.s_xnT, CHUNKS)
            for i in range(TILES):
                ins = pe.matmul(routeP[:, i * E:(i + 1) * E], n.xnT[:, i * P:(i + 1) * P], rT[:, :], start=True, stop=True)
            ins.then_inc(s_logit, 1)
            pe.wait_ge(s_y, 1)
            pe.transpose(hP[0][:, 0:P], gates[:, :, :].rearrange("p t e -> p (t e)"), ident[:, :]).then_inc(s_down, 1)
            pe.wait_ge(s_act, 1)
            with pe.Fori(0, PAIRS) as i:
                def up(u):
                    e, c = divmod(u, CHUNKS)
                    if c == 0:
                        pe.wait_ge(s_wts[e], i * 16 + 16)
                    for k in range(n_up):
                        if gated:
                            blk = (2 if k % 2 == 0 else 0) + k // 2
                            if u == 0:
                                pe.wait_ge(s_y, i * U + 1)
                            elif k % 2 == 0:
                                pe.wait_ge(s_free, i * (2 * U) + 2 * u + k // 2 - 1)
                        else:
                            blk = k
                            if u == 0:
                                pe.wait_ge(s_act, i * (n_up * U) + 1)
                            else:
                                pe.wait_ge(s_act, i * (n_up * U) + (u - 1) * n_up + k + 2)
                        pe.matmul(hP[k][:, :], wts[e][:, blk * P:(blk + 1) * P], n.xnT[:, c * CN:(c + 1) * CN],
                                  start=True, stop=True).then_inc(s_up, 1)

                def down(u):
                    e, c = divmod(u, CHUNKS)
                    pe.wait_ge(s_y, i * U + max(u - 1, 0) + 1)
                    for k in range(n_down):
                        if gated:
                            pe.wait_ge(s_free, i * (2 * U) + 2 * u + k + 1)
                        else:
                            pe.wait_ge(s_act, i * (n_up * U) + u * n_up + k + 2)
                        ins = pe.matmul(yP[u % 2][:, :], wts[e][:, 512 + k * D:512 + (k + 1) * D], hT[u % 2][:, k, :],
                                        start=(k == 0), stop=(k == n_down - 1))
                    ins.then_inc(s_down, 1)

                up(0)
                for u in range(1, U):
                    up(u)
                    down(u - 1)
                down(U - 1)
            pe.wait_ge(s_acc, E * CHUNKS + 1)
            if not gated:
                pe.wait_ge(s_act, E * CHUNKS * n_up + 1)
            else:
                pe.wait_ge(s_free, 2 * E * CHUNKS)
            for c in range(CHUNKS):
                for i in range(CT):
                    j = CT * c + i
                    ins = pe.transpose(hP[c][:, i * P:(i + 1) * P], acc[:, j * P:(j + 1) * P], ident[:, :])
                ins.then_inc(s_back, 1)


ROUTE_TWO = 15

T = B
TAPS = 15


def across_phase(nc, name, x_all, ident, w_in, b_in, w_dyn, b_dyn, w_out, b_out):
    with ExitStack() as ctx:
        def sb(nm, shape, dt=F32):
            return ctx.enter_context(nc.sbuf_tensor(f"{name}_{nm}", shape, dt))

        def ps(nm, shape):
            return ctx.enter_context(nc.psum_tensor(f"{name}_{nm}", shape, F32))

        sem = ctx.enter_context(phase_semaphores(nc, name))

        n = Norm(sb, ps, sem)
        xn = [sb(f"xn{i}", [P, CT, D]) for i in range(2)]
        win = sb("win", [P, 3 * D])
        bin_b = sb("bin_b", [P, 3 * D])
        wdyn = sb("wdyn", [P, H * TAPS])
        bdyn_b = sb("bdyn_b", [P, H * TAPS])
        wout = sb("wout", [P, 2, D])
        bout_b = sb("bout_b", [P, 1, D])
        qkv = [sb(f"qkv{i}", [P, T, 3 * D]) for i in range(2)]
        vT = [sb(f"vT{i}", [P, P]) for i in range(2)]
        taps = [sb(f"taps{i}", [P, T * H, TAPS]) for i in range(2)]
        tstat = sb("tstat", [P, T * H, 1])
        trec = [sb(f"trec{i}", [P, T, H, 1]) for i in range(2)]
        score = sb("score", [P, T, T, H])
        astat = sb("astat", [P, T, 1, H])
        arec = sb("arec", [P, T, H, 1])
        product = [sb(f"product{i}", [P, T, D]) for i in range(2)]
        cproduct = [sb(f"cproduct{i}", [P, T, D]) for i in range(2)]
        cat = sb("cat", [P, T, 2, D])
        catT = [sb(f"catT{i}", [P, 2, P]) for i in range(2)]

        inP = [ps(f"inP{i}", [P, 3 * D]) for i in range(2)]
        attP = ps("attP", [P, 4, D])
        convP = ps("convP", [P, 4, D])
        turnP = ps("turnP", [P, 2, P])
        outP = ps("outP", [P, D])

        s_w = sem("s_w")
        s_xb = sem("s_xb")
        s_in_mm = sem("s_in_mm")
        s_qkv = sem("s_qkv")
        s_vT_mm = sem("s_vT_mm")
        s_vT = sem("s_vT")
        s_dyn_mm = sem("s_dyn_mm")
        s_dyn = sem("s_dyn")
        s_tmax = sem("s_tmax")
        s_texp = sem("s_texp")
        s_tsum = sem("s_tsum")
        s_taps = sem("s_taps")
        s_prod = sem("s_prod")
        s_score = sem("s_score")
        s_amax = sem("s_amax")
        s_aexp = sem("s_aexp")
        s_asum = sem("s_asum")
        s_arec = sem("s_arec")
        s_weigh = sem("s_weigh")
        s_att = sem("s_att")
        s_attn = sem("s_attn")
        s_cprod = sem("s_cprod")
        s_conv = sem("s_conv")
        s_convn = sem("s_convn")
        s_cat_mm = sem("s_cat_mm")
        s_cat = sem("s_cat")
        s_out_mm = sem("s_out_mm")
        s_x = sem("s_x")

        HT = T // 2

        def outD(m):
            return n.turnP[m % 2][:, 0:H * TAPS]

        block = ctx.enter_context(nc.Block())

        @block.sync
        def _(sp):
            sp.dma_start(win[:, :], w_in).then_inc(s_w, 16)
            sp.dma_start(bin_b[:, :], b_in.partition_broadcast(P)).then_inc(s_w, 16)
            sp.dma_start(wdyn[:, :], w_dyn).then_inc(s_w, 16)
            sp.dma_start(bdyn_b[:, :], b_dyn.partition_broadcast(P)).then_inc(s_w, 16)
            sp.dma_start(wout[:, :, :], w_out.rearrange("(c k) n -> k c n", k=P)).then_inc(s_w, 16)
            sp.dma_start(bout_b[:, 0, :], b_out.partition_broadcast(P)).then_inc(s_w, 16)

        @block.gpsimd
        def _(pool):
            for c in range(CHUNKS):
                pool.wait_ge(n.s_stat, c + 1)
                norm_rstd(pool, n, c, base=NEWTON_STEPS * c)
            pool.wait_ge(s_w, 96)
            pool.wait_ge(n.s_norm, CHUNKS)
            pool.tensor_tensor(x_all[:, :, :], x_all[:, :, :], bout_b[:, :, :].to_broadcast([P, TILES, D]), ALU.add)\
                .then_inc(s_xb, 1)
            for half in range(HALVES):
                pool.wait_ge(s_taps, half + 1)
                tap = taps[half][:, :, :].rearrange("p (t h) k -> p t h k", h=H)
                for t in range(T):
                    m = half * T + t
                    if m >= 2:
                        pool.wait_ge(s_conv, m - 1)
                    w = tap[:, t, :, T - 1 - t:2 * T - 1 - t].rearrange("p h (s o) -> p s h o", o=1)
                    pool.tensor_tensor(cproduct[m % 2][:, :, :].rearrange("p s (h d) -> p s h d", d=HD),
                                       qkv[half][:, :, 2 * D:].rearrange("p s (h d) -> p s h d", d=HD),
                                       w.to_broadcast([P, T, H, HD]), ALU.mult).then_inc(s_cprod, 1)

        @block.scalar
        def _(act):
            for c in range(CHUNKS):
                norm_copy(act, n, c)
            for half in range(HALVES):
                for t in range(T):
                    m = half * T + t
                    act.wait_ge(s_vT_mm, m + 1)
                    if m >= 2:
                        act.wait_ge(s_dyn_mm, m - 1)
                    act.activation(vT[m % 2][:, :], turnP[:, 0, :], ACT.Copy).then_inc(s_vT, 1)
                act.wait_ge(s_tmax, 2 * half + 2)
                tap = taps[half][:, :, :].rearrange("p a b -> p (a b)")
                act.activation(tap, tap, ACT.Exp).then_inc(s_texp, 1)
            for half in range(HALVES):
                act.wait_ge(s_amax, 2 * half + 2)
                flat = score[:, :, :, :].rearrange("p a b c -> p (a b c)")
                act.activation(flat, flat, ACT.Exp, scale=SCALE).then_inc(s_aexp, 1)
                for t in range(T):
                    m = half * T + t
                    act.wait_ge(s_cat_mm, m + 1)
                    if m >= 2:
                        act.wait_ge(s_out_mm, m - 1)
                    act.activation(catT[m % 2][:, :, :], turnP[:, :, :], ACT.Copy).then_inc(s_cat, 1)

        @block.vector
        def _(dve):
            norm_stats(dve, n, x_all)
            for c in range(CHUNKS):
                dve.wait_ge(n.s_newton, NEWTON_STEPS * (c + 1))
                dve.wait_ge(n.s_stat, c + 1)
                if c >= 2:
                    dve.wait_ge(n.s_turn, c - 1)
                for i in range(CT):
                    j = CT * c + i
                    ins = dve.tensor_scalar(xn[c % 2][:, i, :], x_all[:, j, :], n.mv[:, j, 0:1], n.rstd[:, j:j + 1],
                                            ALU.subtract, ALU.mult)
                ins.then_inc(n.s_norm, 1)
            dve.wait_ge(s_w, 96)

            def project(half):
                for t in range(T):
                    m = half * T + t
                    dve.wait_ge(s_in_mm, m + 1)
                    dve.tensor_tensor(qkv[half][:, t, :], inP[m % 2][:, :], bin_b[:, :], ALU.add).then_inc(s_qkv, 1)
                    if t >= 1:
                        dynamic(half, t - 1)
                dynamic(half, T - 1)

            def dynamic(half, t):
                dve.wait_ge(s_dyn_mm, half * T + t + 1)
                flat = taps[half][:, :, :].rearrange("p (t h) k -> p t (h k)", h=H)
                dve.tensor_tensor(flat[:, t, :], outD(half * T + t), bdyn_b[:, :], ALU.add).then_inc(s_dyn, 1)

            def tap_max(half):
                dve.wait_ge(s_dyn, T * (half + 1))
                if half:
                    dve.wait_ge(s_tmax, 2)
                dve.tensor_reduce(tstat[:, :, :], taps[half][:, :, :], AX.X, ALU.max).then_inc(s_tmax, 1)
                dve.wait_ge(s_tmax, 2 * half + 1)
                dve.tensor_tensor(taps[half][:, :, :], taps[half][:, :, :],
                                  tstat[:, :, :].to_broadcast([P, T * H, TAPS]), ALU.subtract).then_inc(s_tmax, 1)

            def tap_sum(half):
                dve.wait_ge(s_texp, half + 1)
                flat = trec[half][:, :, :, :].rearrange("p t h o -> p (t h) o")
                dve.tensor_reduce(flat, taps[half][:, :, :], AX.X, ALU.add).then_inc(s_tsum, 1)
                dve.wait_ge(s_tsum, half + 1)
                dve.reciprocal(flat, flat).then_inc(s_taps, 1)

            def scores(half):
                if half:
                    dve.wait_ge(s_weigh, T * half)
                for t in range(T):
                    m = half * T + t
                    if m:
                        dve.wait_ge(s_score, m)
                    if half and t < 2:
                        dve.wait_ge(s_att, T * half)
                    q = qkv[half][:, t:t + 1, 0:D].to_broadcast([P, T, D])
                    dve.tensor_tensor(product[t % 2][:, :, :], q, qkv[half][:, :, D:2 * D], ALU.mult).then_inc(s_prod, 1)
                    dve.wait_ge(s_prod, m + 1)
                    dve.tensor_reduce(score[:, t, :, :],
                                      product[t % 2][:, :, :].rearrange("p s (h d) -> p s h d", d=HD),
                                      AX.X, ALU.add).then_inc(s_score, 1)

            def softmax(half):
                by_source = score[:, :, :, :].rearrange("p t s h -> p t h s")
                dve.wait_ge(s_score, T * (half + 1))
                if half:
                    dve.wait_ge(s_amax, 2)
                dve.tensor_reduce(astat[:, :, 0, :].rearrange("p t (h o) -> p t h o", o=1), by_source, AX.X, ALU.max).then_inc(s_amax, 1)
                dve.wait_ge(s_amax, 2 * half + 1)
                dve.tensor_tensor(score[:, :, :, :], score[:, :, :, :], astat[:, :, :, :].to_broadcast([P, T, T, H]),
                                  ALU.subtract).then_inc(s_amax, 1)
                dve.wait_ge(s_aexp, half + 1)
                if half:
                    dve.wait_ge(s_attn, 2 * half)
                dve.tensor_reduce(arec[:, :, :, :], by_source, AX.X, ALU.add).then_inc(s_asum, 1)
                dve.wait_ge(s_asum, half + 1)
                dve.reciprocal(arec[:, :, :, :], arec[:, :, :, :]).then_inc(s_arec, 1)

            def weigh(half):
                for t in range(T):
                    m = half * T + t
                    if t >= 2:
                        dve.wait_ge(s_att, m - 1)
                    else:
                        dve.wait_ge(s_score, T * (half + 1))
                    w = score[:, t, :, :].rearrange("p s (h o) -> p s h o", o=1)
                    dve.tensor_tensor(product[t % 2][:, :, :].rearrange("p s (h d) -> p s h d", d=HD),
                                      qkv[half][:, :, 2 * D:].rearrange("p s (h d) -> p s h d", d=HD),
                                      w.to_broadcast([P, T, H, HD]), ALU.mult).then_inc(s_weigh, 1)
                    if t == HT:
                        normalise(half, 0)
                normalise(half, 1)

            def normalise(half, j):
                g = 2 * half + j
                ts = slice(HT * j, HT * (j + 1))
                for c, (done, src, r, ready, out) in enumerate((
                        (s_att, attP, arec, s_arec, s_attn), (s_conv, convP, trec[half], s_taps, s_convn))):
                    dve.wait_ge(done, half * T + HT * (j + 1))
                    dve.wait_ge(ready, half + 1)
                    if half:
                        dve.wait_ge(s_cat_mm, T * (half - 1) + HT * (j + 1))
                    dve.tensor_tensor(cat[:, ts, c, :].rearrange("p t (h d) -> p t h d", d=HD),
                                      src[:, :, :].rearrange("p t (h d) -> p t h d", d=HD),
                                      r[:, ts, :, :].to_broadcast([P, HT, H, HD]), ALU.mult).then_inc(out, 1)

            def residual(half):
                for t in range(T):
                    m = half * T + t
                    dve.wait_ge(s_out_mm, m + 1)
                    if m == 0:
                        dve.wait_ge(s_xb, 1)
                    xt = x_all[:, HALVES * t + half, :]
                    dve.tensor_tensor(xt, outP[:, :], xt, ALU.add).then_inc(s_x, 1)

            project(0)
            tap_max(0)
            project(1)
            tap_sum(0)
            tap_max(1)
            scores(0)
            tap_sum(1)
            softmax(0)
            weigh(0)
            residual(0)
            scores(1)
            softmax(1)
            weigh(1)
            residual(1)

        @block.tensor
        def _(pe):
            for c in range(CHUNKS):
                norm_turn(pe, n, c, lambda i: xn[c % 2][:, i, :], ident)
            pe.wait_ge(s_w, 96)
            pe.wait_ge(n.s_xnT, CHUNKS)

            def into(m):
                half, t = divmod(m, T)
                at = (HALVES * t + half) * P
                if m >= 2:
                    pe.wait_ge(s_qkv, m - 1)
                pe.matmul(inP[m % 2][:, :], n.xnT[:, at:at + P], win[:, :], start=True, stop=True).then_inc(s_in_mm, 1)

            into(0)
            for m in range(HALVES * T):
                half, t = divmod(m, T)
                if m + 1 < HALVES * T:
                    into(m + 1)
                pe.wait_ge(s_qkv, m + 1)
                if m:
                    pe.wait_ge(s_vT, m)
                pe.transpose(turnP[:, 0, :], qkv[half][:, t, 2 * D:], ident[:, :]).then_inc(s_vT_mm, 1)
                pe.wait_ge(s_vT, m + 1)
                if m >= 2:
                    pe.wait_ge(s_dyn, m - 1)
                pe.matmul(outD(m), vT[m % 2][:, :], wdyn[:, :], start=True, stop=True).then_inc(s_dyn_mm, 1)
            pe.wait_ge(s_dyn, HALVES * T)

            def add_up(dst, product, ready, m, done):
                pe.wait_ge(ready, m + 1)
                for s in range(T):
                    ins = pe.matmul(dst[:, m % HT, :], ident[:, :], product[:, s, :], start=(s == 0), stop=(s == T - 1))
                ins.then_inc(done, 1)

            for half in range(HALVES):
                for t in range(T):
                    m = half * T + t
                    if m % HT == 0 and m:
                        pe.wait_ge(s_attn, m // HT)
                        pe.wait_ge(s_convn, m // HT)
                    add_up(attP, product[t % 2], s_weigh, m, s_att)
                    add_up(convP, cproduct[m % 2], s_cprod, m, s_conv)
                for t in range(T):
                    m = half * T + t
                    pe.wait_ge(s_attn, 2 * half + t // HT + 1)
                    pe.wait_ge(s_convn, 2 * half + t // HT + 1)
                    if m:
                        pe.wait_ge(s_cat, m)
                    for c in range(2):
                        ins = pe.transpose(turnP[:, c, :], cat[:, t, c, :], ident[:, :])
                    ins.then_inc(s_cat_mm, 1)
                    pe.wait_ge(s_cat, m + 1)
                    if m:
                        pe.wait_ge(s_x, m)
                    for c in range(2):
                        ins = pe.matmul(outP[:, :], catT[m % 2][:, c, :], wout[:, c, :], start=(c == 0), stop=(c == 1))
                    ins.then_inc(s_out_mm, 1)


def build_decoder(nc, a, out):
    with ExitStack() as ctx:
        def sb(name, shape, dt=F32):
            return ctx.enter_context(nc.sbuf_tensor(name, shape, dt))

        x_all = sb("x_all", [P, TILES, D])
        ident = sb("ident", [P, P])
        part_scratch = nc.dram_tensor("part_scratch", [2, 2, SLOTS, P, S], BF16, kind="Internal").ap()
        rel_scratch = nc.dram_tensor("rel_scratch", [2, 6, H, S], BF16, kind="Internal").ap()
        gate_scratch = nc.dram_tensor("gate_scratch", [TILES * E, P], F32, kind="Internal").ap()
        s_in = ctx.enter_context(nc.semaphore("s_in"))
        s_ident = ctx.enter_context(nc.semaphore("s_ident"))
        s_out = ctx.enter_context(nc.semaphore("s_out"))
        s_zeros = ctx.enter_context(nc.semaphore("s_zeros"))
        s_ones = ctx.enter_context(nc.semaphore("s_ones"))
        stackQ, stackK, Vp = ctx.enter_context(attention_buffers(nc))

        with ExitStack() as kv:
            ctxT = kv.enter_context(nc.sbuf_tensor("ctxT_sb", [P, B * S], F32))
            with nc.Block() as block:
                @block.sync
                def _(sp):
                    sp.dma_start(x_all[:, :, :], a["x"].rearrange("(t p) d -> p t d", p=P)).then_inc(s_in, 16)
                    sp.dma_start(ctxT[:, :], a["ctxT"]).then_inc(s_in, 16)
                    sp.wait_ge(s_in, 32)

                @block.vector
                def _(dve):
                    clear_stacks(dve, stackQ, stackK, s_zeros)

                @block.gpsimd
                def _(pool):
                    pool.memset(ident[:, :], 0.0).then_inc(s_ident, 1)
                    pool.wait_ge(s_ident, 1)
                    pool.affine_select(out=ident[:, :], in_=ident[:, :], compare_op=ALU.not_equal, fill=1.0,
                                       base=0, pattern=[[-1, P]], channel_multiplier=1).then_inc(s_ident, 1)
                    pool.wait_ge(s_ident, 2)
                    set_ones(pool, stackK, Vp, s_ones)

            shared = {k: a[f"shared_{k}"] for k in ("wq", "wk", "wv", "wo")}
            cross = {k: a[f"cross_{k}"] for k in ("wq", "wk", "wv", "wo", "bq", "bk", "bv", "bo")}
            attention_phase(nc, "self_cross", x_all, ident,
                            [{**shared, "mqa": True, "ctx": False}, {**cross, "mqa": False, "ctx": True}],
                            ctxT, part_scratch, stackQ, stackK, Vp)
        ffn_phase(nc, "ffn0", x_all, ident, False, a["experts0"], a["router0"], None, gate_scratch)
        across_phase(nc, "across", x_all, ident, a["across_in"], a["across_in_b"], a["across_dyn"], a["across_dyn_b"],
                     a["across_out"], a["across_out_b"])
        with ExitStack() as kv:
            ctxT = kv.enter_context(nc.sbuf_tensor("ctxT_sb1", [P, B * S], F32))
            with nc.Block() as block:
                @block.sync
                def _(sp):
                    sp.dma_start(ctxT[:, :], a["ctxT"]).then_inc(s_in, 16)
                    sp.wait_ge(s_in, 48)

            relative = {k: a[f"relative_{k}"] for k in ("wq", "wk", "wv", "wo", "w_rel")}
            attention_phase(nc, "relative", x_all, ident, [{**relative, "rel_scratch": rel_scratch, "mqa": False, "ctx": True}], ctxT,
                            part_scratch, stackQ, stackK, Vp)
        ffn_phase(nc, "ffn1", x_all, ident, True, a["experts1"], a["router1"], a["rms_scale"], gate_scratch)
        with nc.Block() as block:
            @block.sync
            def _(sp):
                sp.dma_start(out.rearrange("(t p) d -> p t d", p=P), x_all[:, :, :]).then_inc(s_out, 16)
                sp.wait_ge(s_out, 16)


def kernel(**inputs):
    import numpy as np
    import concourse.bacc as bacc
    from concourse.bass_utils import run_bass_kernel_spmd

    i = {k: np.asarray(v) for k, v in inputs.items()}

    def by_dim(w):
        return w.reshape(-1, H, HD).transpose(0, 2, 1).reshape(-1, D)

    def blocks(w):
        e, k, n = w.shape
        return w.reshape(e, k // P, P, n).transpose(0, 2, 1, 3).reshape(e, P, -1)

    w_kv = i["L1_xattn_w_kv"]
    arrays = {
        "x": i["x"].reshape(-1, D), "ctxT": i["ctx_1024"].reshape(-1, D).T,
        "shared_wq": by_dim(i["L0_attn_Wq"]), "shared_wk": by_dim(np.tile(i["L0_attn_Wk"], (1, H))),
        "shared_wv": i["L0_attn_Wv"], "shared_wo": i["L0_attn_Wo"],
        "cross_wq": by_dim(i["L0_xattn_Wq"].T), "cross_wk": by_dim(i["L0_xattn_Wk"].T),
        "cross_wv": i["L0_xattn_Wv"].T, "cross_wo": i["L0_xattn_Wo"].T,
        "cross_bq": by_dim(i["L0_xattn_bq"]).T, "cross_bk": by_dim(i["L0_xattn_bk"]).T,
        "cross_bv": i["L0_xattn_bv"].reshape(D, 1), "cross_bo": i["L0_xattn_bo"],
        "router0": i["L0_ffn_router_w"].T,
        "experts0": np.concatenate([i["L0_ffn_w1"].transpose(0, 2, 1), blocks(i["L0_ffn_w2"].transpose(0, 2, 1)),
                                    blocks(i["L0_ffn_b1"][:, :, None]), blocks(i["L0_ffn_b2"][:, :, None])], -1),
        "across_in": i["L1_attn_in_proj_w"].T, "across_in_b": i["L1_attn_in_proj_b"],
        "across_dyn": i["L1_attn_dyn_w"].T, "across_dyn_b": i["L1_attn_dyn_b"],
        "across_out": i["L1_attn_out_proj_w"].T, "across_out_b": i["L1_attn_out_proj_b"],
        "relative_wq": by_dim(i["L1_xattn_w_q"]), "relative_wk": by_dim(w_kv[:, :D]),
        "relative_wv": w_kv[:, D:], "relative_wo": i["L1_xattn_w_proj"], "relative_w_rel": i["L1_xattn_w_rel"].reshape(H, 1),
        "router1": i["L1_ffn_centroids"].T, "rms_scale": i["L1_ffn_scale"],
        "experts1": np.concatenate([i["L1_ffn_up_w"], blocks(i["L1_ffn_down_w"])], -1),
    }
    arrays = {k: np.ascontiguousarray(v) for k, v in arrays.items()}
    nc = bacc.Bacc("TRN2", target_bir_lowering=False, num_devices=1)
    aps = {k: nc.dram_tensor(k, v.shape, mybir.dt.from_np(v.dtype), kind="ExternalInput").ap() for k, v in arrays.items()}
    out = nc.dram_tensor("out", (B * S, D), F32, kind="ExternalOutput").ap()
    build_decoder(nc, aps, out)
    r = run_bass_kernel_spmd(nc, [arrays], core_ids=[0])
    return r.results[0]["out"].reshape(B, S, D)
```

```python
from contextlib import ExitStack, contextmanager

import concourse.bass as bass
from concourse import mybir

F32 = mybir.dt.float32
BF16 = mybir.dt.bfloat16
F32R = mybir.dt.float32r
I32 = mybir.dt.int32
ALU = mybir.AluOpType
ACT = mybir.ActivationFunctionType
AX = mybir.AxisListType

P = 128
B, S, D = 8, 256, 128
H, HD = 16, 8
TILES = B * S // P
HALVES = S // P
LN_EPS = 1e-5
RMS_EPS = 1e-6
SCALE = HD ** -0.5
RSQRT_SEED = 1597463007.0

QUAD = 4
NQUAD = H // QUAD
SLOTS = 6
ROWS_QK = SLOTS * HD
PART_SLOTS = (((0, 1, 3), (1, 2, 3)), ((3, 1, 2), (0, 4, 2)), ((5, 1, 1), (2, 1, 1)))
ROW_REL = ROWS_QK
ROWS_MAX = 96
ROW_M = 96
ROWS_ALL = 98
VW = HD + 1
VCOLS = H * VW + 32
STACKS = 3
VBUFS = 4
SBANKS = 3


@contextmanager
def phase_semaphores(nc, name):
    taken = []

    def sem(nm):
        taken.append(nc.alloc_semaphore(f"{name}_{nm}"))
        return taken[-1]

    yield sem
    with nc.Block() as block:
        @block.gpsimd
        def _(pool):
            nc.clear_and_free_semaphores(taken)


def newton_rsqrt(eng, done, base, var, gain, eps, y, t):
    k = 0

    def step(ins):
        nonlocal k
        ins.then_inc(done, 1)
        k += 1
        eng.wait_ge(done, base + k)

    step(eng.tensor_scalar(t[0], var, gain, eps, ALU.mult, ALU.add))
    step(eng.tensor_scalar(y.bitcast(I32), t[0].bitcast(I32), -0.5, RSQRT_SEED, ALU.mult, ALU.add))
    for last in (False, True):
        step(eng.tensor_tensor(t[1], y, y, ALU.mult))
        step(eng.tensor_tensor(t[1], t[1], t[0], ALU.mult))
        if last:
            step(eng.tensor_scalar(t[0], t[1], 0.375, -1.25, ALU.mult, ALU.add))
            step(eng.tensor_tensor(t[1], t[1], t[0], ALU.mult))
            step(eng.tensor_scalar(t[1], t[1], 1.875, None, ALU.add))
        else:
            step(eng.tensor_scalar(t[1], t[1], -0.5, 1.5, ALU.mult, ALU.add))
        step(eng.tensor_tensor(y, y, t[1], ALU.mult))
    assert k == NEWTON_STEPS


NEWTON_STEPS = 12


SCORES_LAG = 6
TICK = (
    (0, "negm", -1, 0),
    (0, "read_negm", -1, 0),
    (1, "norm", 2, 0),
    (1, "fin", -2, 0),
    (2, "pv", -2, 2),
    (3, "xnt", 2, 0),
    (3, "load", 1, 0),
    (5, "read_fin", -2, 0),
    (5, "read_xnt", 2, 0),
    (7, "qk", 2, 0),
    (7, "read_qk", 2, 0),
    (7, "ot", -2, 1),
    (7, "pv", -2, 3),
    (9, "v", 2, 0),
    (10, "fin", -2, 1),
    (10, "read_fin", -2, 1),
    (10, "stat", 3, 0),
    (12, "read_v", 2, 0),
    (12, "pv", -1, 0),
    (12, "read_ont", -2, 0),
    (13, "ont", -2, 0),
    (15, "out", -2, 0),
    (15, "pv", -1, 1),
    (15, "read_out", -2, 0),
    (15, "ot", -1, 0),
)


def attention_steps(n):
    out = []

    def add(kind, v, k=0):
        if 0 <= v < n:
            out.append((kind, v, k))

    add("stat", 0)
    for v in range(2):
        for kind in ("norm", "xnt", "read_xnt", "qk", "read_qk", "v", "read_v"):
            add(kind, v)
            if v == 0 and kind == "read_qk":
                add("stat", 1)
        if v == 0:
            add("load", 0)
    for t in range(n + 2):
        for h in range(H):
            m = H * (t - 1) + h - SCORES_LAG
            add("scores", m // H, m % H)
            add("max", t, h)
            for at, kind, dv, k in TICK:
                if at == h and (kind != "stat" or t + dv >= B):
                    add(kind, t + dv, k)
    return out


def attention_phase(nc, name, x_all, ident, layers, ctxT, scratch, stackQ, stackK, Vp, first_load=None):
    n = B * len(layers)
    with ExitStack() as ctx:
        def sb(nm, shape, dt):
            return ctx.enter_context(nc.sbuf_tensor(f"{name}_{nm}", shape, dt))

        def ps(nm, shape):
            return ctx.enter_context(nc.psum_tensor(f"{name}_{nm}", shape, F32))

        sem = ctx.enter_context(phase_semaphores(nc, name))

        bn = sb("bn", [P, TILES, 6], F32)
        mv = sb("mv", [P, TILES, 2], F32)
        nt = [sb(f"nt{i}", [P, TILES], F32) for i in range(2)]
        rstd = sb("rstd", [P, TILES], F32)
        xn = sb("xn", [P, HALVES, D], F32)
        xnT = [sb(f"xnT{i}", [P, S], F32) for i in range(2)]
        qk32_ = [sb(f"qk32_{i}", [P, 2, S], F32) for i in range(2)]
        r32 = sb("r32", [P, 2, S], F32)
        parts_ = [sb(f"parts{i}", [P, 3, 2, S], BF16) for i in range(2)]
        mx = [sb(f"mx{i}", [P, HALVES, H], F32) for i in range(2)]
        mparts = sb("mparts", [H, 2, S], BF16)
        prob = [sb(f"prob{i}", [P, QUAD, HALVES, S], F32) for i in range(2)]
        oT = [sb(f"oT{i}", [P, 2, S], F32) for i in range(2)]
        rec = sb("rec", [P, HALVES, 8, 1], F32)
        on = sb("on", [P, HALVES, D], F32)
        onT = sb("onT", [P, S], F32)

        scoresP = [ps(f"scoresP{i}", [P, HALVES, S]) for i in range(SBANKS)]
        maxP = [ps(f"maxP{i}", [P, HALVES, S]) for i in range(2)]
        outP = ps("outP", [P, 2, S])
        miscA = ps("miscA", [P, 512])
        miscB = ps("miscB", [P, 512])

        W = []
        for i, lay in enumerate(layers):
            w = {k: sb(f"{k}{i}", list(lay[k].shape), F32) for k in ("wq", "wk", "wv", "wo")}
            if lay.get("bq") is not None:
                for k in ("bq", "bk", "bv"):
                    w[k] = sb(f"{k}{i}", [P, 1], F32)
                w["bo"] = sb(f"bo{i}", [P, 1, D], F32)
                w["bvw"] = sb(f"bvw{i}", [P, P], F32)
            W.append(w)
        biased = [i for i, lay in enumerate(layers) if lay.get("bq") is not None]
        rel = layers[0].get("w_rel")
        rel_scratch = layers[0].get("rel_scratch")
        if rel is not None:
            wr = sb("wr", [H, 1], F32)
            wr1 = sb("wr1", [H, 1], F32)
            wparts = sb("wparts", [H, 3, 1], BF16)
            relrow = sb("relrow", [H, 5, S], BF16)
            pos = sb("pos", [H, S], F32)

        s_x_in = [sem("s_x_in0"), sem("s_x_in1")]
        s_ctx = sem("s_ctx")
        s_ident = sem("s_ident")
        s_zeros = sem("s_zeros")
        s_vones = sem("s_vones")
        s_kones = sem("s_kones")
        s_w0 = sem("s_w0")
        s_w = sem("s_w")
        s_bvw = sem("s_bvw")
        s_bo_mm = sem("s_bo_mm")
        s_bo = sem("s_bo")
        s_rel = sem("s_rel")
        s_rel_w = sem("s_rel_w")
        s_relrows = sem("s_relrows")
        s_bn = sem("s_bn")
        s_stat = sem("s_stat")
        s_newton = sem("s_newton")
        s_norm = sem("s_norm")
        s_xbias = sem("s_xbias")
        s_xnT_mm = sem("s_xnT_mm")
        s_xnT = sem("s_xnT")
        s_qk_mm = sem("s_qk_mm")
        s_qk = sem("s_qk")
        s_part = sem("s_part")
        s_parts = sem("s_parts")
        s_spill = sem("s_spill")
        s_load = [sem("s_load0"), sem("s_load1")]
        s_max_mm = sem("s_max_mm")
        s_max = sem("s_max")
        s_negm_mm = sem("s_negm_mm")
        s_mhi = sem("s_mhi")
        s_mlo = sem("s_mlo")
        s_mrows = sem("s_mrows")
        s_v_mm = sem("s_v_mm")
        s_v = sem("s_v")
        s_scores = sem("s_scores")
        s_exp = sem("s_exp")
        s_pv = sem("s_pv")
        s_oT = sem("s_oT")
        s_fin_mm = sem("s_fin_mm")
        s_rec = sem("s_rec")
        s_on = sem("s_on")
        s_ont_mm = sem("s_ont_mm")
        s_onT = sem("s_onT")
        s_out_mm = sem("s_out_mm")
        s_x = sem("s_x")

        STEPS = attention_steps(n)
        n_w = sum(4 + (4 if i in biased else 0) for i in range(len(layers))) - 4

        def layer(v):
            return layers[v // B]

        def head_of(v, h):
            return 0 if layer(v)["mqa"] else h

        def loaded(v, half):
            shared = sum(layer(u)["mqa"] for u in range(v + 1))
            return 32 * (v + 1) - (16 * shared if half else 0)

        def stats(v):
            return min(v + 1, 2) + max(v - B + 1, 0)

        def stat_tiles(v):
            return {0: (0, HALVES), 1: (HALVES, TILES - HALVES)}.get(v, (HALVES * (v % B), HALVES))

        def misc_of(k):
            return miscB if k == 0 else miscA

        def kvT(v):
            if layer(v)["ctx"]:
                return ctxT[:, (v % B) * S:(v % B + 1) * S]
            return xnT[v % 2][:, :]

        block = ctx.enter_context(nc.Block())

        @block.sync
        def _(sp):
            if first_load:
                x_dram = first_load["x"].rearrange("(t p) d -> p t d", p=P)
                sp.dma_start(x_all[:, 0:HALVES, :], x_dram[:, 0:HALVES, :]).then_inc(s_x_in[0], 16)
                sp.dma_start(x_all[:, HALVES:TILES, :], x_dram[:, HALVES:TILES, :]).then_inc(s_x_in[1], 16)
            if rel is not None:
                sp.dma_start(wr[:, :], rel).then_inc(s_rel_w, 16)
            for lay, w in zip(layers, W):
                for k in ("wq", "wk", "wv", "wo"):
                    sp.dma_start(w[k][:, :], lay[k]).then_inc(s_w0 if w is W[0] else s_w, 16)
                if "bq" in w:
                    for k in ("bq", "bk", "bv"):
                        sp.dma_start(w[k][:, :], lay[k]).then_inc(s_w, 16)
                    sp.dma_start(w["bo"][:, 0, :], lay["bo"].partition_broadcast(P)).then_inc(s_w, 16)
            if first_load:
                sp.dma_start(ctxT[:, :], first_load["ctxT"]).then_inc(s_ctx, 16)
            if rel is not None:
                sp.wait_ge(s_rel, 9)
                for qk, at, src in ((0, 0, relrow[:, 0:3, :]), (1, 3, relrow[:, 0:3, :]),
                                    (0, 3, relrow[:, 4:5, :].to_broadcast([H, 3, S])),
                                    (1, 0, relrow[:, 3:4, :].to_broadcast([H, 3, S]))):
                    sp.dma_start(rel_scratch[qk, at:at + 3].rearrange("c h q -> h c q"), src).then_inc(s_rel_w, 16)
                sp.wait_ge(s_rel_w, 16 * 5)
                for i in range(STACKS):
                    for qk, dst in ((0, stackQ[i]), (1, stackK[i])):
                        sp.dma_start(dst[ROW_REL:ROW_REL + 6, :, :], rel_scratch[qk]).then_inc(s_relrows, 16)

            def load(v):
                if v >= STACKS:
                    sp.wait_ge(s_scores, H * (v - STACKS + 1))
                elif first_load:
                    sp.wait_ge(s_zeros, 2 * (v + 1))
                sp.wait_ge(s_spill, 96 * (v + 1))
                for half in range(2):
                    lo = half * H // 2
                    sp.dma_start(stackQ[v % STACKS][0:ROWS_QK, lo:lo + H // 2, :],
                                 scratch[v % 2, 0].rearrange("s (d h) q -> (s d) h q", h=H)[:, lo:lo + H // 2, :])\
                        .then_inc(s_load[half], 16)
                    if layer(v)["mqa"]:
                        nk = 1 - half
                    else:
                        nk = H // 2
                    if nk:
                        sp.dma_start(stackK[v % STACKS][0:ROWS_QK, lo:lo + nk, :],
                                     scratch[v % 2, 1].rearrange("s (d h) q -> (s d) h q", h=H)[:, lo:lo + nk, :])\
                            .then_inc(s_load[half], 16)

            for kind, v, k in STEPS:
                if kind == "read_qk":
                    if v >= 2:
                        sp.wait_ge(s_load[0], loaded(v - 2, 0))
                        sp.wait_ge(s_load[1], loaded(v - 2, 1))
                    parts = parts_[v % 2]
                    for part, (made, count) in enumerate(((s_qk, v + 1), (s_part, 2 * v + 1), (s_parts, v + 1))):
                        sp.wait_ge(made, count)
                        for qk, (first, step, times) in enumerate(PART_SLOTS[part]):
                            src = parts[:, part:part + 1, qk, :]
                            if times > 1:
                                src = src.to_broadcast([P, times, S])
                            to = scratch[v % 2, qk, first:first + step * (times - 1) + 1:step]
                            sp.dma_start(to.rearrange("s p q -> p s q"), src).then_inc(s_spill, 16)
                elif kind == "load":
                    load(v)
                elif kind == "read_negm":
                    sp.wait_ge(s_mlo, v + 1)
                    for c in range(2):
                        sp.dma_start(stackQ[v % STACKS][ROW_M + c:ROW_M + c + 1, :, :], mparts[:, c, :])\
                            .then_inc(s_mrows, 16)

        def cut(eng, v):
            qk32, parts = qk32_[v % 2], parts_[v % 2]
            eng.wait_ge(s_qk, v + 1)
            if v >= 1:
                eng.wait_ge(s_parts, v)
            if v >= 2:
                eng.wait_ge(s_spill, 96 * (v - 1))
            eng.tensor_tensor(parts[:, 1, :, :], qk32[:, :, :], parts[:, 0, :, :], ALU.subtract).then_inc(s_part, 1)
            eng.tensor_tensor(r32[:, :, :], qk32[:, :, :], parts[:, 0, :, :], ALU.subtract).then_inc(s_part, 1)
            eng.wait_ge(s_part, 2 * v + 2)
            eng.tensor_tensor(parts[:, 2, :, :], r32[:, :, :], parts[:, 1, :, :], ALU.subtract).then_inc(s_parts, 1)

        @block.gpsimd
        def _(pool):
            if first_load:
                pool.memset(ident[:, :], 0.0).then_inc(s_ident, 1)
                pool.wait_ge(s_ident, 1)
                pool.affine_select(out=ident[:, :], in_=ident[:, :], compare_op=ALU.not_equal, fill=1.0,
                                   base=0, pattern=[[-1, P]], channel_multiplier=1).then_inc(s_ident, 1)
                for t in Vp:
                    pool.memset(t[:, :, :], 1.0).then_inc(s_vones, 1)
            if rel is not None:
                pool.iota(pos[:, :], [[1, S]], base=0, channel_multiplier=0,
                          allow_small_or_imprecise_dtypes=True).then_inc(s_rel, 1)
            b1 = B * biased[0] if biased else 0
            for kind, v, k in STEPS:
                if kind == "stat" and v > 0:
                    lo, m = stat_tiles(v)
                    pool.wait_ge(s_stat, stats(v))
                    if v >= B:
                        pool.wait_ge(s_norm, v - B + 1)
                    newton_rsqrt(pool, s_newton, NEWTON_STEPS * (stats(v) - 1), mv[:, lo:lo + m, 1], 1.0, LN_EPS,
                                 rstd[:, lo:lo + m], [t[:, 0:m] for t in nt])
                elif kind == "read_qk":
                    cut(pool, v)
                    if v // B in biased:
                        xt = x_all[:, 2 * (v % B):2 * (v % B) + 2, :]
                        bo = W[v // B]["bo"][:, :, :].to_broadcast([P, HALVES, D])
                        if v == b1:
                            pool.wait_ge(s_bo, 1)
                        pool.wait_ge(s_norm, v + 1)
                        pool.tensor_tensor(xt, xt, bo, ALU.add).then_inc(s_xbias, 1)
                    if first_load and 1 <= v <= STACKS:
                        pool.wait_ge(s_parts, v + 1)
                        pool.memset(stackK[v - 1][ROW_M:ROWS_ALL, :, :], 1.0).then_inc(s_kones, 1)
                        pool.wait_ge(s_kones, v)

        @block.scalar
        def _(act):
            for kind, v, k in STEPS:
                if kind == "read_xnt":
                    act.wait_ge(s_xnT_mm, v + 1)
                    act.activation(xnT[v % 2][:, :], miscA[:, 0:S], ACT.Copy).then_inc(s_xnT, 1)
                    if v == 0:
                        for i in biased:
                            act.wait_ge(s_w, 16 * n_w)
                            if first_load:
                                act.wait_ge(s_ident, 2)
                            act.activation(W[i]["bvw"][:, :], ident[:, :], ACT.Identity, bias=W[i]["bv"][:, 0:1], scale=0.0)\
                                .then_inc(s_bvw, 1)
                elif kind == "read_qk":
                    act.wait_ge(s_qk_mm, v + 1)
                    qk32, parts = qk32_[v % 2], parts_[v % 2]
                    if v >= 2:
                        act.wait_ge(s_parts, v - 1)
                        act.wait_ge(s_spill, 96 * (v - 1))
                    w = W[v // B]
                    if "bq" in w:
                        if v == B * biased[0]:
                            act.wait_ge(s_w, 16 * n_w)
                        for c, bias in ((0, w["bq"]), (1, w["bk"])):
                            act.activation(qk32[:, c, :], miscB[:, c * S:(c + 1) * S], ACT.Identity, bias=bias[:, 0:1])
                            ins = act.activation(parts[:, 0, c, :], miscB[:, c * S:(c + 1) * S], ACT.Identity, bias=bias[:, 0:1])
                    else:
                        act.activation(qk32[:, :, :].rearrange("p a b -> p (a b)"), miscB[:, :], ACT.Copy)
                        ins = act.activation(parts[:, 0, :, :].rearrange("p a b -> p (a b)"), miscB[:, :], ACT.Copy)
                    ins.then_inc(s_qk, 1)
                elif kind == "read_v":
                    act.wait_ge(s_v_mm, v + 1)
                    if v == 0 and first_load:
                        act.wait_ge(s_vones, VBUFS)
                    if v >= VBUFS:
                        act.wait_ge(s_pv, NQUAD * (v - VBUFS + 1))
                    nh = 1 if layer(v)["mqa"] else H
                    act.activation(
                        Vp[v % VBUFS][:, :, 0:nh * VW].rearrange("p k (h w) -> p k h w", w=VW)[:, :, :, 0:HD],
                        miscB[:, 0:2 * P].rearrange("p (k c) -> p k c", k=2)[:, :, 0:nh * HD].rearrange("p k (h w) -> p k h w", w=HD),
                        ACT.Copy).then_inc(s_v, 1)
                elif kind == "scores":
                    m = H * v + k
                    act.wait_ge(s_scores, m + 1)
                    q = m // QUAD
                    if k % QUAD == 0 and q >= 2:
                        act.wait_ge(s_pv, q - 1)
                    act.activation(prob[q % 2][:, m % QUAD, :, :].rearrange("p b c -> p (b c)"),
                                   scoresP[m % SBANKS][:, :, :].rearrange("p b c -> p (b c)"),
                                   ACT.Exp, scale=SCALE).then_inc(s_exp, 1)
                elif kind == "ot":
                    act.wait_ge(s_pv, NQUAD * v + 2 * k + 2)
                    if v >= 1:
                        act.wait_ge(s_fin_mm, 2 * (v - 1) + k + 1)
                    act.activation(oT[k][:, :, :].rearrange("p a b -> p (a b)"),
                                   outP[:, :, :].rearrange("p a b -> p (a b)"), ACT.Copy).then_inc(s_oT, 1)
                elif kind == "read_ont":
                    act.wait_ge(s_ont_mm, v + 1)
                    if v >= 1:
                        act.wait_ge(s_out_mm, v)
                    act.activation(onT[:, :], miscA[:, 0:S], ACT.Copy).then_inc(s_onT, 1)

        @block.vector
        def _(dve):
            def clear(i):
                if first_load:
                    for t in (stackQ[i], stackK[i]):
                        dve.memset(t[0:ROW_M, :, :].rearrange("p h q -> p (h q)").bitcast(F32), 0.0).then_inc(s_zeros, 1)

            def rel_rows():
                dve.wait_ge(s_rel_w, 16)
                dve.wait_ge(s_rel, 1)
                k = 1

                def step(ins):
                    nonlocal k
                    ins.then_inc(s_rel, 1)
                    k += 1
                    dve.wait_ge(s_rel, k)

                step(dve.tensor_scalar(wr[:, :], wr[:, :], 1.0 / SCALE, None, ALU.mult))
                step(dve.tensor_copy(wparts[:, 0, :], wr[:, :]))
                step(dve.tensor_tensor(wr1[:, :], wr[:, :], wparts[:, 0, :], ALU.subtract))
                step(dve.tensor_copy(wparts[:, 1, :], wr1[:, :]))
                step(dve.tensor_tensor(wparts[:, 2, :], wr1[:, :], wparts[:, 1, :], ALU.subtract))
                step(dve.tensor_copy(relrow[:, 0:3, :], wparts[:, :, :].to_broadcast([H, 3, S])))
                step(dve.tensor_scalar(relrow[:, 3, :], pos[:, :], -1.0, None, ALU.mult))
                step(dve.tensor_copy(relrow[:, 4, :], pos[:, :]))

            for kind, v, k in STEPS:
                xt = x_all[:, 2 * (v % B):2 * (v % B) + 2, :]
                if kind == "stat":
                    lo, m = stat_tiles(v)
                    if v >= B:
                        dve.wait_ge(s_x, v - B + 1)
                    elif first_load:
                        dve.wait_ge(s_x_in[v], 16)
                    for c in range(lo, lo + m):
                        dve.bn_stats(bn[:, c, :], x_all[:, c, :]).then_inc(s_bn, 1)
                    dve.wait_ge(s_bn, HALVES if v == 0 else TILES + HALVES * (stats(v) - 2))
                    for c in range(lo, lo + m):
                        ins = dve.bn_aggr(mv[:, c, :], bn[:, c, :])
                    ins.then_inc(s_stat, 1)
                    if v == 1:
                        clear(1)
                    if v == 0:
                        dve.wait_ge(s_stat, stats(v))
                        newton_rsqrt(dve, s_newton, NEWTON_STEPS * (stats(v) - 1), mv[:, lo:lo + m, 1], 1.0, LN_EPS,
                                     rstd[:, lo:lo + m], [t[:, 0:m] for t in nt])
                elif kind == "norm":
                    dve.wait_ge(s_newton, NEWTON_STEPS * stats(v))
                    dve.wait_ge(s_stat, stats(v))
                    if v >= 1:
                        dve.wait_ge(s_xnT_mm, v)
                    for c in range(HALVES):
                        j = HALVES * (v % B) + c
                        ins = dve.tensor_scalar(xn[:, c, :], xt[:, c, :], mv[:, j, 0:1], rstd[:, j:j + 1],
                                                ALU.subtract, ALU.mult)
                    ins.then_inc(s_norm, 1)
                    if v == 0 and rel is not None:
                        rel_rows()
                    if v == 1 and biased:
                        w = W[biased[0]]
                        dve.wait_ge(s_bo_mm, 1)
                        dve.tensor_tensor(w["bo"][:, 0, :], miscA[:, 0:D], w["bo"][:, 0, :], ALU.add).then_inc(s_bo, 1)
                    if v < 2:
                        clear(2 * v)
                elif kind == "max":
                    m = H * v + k
                    dve.wait_ge(s_max_mm, m + 1)
                    if k == 0 and v >= 2:
                        dve.wait_ge(s_negm_mm, v - 1)
                    dve.tensor_reduce(mx[v % 2][:, :, k:k + 1], maxP[m % 2][:, :, :], AX.X, ALU.max).then_inc(s_max, 1)
                elif kind == "read_negm":
                    dve.wait_ge(s_negm_mm, v + 1)
                    if v >= 1:
                        dve.wait_ge(s_mrows, 32 * v)
                    dve.tensor_scalar(mparts[:, 0, :], miscA[0:H, 0:S], -1.0, None, ALU.mult).then_inc(s_mhi, 1)
                    dve.wait_ge(s_mhi, v + 1)
                    dve.scalar_tensor_tensor(out=mparts[:, 1, :], in0=miscA[0:H, 0:S], scalar=-1.0,
                                             in1=mparts[:, 0, :], op0=ALU.mult, op1=ALU.subtract).then_inc(s_mlo, 1)
                elif kind == "read_fin":
                    m = 2 * v + k
                    dve.wait_ge(s_fin_mm, m + 1)
                    if m >= 1:
                        dve.wait_ge(s_on, m)
                    grouped = misc_of(k)[:, :].rearrange("p (q h c) -> p q h c", q=HALVES, c=32)
                    dve.reciprocal(rec[:, :, :, :], grouped[:, :, :, HD:HD + 1]).then_inc(s_rec, 1)
                    dve.wait_ge(s_rec, m + 1)
                    if k == 0 and v >= 1:
                        dve.wait_ge(s_ont_mm, v)
                    dve.tensor_tensor(on[:, :, k * 64:(k + 1) * 64].rearrange("p q (h d) -> p q h d", d=HD),
                                      grouped[:, :, :, 0:HD], rec[:, :, :, :].to_broadcast([P, HALVES, 8, HD]),
                                      ALU.mult).then_inc(s_on, 1)
                elif kind == "read_out":
                    dve.wait_ge(s_out_mm, v + 1)
                    if v // B in biased:
                        dve.wait_ge(s_xbias, v - B * biased[0] + 1)
                    dve.tensor_tensor(xt, miscB[:, 0:S].rearrange("p (q d) -> p q d", d=D), xt, ALU.add).then_inc(s_x, 1)

        @block.tensor
        def _(pe):
            if first_load:
                pe.wait_ge(s_ident, 2)
            for kind, v, k in STEPS:
                if kind == "xnt":
                    pe.wait_ge(s_norm, v + 1)
                    if v >= 3:
                        pe.wait_ge(s_mlo, v - 2)
                    elif v >= 1:
                        pe.wait_ge(s_xnT, v)
                    if v == 1 and biased:
                        w = W[biased[0]]
                        pe.wait_ge(s_bvw, 1)
                        pe.matmul(miscA[:, 0:D], w["bvw"][:, :], w["wo"][:, :], start=True, stop=True).then_inc(s_bo_mm, 1)
                        pe.wait_ge(s_bo, 1)
                    for c in range(HALVES):
                        ins = pe.transpose(miscA[:, c * P:(c + 1) * P], xn[:, c, :], ident[:, :])
                    ins.then_inc(s_xnT_mm, 1)
                elif kind == "qk":
                    pe.wait_ge(s_xnT, v + 1)
                    if v >= 4:
                        pe.wait_ge(s_on, 2 * (v - 4) + 1)
                    elif v >= 1:
                        pe.wait_ge(s_v, v)
                    if v == 0:
                        pe.wait_ge(s_w0, 16 * 4)
                    if v == B:
                        pe.wait_ge(s_w, 16 * n_w)
                    if first_load and layer(v)["ctx"]:
                        pe.wait_ge(s_ctx, 16)
                    w = W[v // B]
                    pe.matmul(miscB[:, 0:S], w["wq"][:, :], xnT[v % 2][:, :], start=True, stop=True)
                    pe.matmul(miscB[:, S:2 * S], w["wk"][:, :], kvT(v), start=True, stop=True).then_inc(s_qk_mm, 1)
                elif kind == "v":
                    pe.wait_ge(s_qk, v + 1)
                    nv = HD if layer(v)["mqa"] else D
                    for c in range(HALVES):
                        ins = pe.matmul(miscB[:, c * P:c * P + nv], kvT(v)[:, c * P:(c + 1) * P],
                                        W[v // B]["wv"][:, :], start=True, stop=True)
                    ins.then_inc(s_v_mm, 1)
                elif kind == "max":
                    m = H * v + k
                    if k == 0:
                        pe.wait_ge(s_load[0], loaded(v, 0))
                        if v == 0 and rel is not None:
                            pe.wait_ge(s_relrows, 16 * 2 * STACKS)
                    if k == H // 2:
                        pe.wait_ge(s_load[1], loaded(v, 1))
                    if m >= 2:
                        pe.wait_ge(s_max, m - 1)
                    for c in range(HALVES):
                        ins = pe.matmul(maxP[m % 2][:, c, :], stackQ[v % STACKS][0:ROWS_MAX, k, c * P:(c + 1) * P],
                                        stackK[v % STACKS][0:ROWS_MAX, head_of(v, k), :], start=True, stop=True)
                    ins.then_inc(s_max_mm, 1)
                elif kind == "negm":
                    pe.wait_ge(s_max, H * (v + 1))
                    if v >= 2:
                        pe.wait_ge(s_onT, v - 1)
                    else:
                        pe.wait_ge(s_xnT, min(v + 3, n))
                    for c in range(HALVES):
                        ins = pe.transpose(miscA[0:H, c * P:(c + 1) * P], mx[v % 2][:, c, :], ident[:, :])
                    ins.then_inc(s_negm_mm, 1)
                elif kind == "scores":
                    m = H * v + k
                    if k == 0:
                        pe.wait_ge(s_mrows, 32 * (v + 1))
                        if v < STACKS and first_load:
                            pe.wait_ge(s_kones, v + 1)
                    if m >= SBANKS:
                        pe.wait_ge(s_exp, m - SBANKS + 1)
                    for c in range(HALVES):
                        ins = pe.matmul(scoresP[m % SBANKS][:, c, :],
                                        stackK[v % STACKS][:, head_of(v, k), c * P:(c + 1) * P],
                                        stackQ[v % STACKS][:, k, :], start=True, stop=True)
                    ins.then_inc(s_scores, 1)
                elif kind == "pv":
                    q = NQUAD * v + k
                    pe.wait_ge(s_exp, QUAD * (q + 1))
                    if k == 0:
                        pe.wait_ge(s_v, v + 1)
                    if k % 2 == 0 and q >= 2:
                        pe.wait_ge(s_oT, q // 2)
                    for c in range(HALVES):
                        for g in range(QUAD):
                            at = VW * head_of(v, QUAD * k + g)
                            ins = pe.matmul(outP[32 * g:32 * g + 32, k % 2, :], Vp[v % VBUFS][:, c, at:at + 32],
                                            prob[k % 2][:, g, c, :], start=(c == 0), stop=(c == HALVES - 1),
                                            skip_group_check=True)
                    ins.then_inc(s_pv, 1)
                elif kind == "fin":
                    pe.wait_ge(s_oT, 2 * v + k + 1)
                    if k == 0:
                        if v >= 1:
                            pe.wait_ge(s_x, v)
                        else:
                            pe.wait_ge(s_v, min(v + 4, n))
                    else:
                        pe.wait_ge(s_xnT, min(v + 5, n))
                        pe.wait_ge(s_mlo, min(v + 2, n))
                    for c in range(HALVES):
                        for j in range(2):
                            at = (2 * c + j) * P
                            ins = pe.transpose(misc_of(k)[:, at:at + P], oT[k][:, j, c * P:(c + 1) * P], ident[:, :])
                    ins.then_inc(s_fin_mm, 1)
                elif kind == "ont":
                    pe.wait_ge(s_on, 2 * v + 2)
                    for c in range(HALVES):
                        ins = pe.transpose(miscA[:, c * P:(c + 1) * P], on[:, c, :], ident[:, :])
                    ins.then_inc(s_ont_mm, 1)
                elif kind == "out":
                    pe.wait_ge(s_onT, v + 1)
                    pe.wait_ge(s_v, min(v + 5, n))
                    for c in range(HALVES):
                        ins = pe.matmul(miscB[:, c * D:(c + 1) * D], onT[:, c * P:(c + 1) * P], W[v // B]["wo"][:, :],
                                        start=True, stop=True)
                    ins.then_inc(s_out_mm, 1)


@contextmanager
def attention_buffers(nc):
    with ExitStack() as ctx:
        def sb(nm, shape, dt):
            return ctx.enter_context(nc.sbuf_tensor(nm, shape, dt))

        yield ([sb(f"stackQ{i}", [ROWS_ALL, H, S], BF16) for i in range(STACKS)],
               [sb(f"stackK{i}", [ROWS_ALL, H, S], BF16) for i in range(STACKS)],
               [sb(f"Vp{i}", [P, HALVES, VCOLS], F32) for i in range(VBUFS)])


CHUNKS = 4
CT = TILES // CHUNKS
CN = CT * P
E = 8


class Norm:

    def __init__(self, sb, ps, sem):
        self.bn = sb("bn", [P, TILES, 6], F32)
        self.mv = sb("mv", [P, TILES, 2], F32)
        self.nt = [sb(f"nt{i}", [P, TILES - CT], F32) for i in range(2)]
        self.rstd = sb("rstd", [P, TILES], F32)
        self.xnT = sb("xnT", [P, TILES * P], F32)
        self.turnP = [ps(f"turnP{i}", [P, CN]) for i in range(2)]
        self.s_bn = sem("s_bn")
        self.s_stat = sem("s_stat")
        self.s_newton = sem("s_newton")
        self.s_norm = sem("s_norm")
        self.s_turn = sem("s_turn")
        self.s_xnT = sem("s_xnT")


def norm_stats(dve, n, x_all):
    for c in range(CHUNKS):
        for i in range(CT * c, CT * c + CT):
            dve.bn_stats(n.bn[:, i, :], x_all[:, i, :]).then_inc(n.s_bn, 1)
        dve.wait_ge(n.s_bn, CT * (c + 1))
        for i in range(CT * c, CT * c + CT):
            ins = dve.bn_aggr(n.mv[:, i, :], n.bn[:, i, :])
        ins.then_inc(n.s_stat, 1)


FIRST = slice(0, CT)
REST = slice(CT, TILES)


def roots(pool, n, k, var, eps, out):
    newton_rsqrt(pool, n.s_newton, NEWTON_STEPS * k, var, 1.0, eps, out, [t[:, 0:var.shape[1]] for t in n.nt])


def norm_roots(pool, n, k, tiles):
    pool.wait_ge(n.s_stat, tiles.stop // CT)
    roots(pool, n, k, n.mv[:, tiles, 1], LN_EPS, n.rstd[:, tiles])


def norm_turn(pe, n, c, src, ident):
    pe.wait_ge(n.s_norm, c + 1)
    if c >= 2:
        pe.wait_ge(n.s_xnT, c - 1)
    for i in range(CT):
        ins = pe.transpose(n.turnP[c % 2][:, i * P:(i + 1) * P], src(i), ident[:, :])
    ins.then_inc(n.s_turn, 1)


def norm_copy(act, n, c):
    act.wait_ge(n.s_turn, c + 1)
    act.activation(n.xnT[:, c * CN:(c + 1) * CN], n.turnP[c % 2][:, :], ACT.Copy).then_inc(n.s_xnT, 1)


def ffn_phase(nc, name, x_all, ident, gated, experts, router, rms_scale, gate_scratch, out=None):
    n_up = 4
    n_down = 2 if gated else 4
    w_cols = experts.shape[2]
    M_COLS = (n_up + n_down) * P
    with ExitStack() as ctx:
        def sb(nm, shape, dt=F32):
            return ctx.enter_context(nc.sbuf_tensor(f"{name}_{nm}", shape, dt))

        def ps(nm, shape):
            return ctx.enter_context(nc.psum_tensor(f"{name}_{nm}", shape, F32))

        sem = ctx.enter_context(phase_semaphores(nc, name))

        n = Norm(sb, ps, sem)
        acc = sb("acc", [P, TILES * P])
        xn = acc[:, :].rearrange("p (t d) -> p t d", d=D)
        xhi = sb("xhi", [P, TILES * P], F32R)
        xlo = sb("xlo", [P, TILES * P], F32R)
        rT = sb("rT", [P, E])
        iota = sb("iota", [P, 1, E])
        lg = sb("lg", [P, TILES, E])
        lg2 = sb("lg2", [P, TILES, E])
        t8 = sb("t8", [P, TILES, E])
        first = sb("first", [P, TILES, E])
        second = sb("second", [P, TILES, E])
        gates = sb("gates", [P, TILES, E])
        best = sb("best", [P, TILES, 1])
        at = sb("at", [P, TILES, 1])
        best2 = sb("best2", [P, TILES, 1])
        g1 = sb("g1", [P, TILES, 1])
        g2 = sb("g2", [P, TILES, 1])
        gT = sb("gT", [P, P])
        gb = [sb(f"gb{i}", [P, TILES, P]) for i in range(2)]
        wts = [sb(f"wts{i}", [P, w_cols]) for i in range(2)]
        whi = [sb(f"whi{i}", [P, M_COLS], F32R) for i in range(2)]
        wlo = [sb(f"wlo{i}", [P, M_COLS], F32R) for i in range(2)]
        one = sb("one", [P, 1])
        bias = [sb(f"bias{i}", [P, n_up + 1]) for i in range(2)]
        h32 = [sb(f"h32{i}", [P, CN]) for i in range(2)]
        hhi = [sb(f"hhi{i}", [P, n_down, CN], F32R) for i in range(2)]
        hlo = [sb(f"hlo{i}", [P, n_down, CN], F32R) for i in range(2)]
        sg = [sb(f"sg{i}", [P, CN]) for i in range(2)] if gated else None
        y = [sb(f"y{i}", [P, CN]) for i in range(2)]
        if gated:
            xs = sb("xs", [P, TILES, D])
            sq = [sb(f"sq{i}", [P, D]) for i in range(2)]
            ms = sb("ms", [P, TILES])
            rms = sb("rms", [P, TILES])
            nx = sb("nx", [P, TILES, 1])
            scale_b = sb("scale_b", [P, D])
            rT2 = sb("rT2", [P, E])
            ones = sb("ones", [P, P])

        hP = [ps(f"hP{i}", [P, CN]) for i in range(n_up)]
        yP = [ps(f"yP{i}", [P, CN]) for i in range(2)]
        routeP = yP[0]
        nyP = yP[1]

        s_in = sem("s_in")
        s_setup = sem("s_setup")
        s_sq = sem("s_sq")
        s_ms = sem("s_ms")
        s_xh = sem("s_xh")
        s_skip = sem("s_skip")
        s_rT2 = sem("s_rT2")
        s_logit = sem("s_logit")
        s_route = sem("s_route")
        s_ed = sem("s_ed")
        s_spill = sem("s_spill")
        s_gb = [sem("s_gb0"), sem("s_gb1")]
        s_wts = [sem("s_wts0"), sem("s_wts1")]
        s_whi0 = sem("s_whi0")
        s_whi = sem("s_whi")
        s_split = [sem("s_split0"), sem("s_split1")]
        s_xlo = sem("s_xlo")
        s_gates = sem("s_gates")
        s_gT_mm = sem("s_gT_mm")
        s_gT = sem("s_gT")
        s_clear = sem("s_clear")
        s_up = sem("s_up")
        s_sg = sem("s_sg")
        s_h = sem("s_h")
        s_hi = sem("s_hi")
        s_lo = sem("s_lo")
        s_down = sem("s_down")
        s_y = sem("s_y")
        s_acc = sem("s_acc")
        s_back = sem("s_back")
        s_x = sem("s_x")
        s_out = sem("s_out")

        U = 2 * CHUNKS
        PAIRS = E // 2

        def past(i, u, k=0, per_unit=1):
            return i * (U * per_unit) + (u + 2) * per_unit + k + 1

        def rms_roots(pool, g, k, tiles):
            pool.tensor_tensor(ms[:, tiles], n.mv[:, tiles, 1], n.rstd[:, tiles], ALU.mult).then_inc(s_ms, 1)
            pool.wait_ge(s_ms, 2 * g + 1)
            pool.tensor_tensor(ms[:, tiles], ms[:, tiles], n.rstd[:, tiles], ALU.mult).then_inc(s_ms, 1)
            pool.wait_ge(s_ms, 2 * g + 2)
            roots(pool, n, k, ms[:, tiles], RMS_EPS, rms[:, tiles])

        block = ctx.enter_context(nc.Block())

        @block.sync
        def _(sp):
            sp.dma_start(rT[:, :], router).then_inc(s_in, 16)
            if gated:
                sp.dma_start(scale_b[:, :], rms_scale.partition_broadcast(P)).then_inc(s_in, 16)
            for e in range(2):
                sp.dma_start(wts[e][:, :], experts[e]).then_inc(s_wts[e], 16)
            sp.wait_ge(s_gT, 1)
            sp.dma_start(gate_scratch, gT[:, :]).then_inc(s_spill, 16)
            sp.wait_ge(s_spill, 16)
            by_expert = gate_scratch.rearrange("(t e) p -> e t p", e=E)
            for e in range(2):
                sp.dma_start(gb[e][:, :, :], by_expert[e].partition_broadcast(P)).then_inc(s_gb[e], 16)
            with sp.Fori(0, PAIRS - 1) as i:
                for e in range(2):
                    sp.wait_ge(s_split[e], i + 1)
                    sp.dma_start(wts[e][:, :], experts[bass.ds(i * 2 + 2 + e, 1), :, :].rearrange("o p n -> p (o n)"))\
                        .then_inc(s_wts[e], 16)
                for e in range(2):
                    sp.wait_ge(s_y, past(i, CHUNKS * e + CHUNKS - 1))
                    sp.dma_start(gb[e][:, :, :], by_expert[bass.ds(i * 2 + 2 + e, 1), :, :]
                                 .rearrange("o t p -> (o t) p").partition_broadcast(P)).then_inc(s_gb[e], 16)
            if out is not None:
                for c in range(CHUNKS):
                    sp.wait_ge(s_x, c + 1)
                    tiles = slice(CT * c, CT * (c + 1))
                    sp.dma_start(out.rearrange("(t p) d -> p t d", p=P)[:, tiles, :], x_all[:, tiles, :]).then_inc(s_out, 16)
                sp.wait_ge(s_out, 16 * CHUNKS)

        @block.gpsimd
        def _(pool):
            pool.sem_inc(s_acc, 2)
            pool.memset(one[:, :], 1.0)
            pool.iota(iota[:, 0, :], [[1, E]], base=0, channel_multiplier=0,
                      allow_small_or_imprecise_dtypes=True).then_inc(s_setup, 1)
            if gated:
                pool.memset(ones[:, :], 1.0).then_inc(s_setup, 1)
            norm_roots(pool, n, 0, FIRST)
            if gated:
                rms_roots(pool, 0, 1, FIRST)
            norm_roots(pool, n, 2 if gated else 1, REST)
            if gated:
                rms_roots(pool, 1, 3, REST)

            def columns(part):
                return slice(0, n_up * P) if part == 0 else slice(n_up * P, M_COLS)

            def split(e, part, k):
                cols = columns(part)
                one_b = one[:, :].to_broadcast([P, cols.stop - cols.start])
                pool.tensor_tensor(whi[e][:, cols], wts[e][:, cols], one_b, ALU.mult).then_inc(s_whi, 1)
                pool.wait_ge(s_whi, k)
                finish(e, part)

            def finish(e, part):
                cols = columns(part)
                ins = pool.tensor_tensor(wlo[e][:, cols], wts[e][:, cols], whi[e][:, cols].bitcast(F32), ALU.subtract)
                if part == 1 and not gated:
                    ins = pool.tensor_copy(bias[e][:, :], wts[e][:, M_COLS:w_cols])
                if part == 1:
                    ins.then_inc(s_split[e], 1)

            pool.wait_ge(s_wts[1], 16)
            pool.wait_ge(s_whi0, 2)
            for part in range(2):
                finish(1, part)
            if gated:
                for c in range(CHUNKS):
                    xt = x_all[:, CT * c:CT * c + CT, :]
                    pool.wait_ge(s_xh, c + 1)
                    pool.tensor_tensor(xt, xt, xn[:, CT * c:CT * c + CT, :], ALU.add).then_inc(s_skip, 1)
                pool.wait_ge(s_skip, CHUNKS)
                pool.wait_ge(n.s_norm, CHUNKS)
            pool.wait_ge(n.s_turn, CHUNKS)
            pool.memset(acc[:, :], 0.0).then_inc(s_clear, 1)
            pool.wait_ge(s_clear, 1)

            def add_up(i, u):
                cols = slice((u % CHUNKS) * CN, (u % CHUNKS + 1) * CN)
                pool.wait_ge(s_y, past(i, u))
                pool.wait_ge(s_acc, past(i, u - 2))
                pool.tensor_tensor(acc[:, cols], acc[:, cols], y[u % 2][:, :], ALU.add).then_inc(s_acc, 1)

            add_up(0, 0)
            add_up(0, 1)
            with pool.Fori(0, PAIRS - 1) as i:
                for u in range(2, U + 2):
                    add_up(i, u)
                    e, part = divmod(u - (CHUNKS - 1), CHUNKS)
                    if u >= CHUNKS - 1 and part < 2:
                        if part == 0:
                            pool.wait_ge(s_wts[e], i * 16 + 32)
                            pool.wait_ge(s_down, past(i, CHUNKS * e + CHUNKS - 1))
                            pool.wait_ge(s_y, past(i, CHUNKS * e + CHUNKS - 1))
                        split(e, part, i * 4 + 1 + 2 * e + part)
            for u in range(2, U):
                add_up(PAIRS - 1, u)

        @block.scalar
        def _(act):
            act.sem_inc(s_hi, 2 * n_down)
            if gated:
                act.sem_inc(s_sg, 2 * n_down)

            if gated:
                act.wait_ge(s_in, 32)
                act.activation(rT2[:, :], rT[:, :], ACT.Square).then_inc(s_rT2, 1)
            for e in range(2):
                act.wait_ge(s_wts[e], 16)
                act.activation(whi[e][:, :], wts[e][:, 0:M_COLS], ACT.Copy).then_inc(s_whi0, 1)

            def turned(c):
                cols = slice(c * CN, (c + 1) * CN)
                act.wait_ge(n.s_turn, c + 1)
                act.activation(n.xnT[:, cols], n.turnP[c % 2][:, :], ACT.Copy)
                act.activation(xhi[:, cols], n.turnP[c % 2][:, :], ACT.Copy).then_inc(n.s_xnT, 1)

            def squares(cs):
                for c in cs:
                    act.wait_ge(n.s_norm, c + 1)
                    for i in range(CT * c, CT * (c + 1)):
                        if i >= 2:
                            act.wait_ge(s_sq, i - 1)
                        act.activation(sq[i % 2][:, :], xs[:, i, :], ACT.Square, accum_out=nx[:, i, :]).then_inc(s_sq, 1)

            turned(0)
            if gated:
                squares([0])
            for c in range(1, CHUNKS):
                turned(c)

            def unit(i, u):
                if gated:
                    for k in range(n_down):
                        act.wait_ge(s_up, i * (U * n_up) + u * n_up + 2 * k + 1)
                        act.wait_ge(s_h, past(i, u - 1, k, n_down))
                        act.activation(sg[k][:, :], hP[2 * k][:, :], ACT.Silu).then_inc(s_sg, 1)
                for k in range(n_down):
                    if gated:
                        act.wait_ge(s_h, past(i, u, k, n_down))
                    else:
                        e = u // CHUNKS
                        act.wait_ge(s_up, i * (U * n_up) + u * n_up + k + 1)
                        act.wait_ge(s_lo, past(i, u, k - 2, n_down))
                        act.activation(h32[k % 2][:, :], hP[k][:, :], ACT.Gelu, bias=bias[e][:, k:k + 1])
                    if k == 0:
                        act.wait_ge(s_down, past(i, u - 2))
                    if gated:
                        act.activation(hhi[u % 2][:, k, :], h32[k % 2][:, :], ACT.Copy).then_inc(s_hi, 1)
                    else:
                        act.activation(hhi[u % 2][:, k, :], hP[k][:, :], ACT.Gelu, bias=bias[e][:, k:k + 1])\
                            .then_inc(s_hi, 1)

            unit(0, 0)
            if gated:
                squares(range(1, CHUNKS))
            else:
                act.wait_ge(s_route, ROUTE_TWO)
                act.activation(g2[:, :, :], best2[:, :, :], ACT.Exp).then_inc(s_ed, 1)
            for u in range(1, U):
                unit(0, u)
            with act.Fori(1, PAIRS) as i:
                for u in range(U):
                    unit(i, u)

        @block.vector
        def _(dve):
            dve.sem_inc(s_lo, 2 * n_down)
            dve.sem_inc(s_y, 2)
            if gated:
                dve.sem_inc(s_h, 2 * n_down)
            norm_stats(dve, n, x_all)

            def norm(cs, k):
                for c in cs:
                    dve.wait_ge(n.s_newton, NEWTON_STEPS * (k + 1))
                    dve.wait_ge(n.s_stat, c + 1)
                    for i in range(CT * c, CT * c + CT):
                        ins = dve.tensor_scalar(xn[:, i, :], x_all[:, i, :], n.mv[:, i, 0:1], n.rstd[:, i:i + 1],
                                                ALU.subtract, ALU.mult)
                    ins.then_inc(s_xh if gated else n.s_norm, 1)

            def rms_norm(cs, k):
                for c in cs:
                    dve.wait_ge(s_in, 32)
                    dve.wait_ge(n.s_newton, NEWTON_STEPS * (k + 1))
                    dve.wait_ge(s_xh, c + 1)
                    for i in range(CT * c, CT * c + CT):
                        ins = dve.scalar_tensor_tensor(out=xs[:, i, :], in0=xn[:, i, :], scalar=rms[:, i:i + 1],
                                                       in1=scale_b[:, :], op0=ALU.mult, op1=ALU.mult)
                    ins.then_inc(n.s_norm, 1)

            def cut_tokens(cs):
                for c in cs:
                    cols = slice(c * CN, (c + 1) * CN)
                    dve.wait_ge(n.s_xnT, c + 1)
                    dve.tensor_tensor(xlo[:, cols], n.xnT[:, cols], xhi[:, cols].bitcast(F32), ALU.subtract)\
                        .then_inc(s_xlo, 1)

            norm([0], 0)
            dve.wait_ge(s_wts[0], 16)
            dve.wait_ge(s_whi0, 1)
            ins = dve.tensor_tensor(wlo[0][:, :], wts[0][:, 0:M_COLS], whi[0][:, :].bitcast(F32), ALU.subtract)
            if gated:
                ins.then_inc(s_split[0], 1)
                rms_norm([0], 1)
            else:
                dve.tensor_copy(bias[0][:, :], wts[0][:, M_COLS:w_cols]).then_inc(s_split[0], 1)
            cut_tokens([0])
            rest = range(1, CHUNKS)
            norm(rest, 2 if gated else 1)
            if gated:
                rms_norm(rest, 3)
            cut_tokens(rest)

            def route():
                k = 0

                def step(ins):
                    nonlocal k
                    ins.then_inc(s_route, 1)
                    k += 1
                    dve.wait_ge(s_route, k)

                full = [P, TILES, E]
                io = iota[:, :, :].to_broadcast(full)

                def first_of(values, extreme, reduce, onehot):
                    step(dve.tensor_reduce(extreme[:, :, :], values[:, :, :], AX.X, reduce))
                    step(dve.tensor_tensor(t8[:, :, :], values[:, :, :], extreme[:, :, :].to_broadcast(full), ALU.is_equal))
                    step(dve.scalar_tensor_tensor(out=t8[:, :, :], in0=t8[:, :, :], scalar=-float(E), in1=io,
                                                  op0=ALU.mult, op1=ALU.add))
                    step(dve.tensor_reduce(at[:, :, :], t8[:, :, :], AX.X, ALU.min))
                    step(dve.tensor_scalar(at[:, :, :], at[:, :, :], float(E), None, ALU.add))
                    ins = dve.tensor_tensor(onehot[:, :, :], io, at[:, :, :].to_broadcast(full), ALU.is_equal)
                    if onehot is gates:
                        ins.then_inc(s_gates, 1)
                    else:
                        step(ins)

                dve.wait_ge(s_setup, 1)
                dve.wait_ge(s_logit, 1)
                if gated:
                    dve.wait_ge(s_sq, TILES)
                    step(dve.tensor_copy(lg2[:, 0, :], nyP[:, 0:E]))
                    step(dve.tensor_tensor(t8[:, :, :], lg2[:, 0:1, :].to_broadcast(full), nx[:, :, :].to_broadcast(full), ALU.add))
                    step(dve.scalar_tensor_tensor(out=lg[:, :, :], in0=routeP[:, 0:P].rearrange("p (t e) -> p t e", e=E), scalar=-2.0,
                                                  in1=t8[:, :, :], op0=ALU.mult, op1=ALU.add))
                    first_of(lg, best, ALU.min, gates)
                else:
                    step(dve.tensor_copy(lg[:, :, :], routeP[:, 0:P].rearrange("p (t e) -> p t e", e=E)))
                    first_of(lg, best, ALU.max, first)
                    step(dve.scalar_tensor_tensor(out=lg2[:, :, :], in0=first[:, :, :], scalar=-3e38, in1=lg[:, :, :],
                                                  op0=ALU.mult, op1=ALU.add))
                    first_of(lg2, best2, ALU.max, second)
                    step(dve.tensor_tensor(best2[:, :, :], best2[:, :, :], best[:, :, :], ALU.subtract))
                    assert k == ROUTE_TWO
                    dve.wait_ge(s_ed, 1)
                    step(dve.tensor_scalar(g1[:, :, :], g2[:, :, :], 1.0, None, ALU.add))
                    step(dve.reciprocal(g1[:, :, :], g1[:, :, :]))
                    step(dve.tensor_tensor(g2[:, :, :], g2[:, :, :], g1[:, :, :], ALU.mult))
                    step(dve.tensor_tensor(first[:, :, :], first[:, :, :], g1[:, :, :].to_broadcast(full), ALU.mult))
                    step(dve.tensor_tensor(second[:, :, :], second[:, :, :], g2[:, :, :].to_broadcast(full), ALU.mult))
                    dve.tensor_tensor(gates[:, :, :], first[:, :, :], second[:, :, :], ALU.add).then_inc(s_gates, 1)

            def cut(i, u):
                if gated:
                    for k in range(n_down):
                        dve.wait_ge(s_sg, past(i, u, k, n_down))
                        dve.wait_ge(s_up, i * (U * n_up) + u * n_up + 2 * k + 2)
                        dve.wait_ge(s_lo, past(i, u - 1, k, n_down))
                        dve.tensor_tensor(h32[k][:, :], hP[2 * k + 1][:, :], sg[k][:, :], ALU.mult).then_inc(s_h, 1)
                for k in range(n_down):
                    dve.wait_ge(s_hi, past(i, u, k, n_down))
                    dve.tensor_tensor(hlo[u % 2][:, k, :], h32[k % 2][:, :], hhi[u % 2][:, k, :].bitcast(F32),
                                      ALU.subtract).then_inc(s_lo, 1)

            def combine(i, u):
                e, c = divmod(u % U, CHUNKS)
                if u >= 0 and c == 0:
                    dve.wait_ge(s_gb[e], i * 16 + 16)
                gate = gb[e][:, CT * c:CT * c + CT, :].rearrange("p t q -> p (t q)")
                dve.wait_ge(s_down, past(i, u))
                dve.wait_ge(s_acc, past(i, u - 2))
                if gated:
                    dve.tensor_tensor(y[u % 2][:, :], yP[u % 2][:, :], gate, ALU.mult).then_inc(s_y, 1)
                else:
                    dve.scalar_tensor_tensor(out=y[u % 2][:, :], in0=yP[u % 2][:, :], scalar=bias[e][:, n_up:n_up + 1],
                                             in1=gate, op0=ALU.add, op1=ALU.mult).then_inc(s_y, 1)

            cut(0, 0)
            route()
            dve.wait_ge(s_gT_mm, 1)
            dve.tensor_copy(gT[:, :], n.turnP[0][:, 0:P]).then_inc(s_gT, 1)
            for u in range(1, U):
                cut(0, u)
                combine(0, u - 1)
            with dve.Fori(1, PAIRS) as i:
                for u in range(U):
                    cut(i, u)
                    combine(i, u - 1)
            combine(PAIRS - 1, U - 1)
            for c in range(CHUNKS):
                dve.wait_ge(s_back, c + 1)
                if gated:
                    dve.wait_ge(s_skip, c + 1)
                xt = x_all[:, CT * c:CT * c + CT, :]
                dve.tensor_tensor(xt, n.turnP[c % 2][:, :].rearrange("p (t d) -> p t d", d=D), xt, ALU.add).then_inc(s_x, 1)

        @block.tensor
        def _(pe):
            pe.sem_inc(s_down, 2)

            def product(dst, e, blk, hi, lo, start, stop):
                cols = slice(blk * P, (blk + 1) * P)
                pe.matmul(dst, whi[e][:, cols], hi, start=start, stop=False)
                pe.matmul(dst, whi[e][:, cols], lo, start=False, stop=False)
                return pe.matmul(dst, wlo[e][:, cols], hi, start=False, stop=stop)

            def up(i, u):
                e, c = divmod(u % U, CHUNKS)
                cols = slice(c * CN, (c + 1) * CN)
                if c == 0:
                    pe.wait_ge(s_split[e], i + u // U + 1)
                for k in range(n_up):
                    if gated:
                        blk = (2 if k % 2 == 0 else 0) + k // 2
                        pe.wait_ge(s_sg if k % 2 == 0 else s_h, past(i, u - 1, k // 2, n_down))
                    else:
                        blk = k
                        pe.wait_ge(s_hi, past(i, u - 1, k, n_down))
                    product(hP[k][:, :], e, blk, xhi[:, cols], xlo[:, cols], True, True).then_inc(s_up, 1)

            def down(i, u):
                pe.wait_ge(s_y, past(i, u - 2))
                for k in range(n_down):
                    pe.wait_ge(s_lo, past(i, u, k, n_down))
                    ins = product(yP[u % 2][:, :], u // CHUNKS, n_up + k, hhi[u % 2][:, k, :], hlo[u % 2][:, k, :],
                                  k == 0, k == n_down - 1)
                ins.then_inc(s_down, 1)

            src = (lambda c, i: xs[:, CT * c + i, :]) if gated else (lambda c, i: xn[:, CT * c + i, :])
            norm_turn(pe, n, 0, lambda i: src(0, i), ident)
            pe.wait_ge(n.s_xnT, 1)
            pe.wait_ge(s_xlo, 1)
            up(0, 0)
            for c in range(1, CHUNKS):
                norm_turn(pe, n, c, lambda i: src(c, i), ident)
            pe.wait_ge(n.s_xnT, CHUNKS)
            pe.wait_ge(s_in, 32 if gated else 16)
            if gated:
                pe.wait_ge(s_rT2, 1)
                pe.wait_ge(s_setup, 2)
                pe.matmul(nyP[:, 0:E], ones[:, :], rT2[:, :], start=True, stop=True)
            for i in range(TILES):
                ins = pe.matmul(routeP[:, i * E:(i + 1) * E], n.xnT[:, i * P:(i + 1) * P], rT[:, :], start=True, stop=True)
            ins.then_inc(s_logit, 1)
            pe.wait_ge(s_xlo, CHUNKS)
            up(0, 1)
            pe.wait_ge(s_route, 3 if gated else 1)
            if not gated:
                down(0, 0)
            pe.wait_ge(s_gates, 1)
            pe.transpose(n.turnP[0][:, 0:P], gates[:, :, :].rearrange("p t e -> p (t e)"), ident[:, :]).then_inc(s_gT_mm, 1)
            if gated:
                down(0, 0)

            for u in range(1, U):
                up(0, u + 1)
                down(0, u)
            with pe.Fori(1, PAIRS - 1) as i:
                for u in range(U):
                    up(i, u + 1)
                    down(i, u)

            def back(c):
                pe.wait_ge(s_acc, past(PAIRS - 1, U - CHUNKS + c))
                if c >= 2:
                    pe.wait_ge(s_x, c - 1)
                for i in range(CT):
                    j = CT * c + i
                    ins = pe.transpose(n.turnP[c % 2][:, i * P:(i + 1) * P], acc[:, j * P:(j + 1) * P], ident[:, :])
                ins.then_inc(s_back, 1)

            for u in range(U):
                if u < U - 1:
                    up(PAIRS - 1, u + 1)
                down(PAIRS - 1, u)
                if U - CHUNKS < u < U - 1:
                    back(u - 1 - (U - CHUNKS))
            back(CHUNKS - 2)
            back(CHUNKS - 1)


ROUTE_TWO = 15

T = B
TAPS = 15


def across_phase(nc, name, x_all, ident, w_in, b_in, w_dyn, b_dyn, w_out, b_out):
    with ExitStack() as ctx:
        def sb(nm, shape, dt=F32):
            return ctx.enter_context(nc.sbuf_tensor(f"{name}_{nm}", shape, dt))

        def ps(nm, shape):
            return ctx.enter_context(nc.psum_tensor(f"{name}_{nm}", shape, F32))

        sem = ctx.enter_context(phase_semaphores(nc, name))

        n = Norm(sb, ps, sem)
        xn = [sb(f"xn{i}", [P, CT, D]) for i in range(2)]
        win = sb("win", [P, 3 * D])
        bin_b = sb("bin_b", [P, 3 * D])
        wdyn = sb("wdyn", [P, H * TAPS])
        bdyn_b = sb("bdyn_b", [P, H * TAPS])
        wout = sb("wout", [P, 2, D])
        bout_b = sb("bout_b", [P, 1, D])
        qkv = [sb(f"qkv{i}", [P, T, 3 * D]) for i in range(2)]
        vT = sb("vT", [P, TILES * P])
        bv = sb("bv", [P, 1])
        taps = [sb(f"taps{i}", [P, T * H, TAPS]) for i in range(2)]
        tstat = sb("tstat", [P, T * H, 1])
        trec = [sb(f"trec{i}", [P, T, H, 1]) for i in range(2)]
        score = [sb(f"score{i}", [P, T, T, H]) for i in range(2)]
        astat = [sb(f"astat{i}", [P, T, 1, H]) for i in range(2)]
        arec = [sb(f"arec{i}", [P, T, H, 1]) for i in range(2)]
        product = [sb(f"product{i}", [P, T, D]) for i in range(2)]
        wproduct = [sb(f"wproduct{i}", [P, T, D]) for i in range(2)]
        pproduct = [sb(f"pproduct{i}", [P, T, D]) for i in range(2)]
        cproduct = [sb(f"cproduct{i}", [P, T, D]) for i in range(2)]
        cat = [sb(f"cat{i}", [P, T, 2, D]) for i in range(2)]
        catT = [sb(f"catT{i}", [P, 2, P]) for i in range(2)]

        inP = [ps(f"inP{i}", [P, 3 * D]) for i in range(2)]
        by_t = [t[:, :].rearrange("p (t d) -> p t d", d=D) for t in n.turnP]
        attP = [ps("attP", [P, T // 2, D])[:, :, :], by_t[0]]
        convP = [ps("convP", [P, T // 2, D])[:, :, :], by_t[1]]
        catP = [ps("catP", [P, 2, P])[:, :, :], inP[0][:, 0:2 * P].rearrange("p (c d) -> p c d", d=P)]
        outP = [ps("outP", [P, D])[:, :], inP[1][:, 0:D]]

        s_w = sem("s_w")
        s_xb = sem("s_xb")
        s_in_mm = sem("s_in_mm")
        s_qkv = sem("s_qkv")
        s_vT_mm = sem("s_vT_mm")
        s_vT = sem("s_vT")
        s_dyn_mm = sem("s_dyn_mm")
        s_dyn = sem("s_dyn")
        s_tmax = sem("s_tmax")
        s_tsub = sem("s_tsub")
        s_trec = sem("s_trec")
        s_texp = sem("s_texp")
        s_tsum = sem("s_tsum")
        s_taps = sem("s_taps")
        s_prod = sem("s_prod")
        s_pprod = sem("s_pprod")
        s_score = sem("s_score")
        s_amax = sem("s_amax")
        s_aexp = sem("s_aexp")
        s_asum = sem("s_asum")
        s_arec = sem("s_arec")
        s_weigh = sem("s_weigh")
        s_att = sem("s_att")
        s_attn = sem("s_attn")
        s_cprod = sem("s_cprod")
        s_conv = sem("s_conv")
        s_convn = sem("s_convn")
        s_cat_mm = sem("s_cat_mm")
        s_cat = sem("s_cat")
        s_out_mm = sem("s_out_mm")
        s_x = sem("s_x")

        HT = T // 2
        GROUPS = 2 * HALVES

        def pooled(m):
            return (m - T) // 2 if m >= T and m % 2 else None

        def group(g):
            half, j = divmod(g, 2)
            return half, range(HT * j, HT * (j + 1))

        def outD(m):
            return n.turnP[m % 2][:, 0:H * TAPS]

        def vTP(c):
            return (attP, convP)[c % 2][0].rearrange("p t d -> p (t d)")

        block = ctx.enter_context(nc.Block())

        @block.sync
        def _(sp):
            sp.dma_start(win[:, :], w_in).then_inc(s_w, 16)
            sp.dma_start(bv[:, :], b_in[2 * D:].rearrange("(p o) -> p o", o=1)).then_inc(s_w, 16)
            sp.dma_start(wdyn[:, :], w_dyn).then_inc(s_w, 16)
            sp.dma_start(bin_b[:, :], b_in.partition_broadcast(P)).then_inc(s_w, 16)
            sp.dma_start(bdyn_b[:, :], b_dyn.partition_broadcast(P)).then_inc(s_w, 16)
            sp.dma_start(wout[:, :, :], w_out.rearrange("(c k) n -> k c n", k=P)).then_inc(s_w, 16)
            sp.dma_start(bout_b[:, 0, :], b_out.partition_broadcast(P)).then_inc(s_w, 16)

        @block.gpsimd
        def _(pool):
            norm_roots(pool, n, 0, FIRST)
            norm_roots(pool, n, 1, REST)
            pool.wait_ge(s_w, 112)
            pool.wait_ge(n.s_norm, CHUNKS)
            pool.tensor_tensor(x_all[:, :, :], x_all[:, :, :], bout_b[:, :, :].to_broadcast([P, TILES, D]), ALU.add)\
                .then_inc(s_xb, 1)

            def tap_less_max(half):
                pool.wait_ge(s_tmax, half + 1)
                pool.wait_ge(s_dyn, T * (half + 1))
                pool.tensor_tensor(taps[half][:, :, :], taps[half][:, :, :],
                                   tstat[:, :, :].to_broadcast([P, T * H, TAPS]), ALU.subtract).then_inc(s_tsub, 1)

            def tap_norm(half):
                pool.wait_ge(s_trec, half + 1)
                pool.wait_ge(s_texp, half + 1)
                rec = trec[half][:, :, :, :].rearrange("p t h o -> p (t h) o").to_broadcast([P, T * H, TAPS])
                pool.tensor_tensor(taps[half][:, :, :], taps[half][:, :, :], rec, ALU.mult).then_inc(s_taps, 1)

            def convolve(g):
                half, ts = group(g)
                pool.wait_ge(s_taps, half + 1)
                pool.wait_ge(s_qkv, T * (half + 1))
                tap = taps[half][:, :, :].rearrange("p (t h) k -> p t h k", h=H)
                for t in ts:
                    m = half * T + t
                    if m >= 2:
                        pool.wait_ge(s_conv, m - 1)
                    w = tap[:, t, :, T - 1 - t:2 * T - 1 - t].rearrange("p h (s o) -> p s h o", o=1)
                    pool.tensor_tensor(cproduct[m % 2][:, :, :].rearrange("p s (h d) -> p s h d", d=HD),
                                       qkv[half][:, :, 2 * D:].rearrange("p s (h d) -> p s h d", d=HD),
                                       w.to_broadcast([P, T, H, HD]), ALU.mult).then_inc(s_cprod, 1)

            tap_less_max(0)
            tap_norm(0)
            tap_less_max(1)
            def score_products(g):
                for m in range(HT * g, HT * (g + 1)):
                    if pooled(m) is not None:
                        half, t = divmod(m, T)
                        pool.wait_ge(s_qkv, T * (half + 1))
                        if pooled(m) >= 2:
                            pool.wait_ge(s_score, m - HT + 1)
                        q = qkv[half][:, t:t + 1, 0:D].to_broadcast([P, T, D])
                        pool.tensor_tensor(pproduct[pooled(m) % 2][:, :, :], q, qkv[half][:, :, D:2 * D], ALU.mult)\
                            .then_inc(s_pprod, 1)

            convolve(0)
            tap_norm(1)
            for g in range(1, GROUPS):
                score_products(g)
                convolve(g)

        @block.scalar
        def _(act):
            def v_copy(c):
                act.wait_ge(s_vT_mm, c + 1)
                act.activation(vT[:, c * CN:(c + 1) * CN], vTP(c), ACT.Identity, bias=bv[:, 0:1]).then_inc(s_vT, 1)

            norm_copy(act, n, 0)
            act.wait_ge(s_w, 112)
            v_copy(0)
            for c in range(1, CHUNKS):
                norm_copy(act, n, c)
            for c in range(1, CHUNKS):
                v_copy(c)

            def tap_exp(half):
                act.wait_ge(s_tsub, half + 1)
                tap = taps[half][:, :, :].rearrange("p a b -> p (a b)")
                act.activation(tap, tap, ACT.Exp).then_inc(s_texp, 1)

            def convolved(g):
                half, j = divmod(g, 2)
                act.wait_ge(s_conv, HT * (g + 1))
                act.activation(cat[half][:, HT * j:HT * (j + 1), 1, :], convP[g % 2], ACT.Copy).then_inc(s_convn, 1)

            def score_exp(g):
                half, ts = group(g)
                act.wait_ge(s_amax, 2 * g + 2)
                flat = score[half][:, ts.start:ts.stop, :, :].rearrange("p a b c -> p (a b c)")
                act.activation(flat, flat, ACT.Exp, scale=SCALE).then_inc(s_aexp, 1)

            def turned(ms):
                for m in ms:
                    act.wait_ge(s_cat_mm, m + 1)
                    if m >= 2:
                        act.wait_ge(s_out_mm, m - 1)
                    act.activation(catT[m % 2][:, :, :], catP[m % 2], ACT.Copy).then_inc(s_cat, 1)

            tap_exp(0)
            tap_exp(1)
            for g in range(GROUPS + 2):
                if g >= 2:
                    turned(range(HT * (g - 2), HT * (g - 1)))
                if g < GROUPS:
                    score_exp(g)
                    convolved(g)

        @block.vector
        def _(dve):
            norm_stats(dve, n, x_all)
            for c in range(CHUNKS):
                dve.wait_ge(n.s_newton, NEWTON_STEPS * min(c + 1, 2))
                dve.wait_ge(n.s_stat, c + 1)
                if c >= 2:
                    dve.wait_ge(n.s_turn, c - 1)
                for i in range(CT):
                    j = CT * c + i
                    ins = dve.tensor_scalar(xn[c % 2][:, i, :], x_all[:, j, :], n.mv[:, j, 0:1], n.rstd[:, j:j + 1],
                                            ALU.subtract, ALU.mult)
                ins.then_inc(n.s_norm, 1)
            dve.wait_ge(s_w, 112)

            def projected(m):
                half, t = divmod(m, T)
                dve.wait_ge(s_in_mm, m + 1)
                dve.tensor_tensor(qkv[half][:, t, :], inP[m % 2][:, :], bin_b[:, :], ALU.add).then_inc(s_qkv, 1)

            def tap_logits(m):
                half, t = divmod(m, T)
                dve.wait_ge(s_dyn_mm, m + 1)
                flat = taps[half][:, :, :].rearrange("p (t h) k -> p t (h k)", h=H)
                dve.tensor_tensor(flat[:, t, :], outD(m), bdyn_b[:, :], ALU.add).then_inc(s_dyn, 1)

            def tap_max(half):
                dve.wait_ge(s_dyn, T * (half + 1))
                if half:
                    dve.wait_ge(s_tsub, 1)
                dve.tensor_reduce(tstat[:, :, :], taps[half][:, :, :], AX.X, ALU.max).then_inc(s_tmax, 1)

            def tap_sum(half):
                dve.wait_ge(s_texp, half + 1)
                flat = trec[half][:, :, :, :].rearrange("p t h o -> p (t h) o")
                dve.tensor_reduce(flat, taps[half][:, :, :], AX.X, ALU.add).then_inc(s_tsum, 1)
                dve.wait_ge(s_tsum, half + 1)
                dve.reciprocal(flat, flat).then_inc(s_trec, 1)

            def scores(m):
                half, t = divmod(m, T)
                if m == 0:
                    dve.wait_ge(s_qkv, T)
                if m >= 2:
                    dve.wait_ge(s_score, m - 1)
                if pooled(m) is not None:
                    dve.wait_ge(s_pprod, pooled(m) + 1)
                    src = pproduct[pooled(m) % 2]
                else:
                    q = qkv[half][:, t:t + 1, 0:D].to_broadcast([P, T, D])
                    src = product[m % 2]
                    dve.tensor_tensor(src[:, :, :], q, qkv[half][:, :, D:2 * D], ALU.mult).then_inc(s_prod, 1)
                    dve.wait_ge(s_prod, sum(pooled(i) is None for i in range(m + 1)))
                dve.tensor_reduce(score[half][:, t, :, :], src[:, :, :].rearrange("p s (h d) -> p s h d", d=HD),
                                  AX.X, ALU.add).then_inc(s_score, 1)

            def less_max(g):
                half, ts = group(g)
                ts = slice(ts.start, ts.stop)
                by_source = score[half][:, ts, :, :].rearrange("p t s h -> p t h s")
                dve.wait_ge(s_score, HT * (g + 1))
                dve.tensor_reduce(astat[half][:, ts, 0, :].rearrange("p t (h o) -> p t h o", o=1), by_source, AX.X, ALU.max)\
                    .then_inc(s_amax, 1)
                dve.wait_ge(s_amax, 2 * g + 1)
                dve.tensor_tensor(score[half][:, ts, :, :], score[half][:, ts, :, :],
                                  astat[half][:, ts, :, :].to_broadcast([P, HT, T, H]), ALU.subtract).then_inc(s_amax, 1)

            def weight_sum(g):
                half, ts = group(g)
                rec = arec[half][:, ts.start:ts.stop, :, :]
                by_source = score[half][:, ts.start:ts.stop, :, :].rearrange("p t s h -> p t h s")
                dve.tensor_reduce(rec, by_source, AX.X, ALU.add).then_inc(s_asum, 1)
                dve.wait_ge(s_asum, g + 1)
                dve.reciprocal(rec, rec).then_inc(s_arec, 1)

            def weigh(m):
                half, t = divmod(m, T)
                dve.wait_ge(s_aexp, m // HT + 1)
                if m >= 2:
                    dve.wait_ge(s_att, m - 1)
                w = score[half][:, t, :, :].rearrange("p s (h o) -> p s h o", o=1)
                dve.tensor_tensor(wproduct[m % 2][:, :, :].rearrange("p s (h d) -> p s h d", d=HD),
                                  qkv[half][:, :, 2 * D:].rearrange("p s (h d) -> p s h d", d=HD),
                                  w.to_broadcast([P, T, H, HD]), ALU.mult).then_inc(s_weigh, 1)

            def normalise(g):
                half, ts = group(g)
                dve.wait_ge(s_att, HT * (g + 1))
                dve.wait_ge(s_arec, g + 1)
                dve.tensor_tensor(cat[half][:, ts.start:ts.stop, 0, :].rearrange("p t (h d) -> p t h d", d=HD),
                                  attP[g % 2].rearrange("p t (h d) -> p t h d", d=HD),
                                  arec[half][:, ts.start:ts.stop, :, :].to_broadcast([P, HT, H, HD]), ALU.mult)\
                    .then_inc(s_attn, 1)

            def residual(g):
                for m in range(HT * g, HT * (g + 1)):
                    half, t = divmod(m, T)
                    dve.wait_ge(s_out_mm, m + 1)
                    if m == 0:
                        dve.wait_ge(s_xb, 1)
                    xt = x_all[:, HALVES * t + half, :]
                    dve.tensor_tensor(xt, outP[m % 2], xt, ALU.add).then_inc(s_x, 1)

            projected(0)
            for m in range(HALVES * T):
                if m + 1 < HALVES * T:
                    projected(m + 1)
                tap_logits(m)
                if m == T - 1:
                    tap_max(0)
            tap_sum(0)
            tap_max(1)
            for g in range(GROUPS + 2):
                for t in range(HT):
                    if g < GROUPS:
                        scores(HT * g + t)
                    if 1 <= g <= GROUPS:
                        weigh(HT * (g - 1) + t)
                    if g >= 2 and t == 0:
                        normalise(g - 2)
                    if g >= 2 and t == 2:
                        residual(g - 2)
                if g < GROUPS:
                    less_max(g)
                if g == 0:
                    tap_sum(1)
                elif g <= GROUPS:
                    weight_sum(g - 1)

        @block.tensor
        def _(pe):
            def into(m):
                half, t = divmod(m, T)
                at = (HALVES * t + half) * P
                if m >= 2:
                    pe.wait_ge(s_qkv, m - 1)
                pe.matmul(inP[m % 2][:, :], n.xnT[:, at:at + P], win[:, :], start=True, stop=True).then_inc(s_in_mm, 1)

            norm_turn(pe, n, 0, lambda i: xn[0][:, i, :], ident)
            pe.wait_ge(s_w, 112)
            pe.wait_ge(n.s_xnT, 1)
            into(0)
            into(1)

            def v_into(c):
                pe.wait_ge(n.s_xnT, c + 1)
                if c >= 2:
                    pe.wait_ge(s_vT, c - 1)
                pe.matmul(vTP(c), win[:, 2 * D:], n.xnT[:, c * CN:(c + 1) * CN], start=True, stop=True).then_inc(s_vT_mm, 1)

            v_into(0)
            for c in range(1, CHUNKS):
                norm_turn(pe, n, c, lambda i: xn[c % 2][:, i, :], ident)
            for m in range(HALVES * T):
                half, t = divmod(m, T)
                tile = HALVES * t + half
                at = tile * P
                if m in range(0, 2 * (CHUNKS - 1), 2):
                    v_into(m // 2 + 1)
                pe.wait_ge(s_vT, tile // CT + 1)
                if m < 2:
                    pe.wait_ge(n.s_xnT, CHUNKS - 1 + m)
                else:
                    pe.wait_ge(s_dyn, m - 1)
                pe.matmul(outD(m), vT[:, at:at + P], wdyn[:, :], start=True, stop=True).then_inc(s_dyn_mm, 1)
                if m + 2 < HALVES * T:
                    into(m + 2)
            pe.wait_ge(s_dyn, HALVES * T)

            def add_up(dst, product, ready, m, done, taken):
                g = m // HT
                if m % HT == 0 and g >= 2:
                    pe.wait_ge(taken, g - 1)
                pe.wait_ge(ready, m + 1)
                for s in range(T):
                    ins = pe.matmul(dst[g % 2][:, m % HT, :], ident[:, :], product[m % 2][:, s, :],
                                    start=(s == 0), stop=(s == T - 1))
                ins.then_inc(done, 1)

            def turn(m):
                half, t = divmod(m, T)
                g = m // HT
                pe.wait_ge(s_attn, g + 1)
                pe.wait_ge(s_convn, g + 1)
                if m >= 2:
                    pe.wait_ge(s_cat, m - 1)
                for c in range(2):
                    ins = pe.transpose(catP[m % 2][:, c, :], cat[half][:, t, c, :], ident[:, :])
                ins.then_inc(s_cat_mm, 1)

            def output(m):
                pe.wait_ge(s_cat, m + 1)
                if m >= 2:
                    pe.wait_ge(s_x, m - 1)
                for c in range(2):
                    ins = pe.matmul(outP[m % 2], catT[m % 2][:, c, :], wout[:, c, :], start=(c == 0), stop=(c == 1))
                ins.then_inc(s_out_mm, 1)

            def outputs(ms):
                turn(ms[0])
                for m in ms:
                    if m + 1 in ms:
                        turn(m + 1)
                    output(m)

            for g in range(GROUPS + 2):
                for t in range(HT):
                    if 1 <= g <= GROUPS:
                        add_up(attP, wproduct, s_weigh, HT * (g - 1) + t, s_att, s_attn)
                    if g < GROUPS:
                        add_up(convP, cproduct, s_cprod, HT * g + t, s_conv, s_convn)
                    if g >= 2 and t == 1:
                        outputs(range(HT * (g - 2), HT * (g - 1)))


def build_decoder(nc, a, out):
    with ExitStack() as ctx:
        def sb(name, shape, dt=F32):
            return ctx.enter_context(nc.sbuf_tensor(name, shape, dt))

        x_all = sb("x_all", [P, TILES, D])
        ident = sb("ident", [P, P])
        ctxT = sb("ctxT_sb", [P, B * S])
        part_scratch = nc.dram_tensor("part_scratch", [2, 2, SLOTS, P, S], BF16, kind="Internal").ap()
        rel_scratch = nc.dram_tensor("rel_scratch", [2, 6, H, S], BF16, kind="Internal").ap()
        gate_scratch = nc.dram_tensor("gate_scratch", [TILES * E, P], F32, kind="Internal").ap()
        stackQ, stackK, Vp = ctx.enter_context(attention_buffers(nc))

        shared = {k: a[f"shared_{k}"] for k in ("wq", "wk", "wv", "wo")}
        cross = {k: a[f"cross_{k}"] for k in ("wq", "wk", "wv", "wo", "bq", "bk", "bv", "bo")}
        relative = {k: a[f"relative_{k}"] for k in ("wq", "wk", "wv", "wo", "w_rel")}
        attention_phase(nc, "self_cross", x_all, ident,
                        [{**shared, "mqa": True, "ctx": False}, {**cross, "mqa": False, "ctx": True}],
                        ctxT, part_scratch, stackQ, stackK, Vp, first_load={"x": a["x"], "ctxT": a["ctxT"]})
        ffn_phase(nc, "ffn0", x_all, ident, False, a["experts0"], a["router0"], None, gate_scratch)
        across_phase(nc, "across", x_all, ident, a["across_in"], a["across_in_b"], a["across_dyn"], a["across_dyn_b"],
                     a["across_out"], a["across_out_b"])
        attention_phase(nc, "relative", x_all, ident,
                        [{**relative, "rel_scratch": rel_scratch, "mqa": False, "ctx": True}], ctxT,
                        part_scratch, stackQ, stackK, Vp)
        ffn_phase(nc, "ffn1", x_all, ident, True, a["experts1"], a["router1"], a["rms_scale"], gate_scratch, out)


def kernel(**inputs):
    import numpy as np
    import concourse.bacc as bacc
    from concourse.bass_utils import run_bass_kernel_spmd

    i = {k: np.asarray(v) for k, v in inputs.items()}

    def by_dim(w):
        return w.reshape(-1, H, HD).transpose(0, 2, 1).reshape(-1, D)

    def blocks(w):
        e, k, n = w.shape
        return w.reshape(e, k // P, P, n).transpose(0, 2, 1, 3).reshape(e, P, -1)

    w_kv = i["L1_xattn_w_kv"]
    arrays = {
        "x": i["x"].reshape(-1, D), "ctxT": i["ctx_1024"].reshape(-1, D).T,
        "shared_wq": by_dim(i["L0_attn_Wq"]), "shared_wk": by_dim(np.tile(i["L0_attn_Wk"], (1, H))),
        "shared_wv": i["L0_attn_Wv"], "shared_wo": i["L0_attn_Wo"],
        "cross_wq": by_dim(i["L0_xattn_Wq"].T), "cross_wk": by_dim(i["L0_xattn_Wk"].T),
        "cross_wv": i["L0_xattn_Wv"].T, "cross_wo": i["L0_xattn_Wo"].T,
        "cross_bq": by_dim(i["L0_xattn_bq"]).T, "cross_bk": by_dim(i["L0_xattn_bk"]).T,
        "cross_bv": i["L0_xattn_bv"].reshape(D, 1), "cross_bo": i["L0_xattn_bo"],
        "router0": i["L0_ffn_router_w"].T,
        "experts0": np.concatenate([i["L0_ffn_w1"].transpose(0, 2, 1), blocks(i["L0_ffn_w2"].transpose(0, 2, 1)),
                                    blocks(i["L0_ffn_b1"][:, :, None]), blocks(i["L0_ffn_b2"][:, :, None])], -1),
        "across_in": i["L1_attn_in_proj_w"].T, "across_in_b": i["L1_attn_in_proj_b"],
        "across_dyn": i["L1_attn_dyn_w"].T, "across_dyn_b": i["L1_attn_dyn_b"],
        "across_out": i["L1_attn_out_proj_w"].T, "across_out_b": i["L1_attn_out_proj_b"],
        "relative_wq": by_dim(i["L1_xattn_w_q"]), "relative_wk": by_dim(w_kv[:, :D]),
        "relative_wv": w_kv[:, D:], "relative_wo": i["L1_xattn_w_proj"], "relative_w_rel": i["L1_xattn_w_rel"].reshape(H, 1),
        "router1": i["L1_ffn_centroids"].T, "rms_scale": i["L1_ffn_scale"],
        "experts1": np.concatenate([i["L1_ffn_up_w"], blocks(i["L1_ffn_down_w"])], -1),
    }
    arrays = {k: np.ascontiguousarray(v) for k, v in arrays.items()}
    nc = bacc.Bacc("TRN2", target_bir_lowering=False, num_devices=1)
    aps = {k: nc.dram_tensor(k, v.shape, mybir.dt.from_np(v.dtype), kind="ExternalInput").ap() for k, v in arrays.items()}
    out = nc.dram_tensor("out", (B * S, D), F32, kind="ExternalOutput").ap()
    build_decoder(nc, aps, out)
    r = run_bass_kernel_spmd(nc, [arrays], core_ids=[0])
    return r.results[0]["out"].reshape(B, S, D)
```
